# Optimizing a Trainium2 kernel written in Bass

```python
import numpy as np
import jax
import jax.numpy as jnp

def _softmax(x, axis=-1):
    return jax.nn.softmax(x, axis=axis)

def _gelu(x):
    return jax.nn.gelu(x, approximate=True)

def _silu(x):
    return jax.nn.silu(x)

def _sigmoid(x):
    return jax.nn.sigmoid(x)

def _layernorm(x, axis=-1, eps=1e-05):
    m = jnp.mean(x, axis=axis, keepdims=True)
    v = jnp.var(x, axis=axis, keepdims=True)
    return (x - m) / jnp.sqrt(v + eps)

def _scatter_add(tgt, idx, src, axis=0):
    return tgt.at[idx].add(src)

def _segment_sum(src, seg, n):
    return jax.ops.segment_sum(src, seg, n)
kernel_name = 'mk_adaln_attn_ffn_d1_seqx_r4_448bc6'

def setup_inputs(seed: int=0):
    np.random.seed(seed)
    _w = jnp.asarray

    def _rec_inputs():
        import jax
        import jax.numpy as jnp
        _rk = jax.random.key(seed)
        x = -0.000125 + 0.9999 * jax.random.normal(jax.random.fold_in(_rk, 1), (32, 64, 1024), jnp.float32)
        _lenS = 64 - jax.random.randint(jax.random.fold_in(_rk, 7), (32,), 0, max(1, 64 // 4) + 1, jnp.int32)
        _lenS2 = 64 - jax.random.randint(jax.random.fold_in(_rk, 8), (32,), 0, max(1, 64 // 4) + 1, jnp.int32)
        itok_B_3_7 = jax.random.randint(jax.random.fold_in(_rk, 11), (32,), 3, 8, jnp.int32)
        itok_B_6_15 = jax.random.randint(jax.random.fold_in(_rk, 12), (32,), 6, 16, jnp.int32)
        return (x, itok_B_3_7, itok_B_6_15)
    x, itok_B_3_7, itok_B_6_15 = _rec_inputs()

    def _L0_cond_setup():
        import jax, jax.numpy as jnp
        import numpy as np
        MAX_LORAS, OUT, IN = (8, 1024, 1024)
        B, S = (4, 512)
        key = jax.random.key(seed)
        k1, k2, k3 = jax.random.split(key, 3)
        x = jax.random.normal(k1, (B, S, IN), dtype=jnp.float32)
        weight = jax.random.normal(k2, (MAX_LORAS, OUT, IN), dtype=jnp.float32) * 0.02
        adapter_ids = jax.random.randint(k3, (B,), 0, MAX_LORAS, dtype=jnp.int32)
        return {'x': x, 'weight': weight, 'adapter_ids': adapter_ids}
    _L0_cond_all = _L0_cond_setup()
    _L0_cond_in = {k: v for k, v in _L0_cond_all.items() if k in ('weight',)}
    del _L0_cond_all

    def _L0_attn_setup():
        import jax, jax.numpy as jnp
        import numpy as np
        import math
        D_MODEL = 1024
        N_HEADS = 32
        HEAD_DIM = D_MODEL // N_HEADS
        CLIP_QKV = 8.0
        ALIBI_BIAS_MAX = 8
        LN_EPS = 1e-05

        def _alibi_slopes(total_num_heads: int, alibi_bias_max: int) -> jnp.ndarray:
            next_p2 = 2 ** math.ceil(math.log2(total_num_heads))
            m = jnp.arange(1, next_p2 + 1, dtype=jnp.float32) * (alibi_bias_max / next_p2)
            slopes = 1.0 / jnp.power(2.0, m)
            if next_p2 != total_num_heads:
                slopes = jnp.concatenate([slopes[1::2], slopes[::2]])[:total_num_heads]
            return slopes

        def _layer_norm(x, w, b):
            mu = jnp.mean(x, axis=-1, keepdims=True)
            var = jnp.var(x, axis=-1, keepdims=True)
            return (x - mu) * jax.lax.rsqrt(var + LN_EPS) * w + b
        key = jax.random.key(seed)
        k0, k1, k2 = jax.random.split(key, 3)
        B, S = (2, 512)
        return {'hidden_states': jax.random.normal(k0, (B, S, D_MODEL), dtype=jnp.float32), 'w_qkv': jax.random.normal(k1, (3 * D_MODEL, D_MODEL), dtype=jnp.float32) * 0.02, 'q_ln_w': jnp.ones((D_MODEL,), jnp.float32), 'q_ln_b': jnp.zeros((D_MODEL,), jnp.float32), 'k_ln_w': jnp.ones((D_MODEL,), jnp.float32), 'k_ln_b': jnp.zeros((D_MODEL,), jnp.float32), 'w_out': jax.random.normal(k2, (D_MODEL, D_MODEL), dtype=jnp.float32) * 0.02}
    _L0_attn_all = _L0_attn_setup()
    _L0_attn_in = {k: v for k, v in _L0_attn_all.items() if k in ('w_qkv', 'q_ln_w', 'q_ln_b', 'k_ln_w', 'k_ln_b', 'w_out')}
    del _L0_attn_all

    def _L0_cond2_setup():
        import jax, jax.numpy as jnp
        import numpy as np
        B, S, D_IN, D_OUT = (4, 512, 1024, 1024)
        RANK, MAX_LORAS = (16, 32)
        key = jax.random.key(seed)
        ks = jax.random.split(key, 6)
        x = jax.random.normal(ks[0], (B, S, D_IN), dtype=jnp.float32)
        adapter_ids = jax.random.randint(ks[1], (B,), 0, MAX_LORAS)
        base_weight = jax.random.normal(ks[2], (D_OUT, D_IN), dtype=jnp.float32) * D_IN ** (-0.5)
        base_bias = jax.random.normal(ks[3], (D_OUT,), dtype=jnp.float32) * 0.01
        lora_A_w = jax.random.normal(ks[4], (MAX_LORAS, RANK, D_IN), dtype=jnp.float32) * D_IN ** (-0.5)
        lora_B_w = jax.random.normal(ks[5], (MAX_LORAS, D_OUT, RANK), dtype=jnp.float32) * RANK ** (-0.5)
        return {'x': x, 'adapter_ids': adapter_ids, 'base_weight': base_weight, 'base_bias': base_bias, 'lora_A_w': lora_A_w, 'lora_B_w': lora_B_w}
    _L0_cond2_all = _L0_cond2_setup()
    _L0_cond2_in = {k: v for k, v in _L0_cond2_all.items() if k in ('base_weight', 'base_bias', 'lora_A_w', 'lora_B_w')}
    del _L0_cond2_all

    def _L0_ffn_setup():
        import jax, jax.numpy as jnp
        import numpy as np
        RANKS = (8, 16, 32, 64)
        TOPK = 1
        SCALING = 1.0 / 4
        key = jax.random.key(seed)
        ks = jax.random.split(key, 7)
        D_IN, D_OUT, MAX_R, N_RANKS = (1024, 1024, 64, len(RANKS))
        B_, S_ = (4, 512)
        return {'hidden_states': jax.random.normal(ks[0], (B_, S_, D_IN), jnp.float32), 'W': jax.random.normal(ks[1], (D_OUT, D_IN), jnp.float32) * 0.02, 'b': jax.random.normal(ks[2], (D_OUT,), jnp.float32) * 0.02, 'A': jax.random.normal(ks[3], (MAX_R, D_IN), jnp.float32) * 0.02, 'B': jnp.zeros((D_OUT, MAX_R), jnp.float32) + jax.random.normal(ks[4], (D_OUT, MAX_R), jnp.float32) * 0.02, 'gate_w': jax.random.normal(ks[5], (N_RANKS, D_IN), jnp.float32) * 0.02, 'gate_b': jax.random.normal(ks[6], (N_RANKS,), jnp.float32) * 0.02}
    _L0_ffn_all = _L0_ffn_setup()
    _L0_ffn_in = {k: v for k, v in _L0_ffn_all.items() if k in ('W', 'b', 'A', 'B', 'gate_w', 'gate_b')}
    del _L0_ffn_all
    return {'x': x, 'itok_B_3_7': itok_B_3_7, 'itok_B_6_15': itok_B_6_15, 'L0_cond_weight': _L0_cond_in['weight'], 'L0_attn_w_qkv': _L0_attn_in['w_qkv'], 'L0_attn_q_ln_w': _L0_attn_in['q_ln_w'], 'L0_attn_q_ln_b': _L0_attn_in['q_ln_b'], 'L0_attn_k_ln_w': _L0_attn_in['k_ln_w'], 'L0_attn_k_ln_b': _L0_attn_in['k_ln_b'], 'L0_attn_w_out': _L0_attn_in['w_out'], 'L0_cond2_base_weight': _L0_cond2_in['base_weight'], 'L0_cond2_base_bias': _L0_cond2_in['base_bias'], 'L0_cond2_lora_A_w': _L0_cond2_in['lora_A_w'], 'L0_cond2_lora_B_w': _L0_cond2_in['lora_B_w'], 'L0_ffn_W': _L0_ffn_in['W'], 'L0_ffn_b': _L0_ffn_in['b'], 'L0_ffn_A': _L0_ffn_in['A'], 'L0_ffn_B': _L0_ffn_in['B'], 'L0_ffn_gate_w': _L0_ffn_in['gate_w'], 'L0_ffn_gate_b': _L0_ffn_in['gate_b']}

def reference(x, itok_B_3_7, itok_B_6_15, L0_cond_weight, L0_attn_w_qkv, L0_attn_q_ln_w, L0_attn_q_ln_b, L0_attn_k_ln_w, L0_attn_k_ln_b, L0_attn_w_out, L0_cond2_base_weight, L0_cond2_base_bias, L0_cond2_lora_A_w, L0_cond2_lora_B_w, L0_ffn_W, L0_ffn_b, L0_ffn_A, L0_ffn_B, L0_ffn_gate_w, L0_ffn_gate_b):
    import jax
    import jax.numpy as jnp

    def _L0_cond_ref(x, weight, adapter_ids):
        import jax, jax.numpy as jnp
        import numpy as np
        MAX_LORAS, OUT, IN = (8, 1024, 1024)
        B, S = (4, 512)
        w = weight[adapter_ids]
        return jnp.einsum('bsi,boi->bso', x, w)

    def _L0_attn_ref(hidden_states, w_qkv, q_ln_w, q_ln_b, k_ln_w, k_ln_b, w_out):
        import jax, jax.numpy as jnp
        import numpy as np
        import math
        D_MODEL = 1024
        N_HEADS = 32
        HEAD_DIM = D_MODEL // N_HEADS
        CLIP_QKV = 8.0
        ALIBI_BIAS_MAX = 8
        LN_EPS = 1e-05

        def _alibi_slopes(total_num_heads: int, alibi_bias_max: int) -> jnp.ndarray:
            next_p2 = 2 ** math.ceil(math.log2(total_num_heads))
            m = jnp.arange(1, next_p2 + 1, dtype=jnp.float32) * (alibi_bias_max / next_p2)
            slopes = 1.0 / jnp.power(2.0, m)
            if next_p2 != total_num_heads:
                slopes = jnp.concatenate([slopes[1::2], slopes[::2]])[:total_num_heads]
            return slopes

        def _layer_norm(x, w, b):
            mu = jnp.mean(x, axis=-1, keepdims=True)
            var = jnp.var(x, axis=-1, keepdims=True)
            return (x - mu) * jax.lax.rsqrt(var + LN_EPS) * w + b
        B, S, D = hidden_states.shape
        qkv = jnp.einsum('bsd,ed->bse', hidden_states, w_qkv)
        qkv = jnp.clip(qkv, -CLIP_QKV, CLIP_QKV)
        q, k, v = jnp.split(qkv, 3, axis=-1)
        q = _layer_norm(q, q_ln_w, q_ln_b)
        k = _layer_norm(k, k_ln_w, k_ln_b)
        q = q.reshape(B, S, N_HEADS, HEAD_DIM)
        k = k.reshape(B, S, N_HEADS, HEAD_DIM)
        v = v.reshape(B, S, N_HEADS, HEAD_DIM)
        scale = HEAD_DIM ** (-0.5)
        scores = jnp.einsum('bqhd,bkhd->bhqk', q, k) * scale
        pos = jnp.arange(S)
        rel = pos[None, :] - pos[:, None]
        slopes = _alibi_slopes(N_HEADS, ALIBI_BIAS_MAX)
        bias = slopes[:, None, None] * rel.astype(jnp.float32)
        causal = rel <= 0
        scores = jnp.where(causal[None, None], scores + bias[None], -jnp.inf)
        probs = jax.nn.softmax(scores, axis=-1)
        attn = jnp.einsum('bhqk,bkhd->bqhd', probs, v).reshape(B, S, D)
        return jnp.einsum('bsd,ed->bse', attn, w_out)

    def _L0_cond2_ref(x, adapter_ids, base_weight, base_bias, lora_A_w, lora_B_w):
        import jax, jax.numpy as jnp
        import numpy as np
        B, S, D_IN, D_OUT = (4, 512, 1024, 1024)
        RANK, MAX_LORAS = (16, 32)
        result = jnp.einsum('bsd,od->bso', x, base_weight) + base_bias
        A = lora_A_w[adapter_ids]
        Bw = lora_B_w[adapter_ids]
        h = jnp.einsum('bsd,brd->bsr', x, A)
        lora_out = jnp.einsum('bsr,bor->bso', h, Bw)
        result = result + lora_out
        return result.astype(x.dtype)

    def _L0_ffn_ref(hidden_states, W, b, A, B, gate_w, gate_b):
        import jax, jax.numpy as jnp
        import numpy as np
        RANKS = (8, 16, 32, 64)
        TOPK = 1
        SCALING = 1.0 / 4
        bsz, seq, d_in = hidden_states.shape
        out = jnp.einsum('bsd,od->bso', hidden_states, W) + b
        x = hidden_states.reshape(-1, d_in)
        scores = x @ gate_w.T + gate_b
        probs = jax.nn.softmax(scores, axis=-1)
        routing_weights, selected = jax.lax.top_k(probs, TOPK)
        routing_weights = routing_weights / jnp.sum(routing_weights, axis=-1, keepdims=True)
        lora_outputs = jnp.stack([x @ A[:r, :].T @ B[:, :r].T for r in RANKS], axis=1)
        sel = jnp.take_along_axis(lora_outputs, selected[:, :, None], axis=1)
        final = jnp.sum(sel * routing_weights[:, :, None], axis=1)
        return out + final.reshape(bsz, seq, -1)
    x = x + _L0_attn_ref(_L0_cond_ref(x, L0_cond_weight, itok_B_3_7), L0_attn_w_qkv, L0_attn_q_ln_w, L0_attn_q_ln_b, L0_attn_k_ln_w, L0_attn_k_ln_b, L0_attn_w_out)
    x = x + _L0_ffn_ref(_L0_cond2_ref(x, itok_B_6_15, L0_cond2_base_weight, L0_cond2_base_bias, L0_cond2_lora_A_w, L0_cond2_lora_B_w), L0_ffn_W, L0_ffn_b, L0_ffn_A, L0_ffn_B, L0_ffn_gate_w, L0_ffn_gate_b)
    return x

_drawn_inputs = setup_inputs


def setup_inputs(seed=0):
    import zlib

    import numpy as np

    out = dict(_drawn_inputs(seed))
    spreads = {'L0_attn_q_ln_w': (1.0, 0.6),
     'L0_attn_q_ln_b': (0.0, 0.8),
     'L0_attn_k_ln_w': (1.0, 0.6),
     'L0_attn_k_ln_b': (0.0, 2.0)}
    factors = {'L0_cond2_base_bias': 8.0, 'L0_ffn_b': 3.775, 'L0_ffn_gate_b': 22.47}
    for name, (base, spread) in spreads.items():
        noise = np.random.default_rng([zlib.crc32(name.encode()), seed]).standard_normal(out[name].shape)
        drawn = base * np.exp(spread * noise) if base else spread * noise
        out[name] = jnp.asarray(drawn.astype(out[name].dtype))
    for name, factor in factors.items():
        out[name] = (out[name] * factor).astype(out[name].dtype)
    return out
```

```python
from contextlib import ExitStack

import numpy as np

import concourse.bass as bass
from concourse import mybir

ALU = mybir.AluOpType
ACT = mybir.ActivationFunctionType
AX_X = mybir.AxisListType.X
F32 = mybir.dt.float32
F32R = mybir.dt.float32r
I32 = mybir.dt.int32

P = 128
MASKED = -3.0e38
CLIP = 8.0
LN_EPS = 1e-5
QUARTERS = 4
RAW_SLOTS = 4

Q, K, V, O, H, F = range(6)


def adaln_attention_ffn(nc, x, ids_expert, ids_lora, w_cond, w_qkv, q_w, q_b, k_w, k_b, w_out,
                        w_base, b_base, lora_a, lora_b, w_ffn, b_ffn, ffn_a, ffn_b, gate_w, gate_b, out):
    B, S, D = x.shape
    E = w_cond.shape[0]
    KC = D // P
    NT = B * S // P
    PAIRS = NT // 2
    HEADS = 32
    DH = D // HEADS
    QO = D // QUARTERS
    OB = QO // P
    RANK = lora_a.shape[1]
    N_LORA = lora_a.shape[0]
    MAXR = ffn_a.shape[0]
    NG = gate_w.shape[0]
    AG = MAXR + NG
    R2 = 2 * RANK
    FCH = (D + AG) // 3
    assert S * 2 == P and FCH * 3 == D + AG and 4 * R2 == P and 2 * MAXR == P and NG == 4
    assert D % 512 == 0 and NT % 2 == 0 and HEADS * S == 2048
    SCALE = float(DH) ** -0.5
    SLOPES = [float(np.float32(1.0) / np.float32(2.0) ** np.float32((h + 1) * 8.0 / HEADS)) for h in range(HEADS)]

    x_rows = x.rearrange("b s d -> (b s) d").rearrange("(t p) d -> t p d", p=P)
    out_rows = out.rearrange("b s d -> (b s) d").rearrange("(t p) d -> t p d", p=P)
    wc_rows = w_cond.rearrange("e (q ob p) i -> e q p ob i", q=QUARTERS, p=P)
    w_rows = {Q: w_qkv[0:D, :], K: w_qkv[D:2 * D, :], V: w_qkv[2 * D:3 * D, :], O: w_out, H: w_base, F: w_ffn}
    lora_b_rows = lora_b.rearrange("n (o p) r -> n p o r", p=P)
    ffn_b_rows = ffn_b.rearrange("(o p) r -> p o r", p=P)

    def dram(name, chunked):
        return nc.dram_tensor(name, (NT, P, KC, P) if chunked else (NT, P, D), F32).ap()

    xT_d = dram("xT_d", True)
    cT_d = dram("cT_d", True)
    tr_d = {Q: dram("qT_d", True), K: dram("kT_d", True), V: dram("attT_d", True),
            O: dram("x1T_d", True), H: dram("hT_d", True)}
    x1_d = dram("x1_d", False)
    act_src = {Q: cT_d, K: cT_d, V: cT_d, O: tr_d[V], H: tr_d[O], F: tr_d[H]}

    with ExitStack() as ctx:
        def sb(name, shape, dt=F32, scope=ctx):
            return scope.enter_context(nc.sbuf_tensor(name, shape, dt))

        def sem(name):
            return ctx.enter_context(nc.semaphore(name))

        def sem2(name):
            return [sem(f"{name}{u}") for u in range(2)]

        ident = sb("ident", [P, P])
        ids_sb = sb("ids_sb", [1, 2 * B], I32)
        ln_cols = sb("ln_cols", [P, 4, KC])
        eps_col = sb("eps_col", [P, 1])
        bn_st = sb("bn_st", [P, 2, 6])
        mean_var = sb("mean_var", [P, 2])
        std_rstd = sb("std_rstd", [P, 2])
        wait_pad = sb("wait_pad", [P, 1])
        seq_mask = sb("seq_mask", [R2, P])

        cond = ExitStack()
        wc_hi = sb("wc_hi", [P, E, KC, QO], F32R, cond)
        wc_lo = sb("wc_lo", [P, E, KC, QO], F32R, cond)
        wc_raw = sb("wc_raw", [P, RAW_SLOTS, OB, D], F32, cond)
        x_in = sb("x_in", [P, 2, KC, P], F32, cond)
        x_tr = sb("x_tr", [P, 2, KC, P], F32, cond)
        x_st = sb("x_st", [P, 2, KC, 2, 2, S], F32R, cond)
        c_low = sb("c_low", [S, 2, QO], F32, cond)
        c_nat = sb("c_nat", [P, 2, QO], F32, cond)
        cT_sb = sb("cT_sb", [P, 2, OB, P], F32, cond)
        cond.close()

        w_hi = [sb("w0_hi", [P, KC, D], F32R), sb("w1_hi", [P, KC, AG + D], F32R)]
        w_lo = [sb("w0_lo", [P, KC, D], F32R), sb("w1_lo", [P, KC, AG + D], F32R)]
        w_raw = sb("w_raw", [P, D])
        act_raw = sb("act_raw", [P, 2, KC, P])
        act_hi = sb("act_hi", [P, 2, KC, P], F32R)
        act_lo = sb("act_lo", [P, 2, KC, P], F32R)
        nat = sb("nat", [P, 2, D])
        aux = sb("aux", [P, 2, D])
        tr_sb = sb("tr_sb", [P, 2, KC, P])
        attn = ExitStack()
        v_bd = sb("v_bd", [P, 2, HEADS // 2, 2 * DH], F32, attn)
        alibi = sb("alibi", [P, HEADS, S], F32, attn)
        pT_sb = sb("pT_sb", [P, 2, 4, P], F32, attn)
        rel = sb("rel", [P, S], F32, attn)
        smax = sb("smax", [P, HEADS], F32, attn)
        ssum = sb("ssum", [P, HEADS], F32, attn)
        attn.close()
        bias_row = sb("bias_row", [P, D])
        la_T = sb("la_T", [P, KC, R2])
        lb_raw = sb("lb_raw", [P, KC, R2])
        lb_parts = sb("lb_parts", [P, KC, 4, R2])
        lb_st = sb("lb_st", [P, D], F32R)
        u_seq = sb("u_seq", [R2, P])
        u_st = sb("u_st", [P, P], F32R)
        a_msk = sb("a_msk", [P, MAXR])
        a_parts = sb("a_parts", [P, 2, MAXR])
        aT_st = sb("aT_st", [P, P], F32R)
        gate = sb("gate", [P, 10, NG])
        q_in, k_in = (aux[:, n, :].rearrange("p (k n) -> p k n", k=KC) for n in range(2))
        scores = nat[:, :, :].rearrange("p a n -> p (a n)").rearrange("p (h k) -> p h k", k=S)
        ffn_b_nat = lb_parts[:, :, :, :].rearrange("p k a r -> p k (a r)")

        def bank(name):
            return ctx.enter_context(nc.psum_tensor(name, [P, 512], F32))

        acc = [bank("acc0"), bank("acc1")]
        wps = [bank("wps0"), bank("wps1")]
        xps = [bank(f"xps{n}") for n in range(4)]
        acc3 = [acc[0], acc[1], wps[0]]

        ids_in, ident_ready, cols_in, cols_scaled, consts_ready = (
            sem(n) for n in ("ids_in", "ident_ready", "cols_in", "cols_scaled", "consts_ready"))
        x_loaded, x_turned, x_copied_a, x_copied_v, xT_stored = (
            sem2(n) for n in ("x_loaded", "x_turned", "x_copied_a", "x_copied_v", "xT_stored"))
        wc_loaded = [sem(f"wc_loaded{s}") for s in range(RAW_SLOTS)]
        wc_turned, wc_hi_ready, wc_lo_ready = (
            [sem(f"{n}{b}") for b in range(4)] for n in ("wc_turned", "wc_hi_ready", "wc_lo_ready"))
        xT_loaded, xs_hi_ready, xs_lo_ready, c_low_ready, c_summed, cpair_done, c_turned, cT_ready, cT_stored = (
            sem2(n) for n in ("xT_loaded", "xs_hi_ready", "xs_lo_ready", "c_low_ready", "c_summed",
                              "cpair_done", "c_turned", "cT_ready", "cT_stored"))
        cfirst_done, w_loaded = sem("cfirst_done"), sem("w_loaded")
        w_turned, w_hi_ready, w_lo_ready = (sem2(n) for n in ("w_turned", "w_hi_ready", "w_lo_ready"))
        act_loaded, act_hi_ready, act_lo_ready = (sem2(n) for n in ("act_loaded", "act_hi_ready", "act_lo_ready"))
        acc_done = [sem2(f"acc_done{c}_") for c in range(3)]
        acc_free = [sem(f"acc_free{c}") for c in range(3)]
        stats_step, var_ready, std_ready = (sem(n) for n in ("stats_step", "var_ready", "std_ready"))
        nat_ready, turned, tr_ready, tr_stored = (sem2(n) for n in ("nat_ready", "turned", "tr_ready", "tr_stored"))
        q_loaded, k_loaded, scores_done, scores_biased, max_ready, shifted, exp_ready, sum_ready, rsum_ready, probs_ready, pT_done = (
            sem(n) for n in ("q_loaded", "k_loaded", "scores_done", "scores_biased", "max_ready", "shifted",
                             "exp_ready", "sum_ready", "rsum_ready", "probs_ready", "pT_done"))
        pT_ready, pT_used = sem2("pT_ready"), sem2("pT_used")
        alibi_step = sem("alibi_step")
        res_loaded, x1_stored, out_stored = (sem2(n) for n in ("res_loaded", "x1_stored", "out_stored"))
        bias_h_in, bias_f_in, gate_b_in, mask_ready = (
            sem(n) for n in ("bias_h_in", "bias_f_in", "gate_b_in", "mask_ready"))
        la_loaded, la_turned, la_ready, lb_loaded, lb_split, lb_turned, lb_ready = (
            sem(n) for n in ("la_loaded", "la_turned", "la_ready", "lb_loaded", "lb_split", "lb_turned", "lb_ready"))
        u_done, u_masked, u_step, u_ready = (sem(n) for n in ("u_done", "u_masked", "u_step", "u_ready"))
        fb_loaded, fb_turned, fb_hi, fb_lo = (sem(n) for n in ("fb_loaded", "fb_turned", "fb_hi", "fb_lo"))
        ag_done, gate_step, gate_exp, a_ready, aT_done, aT_ready, xb_ready = (
            sem(n) for n in ("ag_done", "gate_step", "gate_exp", "a_ready", "aT_done", "aT_ready", "xb_ready"))

        def over_pairs(eng, main, tail):
            main(0, 0, 0)
            with eng.Fori(0, PAIRS - 1) as j:
                main(2 * j + 1, j, 1)
                tail(2 * j, j, 0)
                main(2 * j + 2, j + 1, 0)
                tail(2 * j + 1, j, 1)
            main(NT - 1, PAIRS - 1, 1)
            tail(NT - 2, PAIRS - 1, 0)
            tail(NT - 1, PAIRS - 1, 1)

        def over_phases(eng, before, main, prep, tail, mid):
            for p in (Q, K, V, O, H, F):
                before(p)
                main(p, 0, 0, 0)
                prep(p, 0)
                if p != Q:
                    tail(p - 1, NT - 1, PAIRS - 1, 1)
                mid(p, 0, 0, 0)
                with eng.Fori(0, PAIRS - 1) as j:
                    main(p, 2 * j + 1, j, 1)
                    prep(p, j + 1)
                    tail(p, 2 * j, j, 0)
                    mid(p, 2 * j + 1, j, 1)
                    main(p, 2 * j + 2, j + 1, 0)
                    tail(p, 2 * j + 1, j, 1)
                    mid(p, 2 * j + 2, j + 1, 0)
                main(p, NT - 1, PAIRS - 1, 1)
                if p == H:
                    prep(p, KC)
                tail(p, NT - 2, PAIRS - 1, 0)
                mid(p, NT - 1, PAIRS - 1, 1)
            tail(F, NT - 1, PAIRS - 1, 1)

        def uses(p, i):
            return PAIRS * p + i

        def blocks(p, b):
            return KC * p + b

        def nothing(*_):
            pass

        def loads(p, b):
            if p < O:
                return KC * p + b + 1
            return KC * p + 4 * (b + 1) if p == O else KC * (p + 3) + b + 1

        block = ctx.enter_context(nc.Block())

        @block.sync
        def _(sp):
            sp.dma_start(ids_sb[0:1, 0:B], ids_expert.rearrange("(a n) -> a n", a=1)).then_inc(ids_in, 16)
            sp.dma_start(ids_sb[0:1, B:2 * B], ids_lora.rearrange("(a n) -> a n", a=1)).then_inc(ids_in, 16)
            with nc.allow_non_contiguous_dma(reason="layer norm weights by column, once"):
                for n, col in enumerate((q_w, q_b, k_w, k_b)):
                    sp.dma_start(ln_cols[:, n, :], col.rearrange("(k p) -> p k", p=P)).then_inc(cols_in, 16)

            def load_x(t, u):
                sp.dma_start(x_in[:, u, :, :].rearrange("p k n -> p (k n)"),
                             x_rows[bass.ds(t, 1), :, :].rearrange("a p d -> p (a d)")).then_inc(x_loaded[u], 16)

            def store_xT(t, i, u):
                sp.wait_ge(x_copied_a[u], i + 1)
                sp.wait_ge(x_copied_v[u], i + 1)
                sp.dma_start(xT_d[bass.ds(t, 1), :, :, :].rearrange("a p k n -> p (a k n)"),
                             x_tr[:, u, :, :].rearrange("p k n -> p (k n)")).then_inc(xT_stored[u], 16)

            for u in range(2):
                load_x(u, u)
            with sp.Fori(0, PAIRS - 1) as j:
                for u in range(2):
                    sp.wait_ge(x_turned[u], j + 1)
                    load_x(2 * j + 2 + u, u)
                    store_xT(2 * j + u, j, u)
            for u in range(2):
                store_xT(NT - 2 + u, PAIRS - 1, u)

            def load_expert(q, m, s):
                src = wc_rows[4 * m + s, bass.ds(q, 1), :, :, :].rearrange("a p ob i -> p (a ob) i")
                sp.dma_start(wc_raw[:, s, :, :], src).then_inc(wc_loaded[s], 16)

            def load_xT(q, j, u):
                sp.wait_ge(xs_lo_ready[u], 8 * q + j)
                sp.wait_ge(xT_stored[u], 16 * j + 16)
                sp.dma_start(x_in[:, u, :, :].rearrange("p k n -> p (k n)"),
                             xT_d[bass.ds(2 * j + u, 1), :, :, :].rearrange("a p k n -> p (a k n)")).then_inc(xT_loaded[u], 16)

            def quarter(q, last):
                for s in range(RAW_SLOTS):
                    sp.wait_ge(wc_turned[3], 8 * q + s + 1)
                    load_expert(q, 1, s)
                if not last:
                    for s in range(RAW_SLOTS):
                        sp.wait_ge(wc_turned[3], 8 * q + 4 + s + 1)
                        load_expert(q + 1, 0, s)
                def main(t, j, u):
                    if not (isinstance(t, int) and t == NT - 1):
                        load_xT(q, j + u, 1 - u)

                def tail(t, j, u):
                    sp.wait_ge(cT_ready[u], 8 * q + j + 1)
                    sp.dma_start(cT_d[bass.ds(t, 1), :, bass.ds(OB * q, OB), :].rearrange("a p k n -> p (a k n)"),
                                 cT_sb[:, u, :, :].rearrange("p k n -> p (k n)")).then_inc(cT_stored[u], 16)

                load_xT(q, 0, 0)
                over_pairs(sp, main, tail)

            for s in range(RAW_SLOTS):
                load_expert(0, 0, s)
            for u in range(2):
                sp.wait_ge(x_turned[u], PAIRS)
            with sp.Fori(0, QUARTERS - 1) as q:
                quarter(q, False)
            quarter(QUARTERS - 1, True)

            for u in range(2):
                sp.wait_ge(cT_stored[u], 16 * QUARTERS * PAIRS)

            def load_w(p, b):
                sp.wait_ge(w_turned[1], blocks(p, b))
                if isinstance(b, int) and b == KC:
                    sp.dma_start(w_raw[0:MAXR, :], ffn_a).then_inc(w_loaded, 16)
                    sp.dma_start(w_raw[MAXR:AG, :], gate_w).then_inc(w_loaded, 16)
                elif p == O:
                    for g in range(4):
                        src = w_out.rearrange("n (c g d) -> n g c d", g=4, d=DH)[bass.ds(b * P, P), g, :, :]
                        sp.dma_start(w_raw[:, g * KC * DH:(g + 1) * KC * DH].rearrange("p (c d) -> p c d", d=DH), src).then_inc(w_loaded, 16)
                else:
                    sp.dma_start(w_raw[:, :], w_rows[p][bass.ds(b * P, P), :]).then_inc(w_loaded, 16)

            def load_act(p, t, i, u):
                sp.wait_ge(act_lo_ready[u], uses(p, i))
                if p == H and not (isinstance(t, int) and t < 2):
                    sp.wait_ge(u_done, t - 1)
                if p == F:
                    sp.wait_ge(u_done, NT)
                if p == O:
                    sp.wait_ge(tr_stored[u], 16 * (uses(V, i) + 1))
                if p == H:
                    sp.wait_ge(tr_stored[u], 16 * (uses(O, i) + 1))
                if p == F:
                    sp.wait_ge(tr_stored[u], 16 * (uses(H, i) + 1))
                sp.dma_start(act_raw[:, u, :, :].rearrange("p k n -> p (k n)"),
                             act_src[p][bass.ds(t, 1), :, :, :].rearrange("a p k n -> p (a k n)")).then_inc(act_loaded[u], 16)

            def load_lora(t):
                adapters = [sp.value_load(ids_sb[0:1, bass.ds(B + 2 * t + s, 1)], min_val=0, max_val=N_LORA - 1) for s in range(2)]
                sp.wait_ge(lb_split, 4 * t)
                sp.wait_ge(la_turned, t)
                for s, n in enumerate(adapters):
                    if s:
                        sp.wait_ge(la_loaded, 32 * t + 16)
                        sp.wait_ge(lb_loaded, 32 * t + 16)
                    sp.dma_start(aux[s * RANK:(s + 1) * RANK, 0, :],
                                 lora_a[bass.ds(n, 1), :, :].rearrange("a r i -> (a r) i")).then_inc(la_loaded, 16)
                    sp.dma_start(lb_raw[:, :, s * RANK:(s + 1) * RANK],
                                 lora_b_rows[bass.ds(n, 1), :, :, :].rearrange("a p o r -> p (a o) r")).then_inc(lb_loaded, 16)

            def before(p):
                if p == H:
                    for u in range(2):
                        sp.wait_ge(turned[u], uses(V, PAIRS))
                    sp.dma_start(bias_row[:, :], b_base.partition_broadcast(P)).then_inc(bias_h_in, 16)
                    sp.wait_ge(acc_free[1], NT * O + NT - 1)
                    load_lora(0)
                if p == F:
                    sp.wait_ge(lb_turned, 2 * NT)
                    sp.dma_start(ffn_b_nat[:, :, 0:MAXR], ffn_b_rows).then_inc(fb_loaded, 16)
                    sp.wait_ge(fb_loaded, 16)
                    sp.dma_start(ffn_b_nat[:, :, MAXR:2 * MAXR], ffn_b_rows).then_inc(fb_loaded, 16)
                    sp.dma_start(gate[:, 0, :], gate_b.partition_broadcast(P)).then_inc(gate_b_in, 16)
                    sp.wait_ge(acc_free[1], NT * F)
                    sp.dma_start(bias_row[:, :], b_ffn.partition_broadcast(P)).then_inc(bias_f_in, 16)

            def main(p, t, i, u):
                last = isinstance(t, int) and t == NT - 1
                if not last:
                    load_act(p, t + 1, i + u, 1 - u)
                elif p != F:
                    load_act(p + 1, 0, 0, 0)
                if p == V:
                    if isinstance(t, int) and t == 0:
                        for w in range(2):
                            sp.wait_ge(tr_stored[w], 16 * uses(K, 0))
                    sp.wait_ge(scores_done, 4 * t)
                    sp.wait_ge(tr_stored[u], 16 * (uses(K, i) + 1))
                    for n, (dst, src, s) in enumerate(((q_in, tr_d[Q], q_loaded), (k_in, tr_d[K], k_loaded))):
                        sp.dma_start(aux[:, n, :], src[bass.ds(t, 1), :, :, :].rearrange("a p k n -> p (a k n)")).then_inc(s, 16)
                if p == O:
                    if isinstance(t, int) and t == 0:
                        sp.wait_ge(scores_done, 4 * NT)
                    sp.wait_ge(acc_free[1], NT * O + t - 1)
                    sp.dma_start(aux[:, u, :], x_rows[bass.ds(t, 1), :, :].rearrange("a p d -> p (a d)")).then_inc(res_loaded[u], 16)
                if p == H and not last:
                    load_lora(t + 1)
                if p == F:
                    if isinstance(t, int) and t == 0:
                        sp.wait_ge(la_turned, NT)
                    if not (isinstance(t, int) and t < 2):
                        sp.wait_ge(acc_free[2], t - 1)
                    sp.wait_ge(x1_stored[u], 16 * PAIRS)
                    sp.dma_start(aux[:, u, :], x1_d[bass.ds(t, 1), :, :].rearrange("a p d -> p (a d)")).then_inc(res_loaded[u], 16)

            def prep(p, b):
                if p != F:
                    load_w(p + 1, b)

            def tail(p, t, i, u):
                if p == F:
                    for c in range(3):
                        sp.wait_ge(acc_free[c], (NT * F if c < 2 else 0) + t + 1)
                    sp.dma_start(out_rows[bass.ds(t, 1), :, :].rearrange("a p d -> p (a d)"), nat[:, u, :]).then_inc(out_stored[u], 16)
                    return
                if p == O:
                    for c in range(2):
                        sp.wait_ge(acc_free[c], NT * O + t + 1)
                    sp.dma_start(x1_d[bass.ds(t, 1), :, :].rearrange("a p d -> p (a d)"), nat[:, u, :]).then_inc(x1_stored[u], 16)
                sp.wait_ge(tr_ready[u], uses(p, i) + 1)
                sp.dma_start(tr_d[p][bass.ds(t, 1), :, :, :].rearrange("a p k n -> p (a k n)"),
                               tr_sb[:, u, :, :].rearrange("p k n -> p (k n)")).then_inc(tr_stored[u], 16)

            for b in range(KC):
                load_w(Q, b)
            load_act(Q, 0, 0, 0)

            over_phases(sp, before, main, prep, tail, nothing)
            for u in range(2):
                sp.wait_ge(out_stored[u], 16 * PAIRS)
                sp.wait_ge(x1_stored[u], 16 * PAIRS)
                sp.wait_ge(tr_stored[u], 16 * PAIRS * 5)
                sp.wait_ge(xT_stored[u], 16 * PAIRS)

        @block.tensor
        def _(pe):
            pe.wait_ge(ident_ready, 2)

            with pe.Fori(0, PAIRS) as j:
                for u in range(2):
                    pe.wait_ge(x_loaded[u], 16 * j + 16)
                    pe.wait_ge(x_copied_a[u], j)
                    pe.wait_ge(x_copied_v[u], j)
                    for k in range(KC):
                        last = nc.tensor.transpose(xps[2 * u + k // 4][:, k % 4 * P:(k % 4 + 1) * P], x_in[:, u, k, :], ident[:, :])
                    last.then_inc(x_turned[u], 1)
            for u in range(2):
                pe.wait_ge(x_copied_a[u], PAIRS)
                pe.wait_ge(x_copied_v[u], PAIRS)
            pe.wait_ge(ids_in, 32)

            with pe.Fori(0, QUARTERS) as q:
                with pe.Fori(0, 2) as m:
                    for s in range(4):
                        pe.wait_ge(wc_loaded[s], 32 * q + 16 * m + 16)
                        for b in range(4):
                            pe.wait_ge(wc_lo_ready[b], 8 * q + 4 * m + s)
                            for kk in range(2):
                                for ob in range(OB):
                                    last = nc.tensor.transpose(
                                        xps[b][:, kk * QO + ob * P:kk * QO + (ob + 1) * P],
                                        wc_raw[:, s, ob, (2 * b + kk) * P:(2 * b + kk + 1) * P], ident[:, :])
                            last.then_inc(wc_turned[b], 1)
                def main(t, j, u):
                    experts = [pe.value_load(ids_sb[0:1, bass.ds(2 * t + s, 1)], min_val=0, max_val=E - 1) for s in range(2)]
                    if isinstance(t, int) and t == 0:
                        for b in range(4):
                            pe.wait_ge(wc_lo_ready[b], 8 * q + 8)
                    pe.wait_ge(xs_hi_ready[u], 8 * q + j + 1)
                    pe.wait_ge(xs_lo_ready[u], 8 * q + j + 1)
                    for s, e in enumerate(experts):
                        pe.wait_ge(c_summed[s], 16 * q + t)
                        for k in range(KC):
                            for n, w in enumerate((wc_hi, wc_lo)):
                                last = nc.tensor.matmul(
                                    acc[s][:, 0:QO], x_st[:, u, k, s, :, :].rearrange("p a n -> p (a n)"),
                                    w[:, bass.ds(e, 1), k, :].rearrange("p a n -> p (a n)"),
                                    start=(k == 0 and n == 0), stop=(k == KC - 1 and n == 1))
                        last.then_inc(cpair_done[u] if s else cfirst_done, 1)

                def tail(t, j, u):
                    pe.wait_ge(c_summed[0], 16 * q + t + 1)
                    pe.wait_ge(c_summed[1], 16 * q + t + 1)
                    pe.wait_ge(cT_ready[u], 8 * q + j)
                    for ob in range(OB):
                        last = nc.tensor.transpose(wps[u][:, ob * P:(ob + 1) * P], c_nat[:, u, ob * P:(ob + 1) * P], ident[:, :])
                    last.then_inc(c_turned[u], 1)

                over_pairs(pe, main, tail)

            def turn_w(p, b):
                rows = AG if isinstance(b, int) and b == KC else P
                extra = 16 if rows == AG else 0
                pe.wait_ge(w_loaded, 16 * loads(p, b) + extra)
                for h in range(2):
                    pe.wait_ge(w_lo_ready[h], blocks(p, b))
                    for k in range(4):
                        last = nc.tensor.transpose(wps[h][:, k * P:k * P + rows],
                                                   w_raw[0:rows, (4 * h + k) * P:(4 * h + k + 1) * P], ident[0:rows, 0:rows])
                    last.then_inc(w_turned[h], 1)

            def turn_lora(t):
                pe.wait_ge(la_loaded, 32 * t + 32)
                pe.wait_ge(u_masked, t)
                pe.wait_ge(lb_split, 4 * t + 4)
                for r in range(2):
                    pe.wait_ge(lb_ready, 2 * t + r)
                    for o in range(4):
                        last = nc.tensor.transpose(xps[3][:, o * P:(o + 1) * P],
                                                   lb_parts[:, 4 * r + o, :, :].rearrange("p a r -> p (a r)"), ident[:, :])
                    last.then_inc(lb_turned, 1)
                    if r == 0:
                        for k in range(KC):
                            last = nc.tensor.transpose(xps[2][:, k * R2:(k + 1) * R2], aux[0:R2, 0, k * P:(k + 1) * P], ident[0:R2, 0:R2])
                        last.then_inc(la_turned, 1)

            def before(p):
                for h in range(2):
                    pe.wait_ge(w_lo_ready[h], blocks(p + 1, 1 if p == F else 0))
                if p == H:
                    pe.wait_ge(tr_ready[1], uses(O, PAIRS - 1))
                    turn_lora(0)
                if p == F:
                    pe.wait_ge(fb_loaded, 32)
                    pe.wait_ge(lb_ready, 2 * NT)
                    pe.wait_ge(u_masked, NT)
                    for r in range(2):
                        for o in range(4):
                            last = nc.tensor.transpose(xps[2 + r][:, o * P:(o + 1) * P], ffn_b_nat[:, 4 * r + o, :], ident[:, :])
                    last.then_inc(fb_turned, 1)

            def products(p, u, c, dst, cols, close):
                r = p % 2
                for k in range(KC):
                    for n, (a, w) in enumerate(((act_hi, w_hi[r]), (act_hi, w_lo[r]), (act_lo, w_hi[r]))):
                        last = nc.tensor.matmul(dst, a[:, u, k, :], w[:, k, cols], start=(k == 0 and n == 0),
                                                stop=(close and k == KC - 1 and n == 2))
                return last

            def main(p, t, i, u):
                pe.wait_ge(act_hi_ready[u], uses(p, i) + 1)
                pe.wait_ge(act_lo_ready[u], uses(p, i) + 1)
                if p == H:
                    pe.wait_ge(la_ready, t + 1)
                    for k in range(KC):
                        last = nc.tensor.matmul(xps[2][0:R2, 256:256 + P], la_T[:, k, :], act_raw[:, u, k, :],
                                                start=(k == 0), stop=(k == KC - 1))
                    last.then_inc(u_done, 1)
                if p != F:
                    for c in range(2):
                        pe.wait_ge(acc_free[c], NT * p + t)
                        last = products(p, u, c, acc[c][:, :], slice(c * 512, (c + 1) * 512), p != H)
                        if p == H:
                            if c == 0:
                                pe.wait_ge(u_ready, t + 1)
                                pe.wait_ge(lb_ready, 2 * t + 2)
                            last = nc.tensor.matmul(acc[c][:, :], u_st[:, :], lb_st[:, c * 512:(c + 1) * 512], start=False, stop=True)
                        last.then_inc(acc_done[c][u], 1)
                    return
                for c in range(3):
                    pe.wait_ge(acc_free[c], (NT * F if c < 2 else 0) + t)
                    last = products(p, u, c, acc3[c][:, 0:FCH], slice(c * FCH, (c + 1) * FCH), True)
                    if c == 0:
                        last.then_inc(ag_done, 1)
                    if c == 1:
                        pe.wait_ge(a_ready, 2 * t + 2)
                        nc.tensor.transpose(wps[1][:, 0:P], a_parts[:, :, :].rearrange("p a r -> p (a r)"), ident[:, :]).then_inc(aT_done, 1)
                pe.wait_ge(aT_ready, t + 1)
                if isinstance(t, int) and t == 0:
                    pe.wait_ge(fb_lo, 2)
                for c in range(3):
                    first = AG if c == 0 else 0
                    for n, w in enumerate((w_hi[0], w_lo[0])):
                        last = nc.tensor.matmul(acc3[c][:, first:FCH], aT_st[:, :], w[:, 0, c * FCH + first - AG:(c + 1) * FCH - AG],
                                                start=False, stop=(n == 1), skip_group_check=True)
                    last.then_inc(acc_done[c][u], 1)

            def prep(p, b):
                if p != F:
                    turn_w(p + 1, b)

            def tail(p, t, i, u):
                if p == F:
                    return
                if p == V:
                    pe.wait_ge(acc_free[1], NT * V + t + 1)
                    pe.wait_ge(tr_ready[1 - u], uses(V, i + u))

                    def turn_probs(g):
                        pe.wait_ge(probs_ready, 4 * t + g + 1)
                        pe.wait_ge(pT_ready[g % 2], 2 * t + g // 2)
                        for n in range(4):
                            h = 8 * g + 2 * n
                            last = nc.tensor.transpose(xps[g % 2][:, n * P:(n + 1) * P],
                                                       scores[:, h:h + 2, :].rearrange("p h k -> p (h k)"), ident[:, :])
                        last.then_inc(pT_done, 1)

                    def weigh_v(g):
                        pe.wait_ge(pT_ready[g % 2], 2 * t + g // 2 + 1)
                        for n in range(4):
                            hp = 4 * g + n
                            for s in range(2):
                                col = hp // 2 % 4 * P + s * S
                                last = nc.tensor.matmul(xps[2 + hp // 8][S * (hp % 2):S * (hp % 2) + S, col:col + S],
                                                        v_bd[:, s, hp, :], pT_sb[:, g % 2, n, s * S:(s + 1) * S], start=True, stop=True)
                        last.then_inc(pT_used[g % 2] if g < 3 else turned[u], 1)

                    turn_probs(0)
                    for g in range(4):
                        if g < 3:
                            turn_probs(g + 1)
                        weigh_v(g)
                    return
                a, b = (0, 1) if p == H else (2 * u, 2 * u + 1)
                if p in (Q, K):
                    pe.wait_ge(nat_ready[u], uses(p, i) + 1)
                else:
                    for c in range(2):
                        pe.wait_ge(acc_free[c], NT * p + t + 1)
                pe.wait_ge(tr_ready[u], uses(p, i))
                if p == H:
                    pe.wait_ge(tr_ready[1 - u], uses(p, i + u))
                if p == O and isinstance(t, int) and t == NT - 1:
                    pe.wait_ge(la_ready, 1)
                    pe.wait_ge(lb_ready, 2)
                    pe.wait_ge(u_masked, 1)
                for k in range(KC):
                    last = nc.tensor.transpose(xps[(a, b)[k // 4]][:, k % 4 * P:(k % 4 + 1) * P], nat[:, u, k * P:(k + 1) * P], ident[:, :])
                last.then_inc(turned[u], 1)

            def mid(p, t, i, u):
                if p == H and isinstance(t, int) and t == 0:
                    pe.wait_ge(tr_ready[1], uses(O, PAIRS))
                if p == H and not (isinstance(t, int) and t == NT - 1):
                    turn_lora(t + 1)
                if p != V:
                    return
                pe.wait_ge(q_loaded, 16 * t + 16)
                pe.wait_ge(k_loaded, 16 * t + 16)
                if isinstance(t, int) and t == 0:
                    for w in range(2):
                        pe.wait_ge(tr_ready[w], uses(V, 0))
                else:
                    pe.wait_ge(tr_ready[1 - u], uses(V, i + u))
                pe.wait_ge(scores_biased, 4 * t)
                for c in range(KC):
                    for g in range(4):
                        rows = slice(DH * g, DH * g + DH)
                        for s in range(2):
                            last = nc.tensor.matmul(xps[g][s * S:(s + 1) * S, c * S:(c + 1) * S],
                                                    q_in[rows, c, s * S:(s + 1) * S], k_in[rows, c, s * S:(s + 1) * S],
                                                    start=True, stop=True)
                        if c == KC - 1:
                            last.then_inc(scores_done, 1)

            for b in range(KC):
                turn_w(Q, b)
            over_phases(pe, before, main, prep, tail, mid)

        @block.scalar
        def _(act):
            with act.Fori(0, PAIRS) as j:
                for u in range(2):
                    act.wait_ge(x_turned[u], j + 1)
                    act.wait_ge(xT_stored[u], 16 * j)
                    nc.scalar.activation(x_tr[:, u, 0:4, :].rearrange("p k n -> p (k n)"), xps[2 * u][:, :], ACT.Copy).then_inc(x_copied_a[u], 1)

            with act.Fori(0, QUARTERS) as q:
                for w in range(2):
                    act.wait_ge(cpair_done[w], 8 * q)
                with act.Fori(0, 2) as m:
                    for s in range(4):
                        for b in range(4):
                            act.wait_ge(wc_turned[b], 8 * q + 4 * m + s + 1)
                            nc.scalar.activation(wc_hi[:, bass.ds(4 * m + s, 1), 2 * b:2 * b + 2, :].rearrange("p e k n -> p (e k n)"),
                                                 xps[b][:, :], ACT.Copy).then_inc(wc_hi_ready[b], 1)

                def split_hi(j, u):
                    act.wait_ge(xT_loaded[u], 128 * q + 16 * j + 16)
                    act.wait_ge(cpair_done[u], 8 * q + j)
                    nc.scalar.activation(x_st[:, u, :, :, 0, :], x_in[:, u, :, :].rearrange("p k (s n) -> p k s n", s=2),
                                         ACT.Copy).then_inc(xs_hi_ready[u], 1)

                def main(t, j, u):
                    if not (isinstance(t, int) and t == NT - 1):
                        split_hi(j + u, 1 - u)
                    for s in range(2):
                        if s:
                            act.wait_ge(cpair_done[u], 8 * q + j + 1)
                        else:
                            act.wait_ge(cfirst_done, 16 * q + t + 1)
                        act.wait_ge(c_summed[s], 16 * q + t)
                        nc.scalar.activation(c_low[:, s, :], acc[s][S:P, 0:QO], ACT.Copy).then_inc(c_low_ready[s], 1)

                def tail(t, j, u):
                    act.wait_ge(c_turned[u], 8 * q + j + 1)
                    act.wait_ge(cT_stored[u], 128 * q + 16 * j)
                    nc.scalar.activation(cT_sb[:, u, :, :].rearrange("p o n -> p (o n)"), wps[u][:, 0:QO], ACT.Copy).then_inc(cT_ready[u], 1)

                split_hi(0, 0)
                over_pairs(act, main, tail)

            act.wait_ge(consts_ready, 1)

            def split_w(p, b):
                r = p % 2
                last_block = isinstance(b, int) and b == KC
                n, off = (AG, 0) if last_block else (P, AG if p == F else 0)
                if isinstance(b, int) and b == 0 and p >= 1:
                    for w in range(2):
                        act.wait_ge(acc_done[1][w], uses(p - 1, 0))
                for h in range(2):
                    act.wait_ge(w_turned[h], blocks(p, b) + 1)
                    cols = slice(0, AG) if last_block else bass.ds(off + b * P, P)
                    nc.scalar.activation(w_hi[r][:, 4 * h:4 * h + 4, cols],
                                         wps[h][:, :].rearrange("p (k n) -> p k n", k=4)[:, :, 0:n], ACT.Copy).then_inc(w_hi_ready[h], 1)

            def split_act(p, t, i, u):
                act.wait_ge(act_loaded[u], 16 * (uses(p, i) + 1))
                if p == F and not (isinstance(i, int) and i == 0):
                    act.wait_ge(acc_done[2][u], i)
                else:
                    act.wait_ge(acc_done[1][u], uses(p, i))
                nc.scalar.activation(act_hi[:, u, :, :], act_raw[:, u, :, :], ACT.Copy).then_inc(act_hi_ready[u], 1)

            def before(p):
                if p == H:
                    copy_lora0()
                if p == F:
                    act.wait_ge(fb_turned, 1)
                    for r in range(2):
                        nc.scalar.activation(w_hi[0][:, 0, r * 512:(r + 1) * 512], xps[2 + r][:, :], ACT.Copy).then_inc(fb_hi, 1)

            def copy_b(t, i, u):
                for r in range(2):
                    act.wait_ge(lb_turned, 2 * t + r + 1)
                    act.wait_ge(acc_done[1][1 - u], uses(H, i + u))
                    nc.scalar.activation(lb_st[:, r * 512:(r + 1) * 512], xps[3][:, :], ACT.Copy).then_inc(lb_ready, 1)

            def copy_a(t):
                act.wait_ge(la_turned, t + 1)
                act.wait_ge(u_done, t)
                nc.scalar.activation(la_T[:, :, :].rearrange("p k r -> p (k r)"), xps[2][:, 0:KC * R2], ACT.Copy).then_inc(la_ready, 1)

            def copy_lora0():
                copy_a(0)
                for r in range(2):
                    act.wait_ge(lb_turned, r + 1)
                    nc.scalar.activation(lb_st[:, r * 512:(r + 1) * 512], xps[3][:, :], ACT.Copy).then_inc(lb_ready, 1)

            def main(p, t, i, u):
                if not (isinstance(t, int) and t == NT - 1):
                    split_act(p, t + 1, i + u, 1 - u)
                elif p != F:
                    split_act(p + 1, 0, 0, 0)
                if p in (Q, K):
                    act.wait_ge(var_ready, NT * p + t + 1)
                    nc.scalar.activation(std_rstd[:, 0:1], mean_var[:, 1:2], ACT.Sqrt, bias=eps_col[:, 0:1]).then_inc(std_ready, 1)
                if p == F:
                    act.wait_ge(gate_step, 7 * t + 3)
                    nc.scalar.activation(gate[:, 4, :], gate[:, 3, :], ACT.Exp).then_inc(gate_exp, 1)
                    act.wait_ge(aT_done, t + 1)
                    act.wait_ge(acc_free[2], t)
                    nc.scalar.activation(aT_st[:, :], wps[1][:, 0:P], ACT.Copy).then_inc(aT_ready, 1)

            def prep(p, b):
                if p != F:
                    split_w(p + 1, b)

            def tail(p, t, i, u):
                if p == F:
                    return
                if p == V:
                    for g in range(4):
                        act.wait_ge(pT_done, 4 * t + g + 1)
                        if g >= 2:
                            act.wait_ge(pT_used[g % 2], (2 * t if g % 2 == 0 else t) + 1)
                        elif g == 0:
                            act.wait_ge(pT_used[0], 2 * t)
                        elif not (isinstance(t, int) and t == 0):
                            act.wait_ge(turned[1 - u], uses(V, i + u))
                        nc.scalar.activation(pT_sb[:, g % 2, :, :].rearrange("p a n -> p (a n)"), xps[g % 2][:, :], ACT.Copy).then_inc(pT_ready[g % 2], 1)
                act.wait_ge(turned[u], uses(p, i) + 1)
                act.wait_ge(tr_stored[u], 16 * uses(p, i))
                if p in (Q, K):
                    for k in range(KC):
                        last = nc.scalar.activation(tr_sb[:, u, k, :], xps[2 * u + k // 4][:, k % 4 * P:(k % 4 + 1) * P], ACT.Identity,
                                                    scale=ln_cols[:, 2 * p, k:k + 1], bias=ln_cols[:, 2 * p + 1, k:k + 1])
                else:
                    a = {V: 2, O: 2 * u, H: 0}[p]
                    for h in range(2):
                        last = nc.scalar.activation(tr_sb[:, u, 4 * h:4 * h + 4, :].rearrange("p k n -> p (k n)"), xps[a + h][:, :], ACT.Copy)
                last.then_inc(tr_ready[u], 1)

            def mid(p, t, i, u):
                if p == H and not (isinstance(t, int) and t == NT - 1):
                    copy_a(t + 1)
                    copy_b(t + 1, i + u, 1 - u)
                if p != V:
                    return
                for g in range(4):
                    act.wait_ge(shifted, 4 * t + g + 1)
                    part = scores[:, 8 * g:8 * g + 8, :]
                    nc.scalar.activation(part, part, ACT.Exp).then_inc(exp_ready, 1)

            act.wait_ge(cols_scaled, 1)
            for b in range(KC):
                split_w(Q, b)
            split_act(Q, 0, 0, 0)
            over_phases(act, before, main, prep, tail, mid)

        @block.vector
        def _(dve):
            with dve.Fori(0, PAIRS) as j:
                for u in range(2):
                    dve.wait_ge(x_turned[u], j + 1)
                    dve.wait_ge(xT_stored[u], 16 * j)
                    nc.vector.tensor_copy(x_tr[:, u, 4:8, :].rearrange("p k n -> p (k n)"), xps[2 * u + 1][:, :]).then_inc(x_copied_v[u], 1)

            dve.wait_ge(cols_in, 64)
            nc.vector.tensor_scalar(ln_cols[:, 0:2, :], ln_cols[:, 0:2, :], SCALE, None, ALU.mult).then_inc(cols_scaled, 1)

            with dve.Fori(0, QUARTERS) as q:
                with dve.Fori(0, 2) as m:
                    for s in range(4):
                        for b in range(4):
                            dve.wait_ge(wc_hi_ready[b], 8 * q + 4 * m + s + 1)
                            at = (slice(None), bass.ds(4 * m + s, 1), slice(2 * b, 2 * b + 2), slice(None))
                            nc.vector.tensor_tensor(wc_lo[at].rearrange("p e k n -> p (e k n)"), xps[b][:, :],
                                                    wc_hi[at].rearrange("p e k n -> p (e k n)").bitcast(F32), ALU.subtract).then_inc(wc_lo_ready[b], 1)

                def main(t, j, u):
                    for s in range(2):
                        dve.wait_ge(c_low_ready[s], 16 * q + t + 1)
                        dve.wait_ge(c_turned[u], 8 * q + j)
                        nc.vector.tensor_tensor(c_nat[s * S:(s + 1) * S, u, :], acc[s][0:S, 0:QO], c_low[:, s, :], ALU.add).then_inc(c_summed[s], 1)

                over_pairs(dve, main, nothing)

            def split_w(p, b):
                r = p % 2
                last_block = isinstance(b, int) and b == KC
                n, off = (AG, 0) if last_block else (P, AG if p == F else 0)
                for h in range(2):
                    dve.wait_ge(w_hi_ready[h], blocks(p, b) + 1)
                    cols = slice(0, AG) if last_block else bass.ds(off + b * P, P)
                    nc.vector.tensor_tensor(w_lo[r][:, 4 * h:4 * h + 4, cols],
                                            wps[h][:, :].rearrange("p (k n) -> p k n", k=4)[:, :, 0:n],
                                            w_hi[r][:, 4 * h:4 * h + 4, cols].bitcast(F32), ALU.subtract).then_inc(w_lo_ready[h], 1)

            def split_b(t):
                dve.wait_ge(lb_loaded, 32 * t + 32)
                dve.wait_ge(lb_turned, 2 * t)
                hi, lo = lb_parts[:, :, 0, :], lb_parts[:, :, 1, :]
                nc.vector.tensor_copy(hi.bitcast(F32R), lb_raw[:, :, :]).then_inc(lb_split, 1)
                nc.vector.tensor_copy(lb_parts[:, :, 2, :].bitcast(F32R), lb_raw[:, :, :]).then_inc(lb_split, 1)
                dve.wait_ge(lb_split, 4 * t + 1)
                nc.vector.tensor_tensor(lo.bitcast(F32R), lb_raw[:, :, :], hi, ALU.subtract).then_inc(lb_split, 1)
                nc.vector.tensor_tensor(lb_parts[:, :, 3, :].bitcast(F32R), lb_raw[:, :, :], hi, ALU.subtract).then_inc(lb_split, 1)

            def before(p):
                if p == H:
                    split_b(0)
                    dve.wait_ge(bias_h_in, 16)
                    dve.wait_ge(mask_ready, 3)
                if p == F:
                    dve.wait_ge(fb_hi, 2)
                    for r in range(2):
                        nc.vector.tensor_tensor(w_lo[0][:, 0, r * 512:(r + 1) * 512], xps[2 + r][:, :],
                                                w_hi[0][:, 0, r * 512:(r + 1) * 512].bitcast(F32), ALU.subtract).then_inc(fb_lo, 1)
                    dve.wait_ge(gate_b_in, 16)

            def main(p, t, i, u):
                if p in (Q, K):
                    n = NT * p + t
                    dve.wait_ge(turned[u], uses(p, i))
                    for c in range(2):
                        dve.wait_ge(acc_done[c][u], uses(p, i) + 1)
                        nc.vector.tensor_scalar(nat[:, u, c * 512:(c + 1) * 512], acc[c][:, :], CLIP, -CLIP, ALU.min, ALU.max).then_inc(acc_free[c], 1)
                    for c in range(2):
                        dve.wait_ge(acc_free[c], n + 1)
                        nc.vector.bn_stats(bn_st[:, c, :], nat[:, u, c * 512:(c + 1) * 512]).then_inc(stats_step, 1)
                    dve.wait_ge(stats_step, 3 * n + 2)
                    nc.vector.tensor_copy(wait_pad[:, :], bn_st[:, 1, 0:1])
                    nc.vector.bn_aggr(mean_var[:, :], bn_st[:, :, :].rearrange("p a b -> p (a b)")).then_inc(var_ready, 1)
                    dve.wait_ge(std_ready, n + 1)
                    nc.vector.reciprocal(std_rstd[:, 1:2], std_rstd[:, 0:1]).then_inc(stats_step, 1)
                    dve.wait_ge(stats_step, 3 * n + 3)
                    dve.wait_ge(var_ready, n + 1)
                    nc.vector.tensor_scalar(nat[:, u, :], nat[:, u, :], mean_var[:, 0:1], std_rstd[:, 1:2],
                                            ALU.subtract, ALU.mult).then_inc(nat_ready[u], 1)
                if p == V:
                    if isinstance(t, int) and t == 0:
                        dve.wait_ge(alibi_step, HEADS + 5)
                    else:
                        dve.wait_ge(turned[1 - u], uses(V, i + u))
                    for c in range(2):
                        dve.wait_ge(acc_done[c][u], uses(p, i) + 1)
                        heads = acc[c][:, :].rearrange("p (a two g d) -> p g a two d", two=2, g=4, d=DH)
                        for s in range(2):
                            pairs = v_bd[:, s, :, :].rearrange("p (g m) d -> p g m d", g=4)
                            for two in range(2):
                                last = nc.vector.tensor_scalar(pairs[two * S:(two + 1) * S, :, 2 * c:2 * c + 2, two * DH:(two + 1) * DH],
                                                               heads[s * S:(s + 1) * S, :, :, two, :], CLIP, -CLIP, ALU.min, ALU.max)
                        last.then_inc(acc_free[c], 1)
                if p == O:
                    dve.wait_ge(turned[u], uses(p, i))
                    if isinstance(t, int) and t == 0:
                        dve.wait_ge(turned[1], uses(O, 0))
                    dve.wait_ge(x1_stored[u], 16 * i)
                    dve.wait_ge(res_loaded[u], 16 * i + 16)
                    for c in range(2):
                        dve.wait_ge(acc_done[c][u], uses(p, i) + 1)
                        part = (slice(None), u, slice(c * 512, (c + 1) * 512))
                        nc.vector.tensor_tensor(nat[part], acc[c][:, :], aux[part], ALU.add).then_inc(acc_free[c], 1)
                if p == H:
                    dve.wait_ge(u_done, t + 1)
                    nc.vector.tensor_tensor(u_seq[:, :], xps[2][0:R2, 256:256 + P], seq_mask[:, :], ALU.mult).then_inc(u_masked, 1)
                    dve.wait_ge(u_masked, t + 1)
                    if not (isinstance(t, int) and t == 0):
                        dve.wait_ge(acc_done[1][1 - u], uses(H, i + u))
                    nc.vector.tensor_copy(u_st[0:R2, :], u_seq[:, :]).then_inc(u_step, 1)
                    nc.vector.tensor_copy(u_st[R2:2 * R2, :], u_seq[:, :]).then_inc(u_step, 1)
                    dve.wait_ge(u_step, 3 * t + 2)
                    nc.vector.tensor_tensor(u_st[2 * R2:3 * R2, :], u_seq[:, :], u_st[0:R2, :].bitcast(F32), ALU.subtract).then_inc(u_step, 1)
                    nc.vector.tensor_tensor(u_st[3 * R2:4 * R2, :], u_seq[:, :], u_st[0:R2, :].bitcast(F32), ALU.subtract).then_inc(u_ready, 1)
                    dve.wait_ge(turned[u], uses(p, i))
                    dve.wait_ge(x1_stored[u], 16 * PAIRS)
                    for c in range(2):
                        dve.wait_ge(acc_done[c][u], uses(p, i) + 1)
                        nc.vector.tensor_tensor(nat[:, u, c * 512:(c + 1) * 512], acc[c][:, :], bias_row[:, c * 512:(c + 1) * 512], ALU.add).then_inc(acc_free[c], 1)
                if p == F:
                    gates(t)
                    dve.wait_ge(turned[u], uses(F, 0))
                    dve.wait_ge(out_stored[u], 16 * i)
                    dve.wait_ge(xb_ready, t + 1)
                    for c in range(3):
                        dve.wait_ge(acc_done[c][u], (uses(p, i) if c < 2 else i) + 1)
                        first = AG if c == 0 else 0
                        part = (slice(None), u, slice(c * FCH + first - AG, (c + 1) * FCH - AG))
                        nc.vector.tensor_tensor(nat[part], acc3[c][:, first:FCH], aux[part], ALU.add).then_inc(acc_free[c], 1)

            def gates(t):
                n = 7 * t
                dve.wait_ge(ag_done, t + 1)
                nc.vector.tensor_tensor(gate[:, 1, :], acc[0][:, MAXR:AG], gate[:, 0, :], ALU.add).then_inc(gate_step, 1)
                dve.wait_ge(gate_step, n + 1)
                nc.vector.tensor_reduce(gate[:, 2, 0:1], gate[:, 1, :], AX_X, ALU.max).then_inc(gate_step, 1)
                dve.wait_ge(gate_step, n + 2)
                nc.vector.tensor_scalar(gate[:, 3, :], gate[:, 1, :], gate[:, 2, 0:1], None, ALU.subtract).then_inc(gate_step, 1)
                dve.wait_ge(gate_exp, t + 1)
                nc.vector.tensor_scalar(gate[:, 5, :], gate[:, 4, :], 1.0, None, ALU.is_lt).then_inc(gate_step, 1)
                dve.wait_ge(gate_step, n + 4)
                nc.vector.tensor_tensor(gate[:, 6, 0:1], gate[:, 5, 0:1], gate[:, 5, 1:2], ALU.mult).then_inc(gate_step, 1)
                dve.wait_ge(gate_step, n + 5)
                nc.vector.tensor_tensor(gate[:, 7, 0:1], gate[:, 6, 0:1], gate[:, 5, 2:3], ALU.mult).then_inc(gate_step, 1)
                dve.wait_ge(gate_step, n + 6)
                nc.vector.tensor_copy(a_msk[:, 0:8], acc[0][:, 0:8])
                nc.vector.tensor_scalar(a_msk[:, 8:16], acc[0][:, 8:16], gate[:, 5, 0:1], None, ALU.mult)
                nc.vector.tensor_scalar(a_msk[:, 16:32], acc[0][:, 16:32], gate[:, 6, 0:1], None, ALU.mult)
                nc.vector.tensor_scalar(a_msk[:, 32:64], acc[0][:, 32:64], gate[:, 7, 0:1], None, ALU.mult).then_inc(gate_step, 1)
                dve.wait_ge(gate_step, n + 7)
                dve.wait_ge(aT_done, t)
                nc.vector.tensor_copy(a_parts[:, 0, :].bitcast(F32R), a_msk[:, :]).then_inc(a_ready, 1)
                dve.wait_ge(a_ready, 2 * t + 1)
                nc.vector.tensor_tensor(a_parts[:, 1, :].bitcast(F32R), a_msk[:, :], a_parts[:, 0, :], ALU.subtract).then_inc(a_ready, 1)

            def prep(p, b):
                if p != F:
                    split_w(p + 1, b)

            def mid(p, t, i, u):
                if p == H and not (isinstance(t, int) and t == NT - 1):
                    split_b(t + 1)
                if p != V:
                    return
                if isinstance(t, int) and t == 0:
                    for w in range(2):
                        dve.wait_ge(turned[w], uses(V, 0))
                for g in range(4):
                    n, part = 4 * t + g, scores[:, 8 * g:8 * g + 8, :]
                    dve.wait_ge(scores_done, n + 1)
                    nc.vector.tensor_tensor(part, xps[g][:, :].rearrange("p (h k) -> p h k", k=S), alibi[:, 8 * g:8 * g + 8, :], ALU.add).then_inc(scores_biased, 1)
                    dve.wait_ge(scores_biased, n + 1)
                    nc.vector.tensor_reduce(smax[:, 8 * g:8 * g + 8], part, AX_X, ALU.max).then_inc(max_ready, 1)
                    dve.wait_ge(max_ready, n + 1)
                    nc.vector.tensor_tensor(part, part, smax[:, 8 * g:8 * g + 8].unsqueeze(2).to_broadcast([P, 8, S]), ALU.subtract).then_inc(shifted, 1)
                for g in range(4):
                    n, part = 4 * t + g, scores[:, 8 * g:8 * g + 8, :]
                    dve.wait_ge(exp_ready, n + 1)
                    nc.vector.tensor_reduce(ssum[:, 8 * g:8 * g + 8], part, AX_X, ALU.add).then_inc(sum_ready, 1)
                    dve.wait_ge(sum_ready, n + 1)
                    nc.vector.reciprocal(smax[:, 8 * g:8 * g + 8], ssum[:, 8 * g:8 * g + 8]).then_inc(rsum_ready, 1)
                    dve.wait_ge(rsum_ready, n + 1)
                    nc.vector.tensor_tensor(part, part, smax[:, 8 * g:8 * g + 8].unsqueeze(2).to_broadcast([P, 8, S]), ALU.mult).then_inc(probs_ready, 1)

            for b in range(KC):
                split_w(Q, b)
            over_phases(dve, before, main, prep, nothing, mid)

        @block.gpsimd
        def _(pool):
            nc.gpsimd.memset(ident[:, :], 0.0).then_inc(ident_ready, 1)
            nc.gpsimd.memset(eps_col[:, :], LN_EPS).then_inc(consts_ready, 1)
            pool.wait_ge(ident_ready, 1)
            nc.gpsimd.affine_select(out=ident[:, :], in_=ident[:, :], compare_op=ALU.not_equal, fill=1.0, base=0,
                                    pattern=[[-1, P]], channel_multiplier=1).then_inc(ident_ready, 1)
            nc.gpsimd.memset(seq_mask[:, :], 1.0).then_inc(mask_ready, 1)
            pool.wait_ge(mask_ready, 1)
            nc.gpsimd.affine_select(out=seq_mask[:, :].rearrange("r (s n) -> r s n", s=2), in_=seq_mask[:, :].rearrange("r (s n) -> r s n", s=2),
                                    compare_op=ALU.is_ge, fill=0.0, base=0, pattern=[[-RANK, 2], [0, S]], channel_multiplier=1).then_inc(mask_ready, 1)
            pool.wait_ge(mask_ready, 2)
            nc.gpsimd.affine_select(out=seq_mask[:, :].rearrange("r (s n) -> r s n", s=2), in_=seq_mask[:, :].rearrange("r (s n) -> r s n", s=2),
                                    compare_op=ALU.is_ge, fill=0.0, base=RANK - 1, pattern=[[RANK, 2], [0, S]], channel_multiplier=-1).then_inc(mask_ready, 1)

            with pool.Fori(0, QUARTERS) as q:
                def split_lo(j, u):
                    pool.wait_ge(xs_hi_ready[u], 8 * q + j + 1)
                    nc.gpsimd.tensor_tensor(x_st[:, u, :, :, 1, :], x_in[:, u, :, :].rearrange("p k (s n) -> p k s n", s=2),
                                            x_st[:, u, :, :, 0, :].bitcast(F32), ALU.subtract).then_inc(xs_lo_ready[u], 1)

                def main(t, j, u):
                    if not (isinstance(t, int) and t == NT - 1):
                        split_lo(j + u, 1 - u)

                split_lo(0, 0)
                over_pairs(pool, main, nothing)

            for u in range(2):
                pool.wait_ge(cT_stored[u], 16 * QUARTERS * PAIRS)

            def split_act(p, i, u):
                pool.wait_ge(act_hi_ready[u], uses(p, i) + 1)
                nc.gpsimd.tensor_tensor(act_lo[:, u, :, :], act_raw[:, u, :, :], act_hi[:, u, :, :].bitcast(F32), ALU.subtract).then_inc(act_lo_ready[u], 1)

            def build_alibi():
                nc.gpsimd.memset(v_bd[:, :, :, :], 0.0).then_inc(alibi_step, 1)
                for s in range(2):
                    pool.wait_ge(alibi_step, s + 1)
                    nc.gpsimd.iota(rel[s * S:(s + 1) * S, :], pattern=[[1, S]], base=0, channel_multiplier=-1,
                                   allow_small_or_imprecise_dtypes=True).then_inc(alibi_step, 1)
                pool.wait_ge(alibi_step, 3)
                for n in range(HEADS):
                    nc.gpsimd.tensor_scalar(alibi[:, n, :], rel[:, :], SLOPES[4 * (n % 8) + n // 8], None, ALU.mult).then_inc(alibi_step, 1)
                for s in range(2):
                    pool.wait_ge(alibi_step, HEADS + 3 + s)
                    rows = alibi[s * S:(s + 1) * S, :, :]
                    nc.gpsimd.affine_select(out=rows, in_=rows, compare_op=ALU.is_ge, fill=MASKED, base=0,
                                            pattern=[[0, HEADS], [-1, S]], channel_multiplier=1).then_inc(alibi_step, 1)
                pool.wait_ge(alibi_step, HEADS + 5)

            def main(p, t, i, u):
                if not (isinstance(t, int) and t == NT - 1):
                    split_act(p, i + u, 1 - u)
                elif p != F:
                    split_act(p + 1, 0, 0)
                if p == F:
                    if isinstance(t, int) and t == 0:
                        pool.wait_ge(bias_f_in, 16)
                    pool.wait_ge(res_loaded[u], 16 * (PAIRS + i + 1))
                    nc.gpsimd.tensor_tensor(aux[:, u, :], aux[:, u, :], bias_row[:, :], ALU.add).then_inc(xb_ready, 1)

            split_act(Q, 0, 0)
            build_alibi()
            over_phases(pool, nothing, main, nothing, nothing, nothing)


_INS = ["x", "itok_B_3_7", "itok_B_6_15", "L0_cond_weight", "L0_attn_w_qkv", "L0_attn_q_ln_w", "L0_attn_q_ln_b",
        "L0_attn_k_ln_w", "L0_attn_k_ln_b", "L0_attn_w_out", "L0_cond2_base_weight", "L0_cond2_base_bias",
        "L0_cond2_lora_A_w", "L0_cond2_lora_B_w", "L0_ffn_W", "L0_ffn_b", "L0_ffn_A", "L0_ffn_B",
        "L0_ffn_gate_w", "L0_ffn_gate_b"]


def kernel(**inputs):
    import numpy as _np
    import concourse.bacc as _bacc
    from concourse import mybir as _mybir
    from concourse.bass_utils import run_bass_kernel_spmd as _run

    nc = _bacc.Bacc("TRN2", target_bir_lowering=False, num_devices=1)
    arrays, args = {}, []
    for name in _INS:
        a = _np.ascontiguousarray(inputs[name])
        arrays[f"in_{name}"] = a
        args.append(nc.dram_tensor(f"in_{name}", a.shape, _mybir.dt.from_np(a.dtype), kind="ExternalInput").ap())
    args.append(nc.dram_tensor("out_0", inputs["x"].shape, _mybir.dt.float32, kind="ExternalOutput").ap())
    adaln_attention_ffn(nc, *args)
    r = _run(nc, [arrays], core_ids=[0])
    return r.results[0]["out_0"]
```

```python
from contextlib import ExitStack
from functools import partial

import numpy as np

import concourse.bass as bass
from concourse import mybir

ALU = mybir.AluOpType
ACT = mybir.ActivationFunctionType
AX_X = mybir.AxisListType.X
F32 = mybir.dt.float32
F32R = mybir.dt.float32r
I32 = mybir.dt.int32

P = 128
MASKED = -3.0e38
CLIP = 8.0
LN_EPS = 1e-5
QUARTERS = 4
RAW_SLOTS = 8

Q, K, V, O, H, F = range(6)


def adaln_attention_ffn(nc, x, ids_expert, ids_lora, w_cond, w_qkv, q_w, q_b, k_w, k_b, w_out,
                        w_base, b_base, lora_a, lora_b, w_ffn, b_ffn, ffn_a, ffn_b, gate_w, gate_b, out):
    B, S, D = x.shape
    E = w_cond.shape[0]
    KC = D // P
    NT = B * S // P
    PAIRS = NT // 2
    HEADS = 32
    DH = D // HEADS
    QO = D // QUARTERS
    OB = QO // P
    RANK = lora_a.shape[1]
    N_LORA = lora_a.shape[0]
    MAXR = ffn_a.shape[0]
    NG = gate_w.shape[0]
    AG = MAXR + NG
    R2 = 2 * RANK
    FCH = (D + AG) // 3
    assert S * 2 == P and FCH * 3 == D + AG and 4 * R2 == P and 2 * MAXR == P and NG == 4
    assert RAW_SLOTS == KC and E * OB == 2 * RAW_SLOTS and OB == 2 and E == 8
    assert D % 512 == 0 and NT % 2 == 0 and HEADS * S == 2048
    SCALE = float(DH) ** -0.5
    SLOPES = [float(np.float32(1.0) / np.float32(2.0) ** np.float32((h + 1) * 8.0 / HEADS)) for h in range(HEADS)]

    x_rows = x.rearrange("b s d -> (b s) d").rearrange("(t p) d -> t p d", p=P)
    out_rows = out.rearrange("b s d -> (b s) d").rearrange("(t p) d -> t p d", p=P)
    wc_rows = w_cond.rearrange("e (q ob p) i -> q ob e p i", q=QUARTERS, p=P)
    w_rows = {Q: w_qkv[0:D, :], K: w_qkv[D:2 * D, :], V: w_qkv[2 * D:3 * D, :], O: w_out, H: w_base, F: w_ffn}
    lora_b_rows = lora_b.rearrange("n (o p) r -> n p o r", p=P)
    ffn_b_rows = ffn_b.rearrange("(o p) r -> p o r", p=P)

    def dram(name, chunked):
        return nc.dram_tensor(name, (NT, P, KC, P) if chunked else (NT, P, D), F32).ap()

    xT_d = dram("xT_d", True)
    cT_d = dram("cT_d", True)
    tr_d = {Q: dram("qT_d", True), K: dram("kT_d", True), V: dram("attT_d", True),
            O: dram("x1T_d", True), H: dram("hT_d", True)}
    x1_d = dram("x1_d", False)
    act_src = {Q: cT_d, K: cT_d, V: cT_d, O: tr_d[V], H: tr_d[O], F: tr_d[H]}

    with ExitStack() as ctx:
        def sb(name, shape, dt=F32, scope=ctx):
            return scope.enter_context(nc.sbuf_tensor(name, shape, dt))

        def sem(name):
            return ctx.enter_context(nc.semaphore(name))

        def sem2(name):
            return [sem(f"{name}{u}") for u in range(2)]

        ident = sb("ident", [P, P])
        ids_sb = sb("ids_sb", [1, 2 * B], I32)
        ln_cols = sb("ln_cols", [P, 4, KC])
        eps_col = sb("eps_col", [P, 1])
        bn_st = sb("bn_st", [P, 2, 6])
        mean_var = sb("mean_var", [P, 2])
        std_rstd = sb("std_rstd", [P, 2])
        wait_pad = sb("wait_pad", [P, 1])
        seq_mask = sb("seq_mask", [R2, P])

        w_raw = sb("w_raw", [P, D])

        cond = ExitStack()
        wc = sb("wc", [P, E, KC, 2, QO], F32R, cond)
        c_sum = sb("c_sum", [P, 2, 2, QO], F32, cond)
        over_w = sb("over_w", [P, 2 * KC * (D + D + AG) - 2 * E * KC * QO - 4 * QO], F32, cond)
        x_in = sb("x_in", [P, 2, KC, P], F32, cond)
        x_tr = sb("x_tr", [P, 2, KC, P], F32, cond)
        x_st = sb("x_st", [P, 2, KC, 2, 2, S], F32R, cond)
        wc_raw = sb("wc_raw", [P, RAW_SLOTS, D], F32, cond)
        c_low = sb("c_low", [S, 2, 2, QO], F32, cond)
        cT_sb = sb("cT_sb", [P, 2, OB, P], F32, cond)
        cond.close()

        w_hi = [sb("w0_hi", [P, KC, D], F32R), sb("w1_hi", [P, KC, AG + D], F32R)]
        w_lo = [sb("w0_lo", [P, KC, D], F32R), sb("w1_lo", [P, KC, AG + D], F32R)]
        act_raw = sb("act_raw", [P, 2, KC, P])
        act_hi = sb("act_hi", [P, 2, KC, P], F32R)
        act_lo = sb("act_lo", [P, 2, KC, P], F32R)
        nat = sb("nat", [P, 2, D])
        aux = sb("aux", [P, 2, D])
        tr_sb = sb("tr_sb", [P, 2, KC, P])
        attn = ExitStack()
        v_bd = sb("v_bd", [P, 2, HEADS // 2, 2 * DH], F32, attn)
        alibi = sb("alibi", [P, HEADS, S], F32, attn)
        pT_sb = sb("pT_sb", [P, 2, 4, P], F32, attn)
        rel = sb("rel", [P, S], F32, attn)
        smax = sb("smax", [P, HEADS], F32, attn)
        ssum = sb("ssum", [P, HEADS], F32, attn)
        attn.close()
        bias_row = sb("bias_row", [P, D])
        la_T = sb("la_T", [P, KC, R2])
        la_raw = sb("la_raw", [R2, D])
        lb_raw = sb("lb_raw", [P, KC, R2])
        lb_parts = sb("lb_parts", [P, KC, 4, R2])
        lb_st = sb("lb_st", [P, D], F32R)
        u_seq = sb("u_seq", [R2, P])
        u_st = sb("u_st", [P, P], F32R)
        a_msk = sb("a_msk", [P, MAXR])
        a_parts = sb("a_parts", [P, 2, MAXR])
        aT_st = sb("aT_st", [P, P], F32R)
        gate = sb("gate", [P, 10, NG])
        q_in, k_in = (aux[:, n, :].rearrange("p (k n) -> p k n", k=KC) for n in range(2))
        v_nat = tr_sb[:, 0, :, :].rearrange("p k n -> p (k n)")
        scores = nat[:, :, :].rearrange("p a n -> p (a n)").rearrange("p (h k) -> p h k", k=S)
        ffn_b_nat = lb_parts[:, :, :, :].rearrange("p k a r -> p k (a r)")

        def bank(name):
            return ctx.enter_context(nc.psum_tensor(name, [P, 512], F32))

        acc = [bank("acc0"), bank("acc1")]
        wps = [bank("wps0"), bank("wps1")]
        xps = [bank(f"xps{n}") for n in range(4)]
        acc3 = [acc[0], acc[1], wps[0]]

        ids_in, ident_ready, cols_in, cols_scaled, consts_ready = (
            sem(n) for n in ("ids_in", "ident_ready", "cols_in", "cols_scaled", "consts_ready"))
        x_loaded, xT_stored = sem2("x_loaded"), sem2("xT_stored")
        x_turned, x_copied_a, x_copied_v = (sem(n) for n in ("x_turned", "x_copied_a", "x_copied_v"))
        wc_loaded = [sem(f"wc_loaded{s}") for s in range(RAW_SLOTS)]
        wc_turned, wc_hi_ready, wc_lo_ready = (
            [sem(f"{n}{b}") for b in range(4)] for n in ("wc_turned", "wc_hi_ready", "wc_lo_ready"))
        xT_loaded, xs_hi_ready, xs_lo_ready, c_low_ready, c_summed, c_ready, cpair_done, c_turned, cT_ready, cT_stored = (
            sem2(n) for n in ("xT_loaded", "xs_hi_ready", "xs_lo_ready", "c_low_ready", "c_summed", "c_ready",
                              "cpair_done", "c_turned", "cT_ready", "cT_stored"))
        cfirst_done, w_loaded = sem("cfirst_done"), sem("w_loaded")
        w_turned, w_hi_ready, w_lo_ready = (sem2(n) for n in ("w_turned", "w_hi_ready", "w_lo_ready"))
        act_loaded, act_hi_ready, act_lo_ready = (sem2(n) for n in ("act_loaded", "act_hi_ready", "act_lo_ready"))
        acc_done = [sem2(f"acc_done{c}_") for c in range(3)]
        acc_free = [sem(f"acc_free{c}") for c in range(3)]
        stats_step, var_ready, std_ready = (sem(n) for n in ("stats_step", "var_ready", "std_ready"))
        nat_ready, turned, tr_ready, tr_stored = (sem2(n) for n in ("nat_ready", "turned", "tr_ready", "tr_stored"))
        q_loaded, k_loaded, scores_done, scores_biased, max_ready, shifted, exp_ready, sum_ready, rsum_ready, probs_ready, pT_done = (
            sem(n) for n in ("q_loaded", "k_loaded", "scores_done", "scores_biased", "max_ready", "shifted",
                             "exp_ready", "sum_ready", "rsum_ready", "probs_ready", "pT_done"))
        pT_ready, pT_used = sem2("pT_ready"), sem2("pT_used")
        alibi_step, v_spread = sem("alibi_step"), sem("v_spread")
        res_loaded, x1_stored, out_stored = (sem2(n) for n in ("res_loaded", "x1_stored", "out_stored"))
        bias_h_in, bias_f_in, gate_b_in, mask_ready = (
            sem(n) for n in ("bias_h_in", "bias_f_in", "gate_b_in", "mask_ready"))
        la_loaded, lb_loaded, fb_loaded = sem2("la_loaded"), sem2("lb_loaded"), sem2("fb_loaded")
        la_turned, la_ready, lb_split, lb_turned, lb_ready = (
            sem(n) for n in ("la_turned", "la_ready", "lb_split", "lb_turned", "lb_ready"))
        u_done, u_masked, u_step, u_ready = (sem(n) for n in ("u_done", "u_masked", "u_step", "u_ready"))
        fb_turned, fb_hi, fb_lo = (sem(n) for n in ("fb_turned", "fb_hi", "fb_lo"))
        ag_done, gate_step, gate_exp, a_ready, aT_done, aT_ready, xb_ready = (
            sem(n) for n in ("ag_done", "gate_step", "gate_exp", "a_ready", "aT_done", "aT_ready", "xb_ready"))

        def over_tiles(eng, main, tail):
            def pair(j):
                main(2 * j + 1, j, 1)
                tail(2 * j, j, 0)
                main(2 * j + 2, j + 1, 0)
                tail(2 * j + 1, j, 1)

            main(0, 0, 0)
            with eng.Fori(0, PAIRS - 2) as j:
                pair(j)
            pair(PAIRS - 2)
            main(NT - 1, PAIRS - 1, 1)
            tail(NT - 2, PAIRS - 1, 0)
            tail(NT - 1, PAIRS - 1, 1)

        def banks(s):
            return 2 * (s % 2), 2 * (s % 2) + 1

        def turns(q, m, s):
            return RAW_SLOTS * q + RAW_SLOTS // 2 * m + s // 2

        def over_phases(eng, before, main, prep, tail, mid):
            for p in (Q, K, V, O, H, F):
                def pair(j):
                    main(p, 2 * j + 1, j, 1)
                    prep(p, j + 1)
                    tail(p, 2 * j, j, 0)
                    mid(p, 2 * j + 1, j, 1)
                    main(p, 2 * j + 2, j + 1, 0)
                    tail(p, 2 * j + 1, j, 1)
                    mid(p, 2 * j + 2, j + 1, 0)

                before(p)
                main(p, 0, 0, 0)
                prep(p, 0)
                if p != Q:
                    tail(p - 1, NT - 1, PAIRS - 1, 1)
                mid(p, 0, 0, 0)
                with eng.Fori(0, PAIRS - 2) as j:
                    pair(j)
                pair(PAIRS - 2)
                main(p, NT - 1, PAIRS - 1, 1)
                if p == H:
                    prep(p, KC)
                tail(p, NT - 2, PAIRS - 1, 0)
                mid(p, NT - 1, PAIRS - 1, 1)
            tail(F, NT - 1, PAIRS - 1, 1)

        def uses(p, i):
            return PAIRS * p + i

        def blocks(p, b):
            return KC * p + b

        def nothing(*_):
            pass

        def loads(p, b):
            if p < O:
                return KC * (p - 1) + b + 1
            return KC * (p - 1) + 4 * (b + 1) if p == O else KC * (p + 2) + b + 1

        block = ctx.enter_context(nc.Block())

        @block.sync
        def _(sp):
            sp.dma_start(ids_sb[0:1, 0:B], ids_expert.rearrange("(a n) -> a n", a=1)).then_inc(ids_in, 16)
            sp.dma_start(ids_sb[0:1, B:2 * B], ids_lora.rearrange("(a n) -> a n", a=1)).then_inc(ids_in, 16)
            with nc.allow_non_contiguous_dma(reason="layer norm weights by column, once"):
                for n, col in enumerate((q_w, q_b, k_w, k_b)):
                    sp.dma_start(ln_cols[:, n, :], col.rearrange("(k p) -> p k", p=P)).then_inc(cols_in, 16)

            def load_block(q, m, s):
                if q == QUARTERS:
                    sp.dma_start(wc_raw[:, s, :], w_rows[Q][s * P:(s + 1) * P, :]).then_inc(wc_loaded[s], 16)
                else:
                    sp.dma_start(wc_raw[:, s, :], wc_rows[q, s % OB, (RAW_SLOTS * m + s) // OB, :, :]).then_inc(wc_loaded[s], 16)

            def load_next(q, slots):
                for s in slots:
                    sp.wait_ge(wc_turned[banks(s)[1]], turns(q, 1, s) + 1)
                    load_block(q + 1, 0, s)

            def load_x(t, u):
                sp.dma_start(x_in[:, u, :, :].rearrange("p k n -> p (k n)"),
                             x_rows[bass.ds(t, 1), :, :].rearrange("a p d -> p (a d)")).then_inc(x_loaded[u], 16)

            def load_xT(q, t, i, u):
                sp.wait_ge(xs_lo_ready[u], PAIRS * q + i)
                sp.wait_ge(xT_stored[u], 16 * PAIRS)
                sp.dma_start(x_tr[:, u, :, :].rearrange("p k n -> p (k n)"),
                             xT_d[bass.ds(t, 1), :, :, :].rearrange("a p k n -> p (a k n)")).then_inc(xT_loaded[u], 16)

            def quarter(q):
                def main(t, j, u):
                    last = isinstance(t, int) and t >= NT - 2
                    if q == 0:
                        if not last:
                            sp.wait_ge(x_turned, t + 1)
                            load_x(t + 2, u)
                        sp.wait_ge(x_copied_a, t + 1)
                        sp.wait_ge(x_copied_v, t + 1)
                        sp.dma_start(xT_d[bass.ds(t, 1), :, :, :].rearrange("a p k n -> p (a k n)"),
                                     x_tr[:, u, :, :].rearrange("p k n -> p (k n)")).then_inc(xT_stored[u], 16)
                    elif not last:
                        load_xT(q, t + 2, j + 1, u)
                    if last and q < QUARTERS - 1:
                        load_xT(q + 1, u, 0, u)
                    if last and q == QUARTERS - 1:
                        load_act(Q, u, 0, u)
                    if isinstance(t, int):
                        load_next(q, {0: (2, 3), NT - 3: (4, 5), NT - 2: (6,), NT - 1: (7,)}[t])

                def tail(t, j, u):
                    sp.wait_ge(cT_ready[u], PAIRS * q + j + 1)
                    sp.dma_start(cT_d[bass.ds(t, 1), :, OB * q:OB * q + OB, :].rearrange("a p k n -> p (a k n)"),
                                 cT_sb[:, u, :, :].rearrange("p k n -> p (k n)")).then_inc(cT_stored[u], 16)

                for s in range(RAW_SLOTS):
                    sp.wait_ge(wc_turned[banks(s)[1]], turns(q, 0, s) + 1)
                    load_block(q, 1, s)
                load_next(q, (0, 1))
                over_tiles(sp, main, tail)

            def load_w(p, b):
                sp.wait_ge(w_turned[1], blocks(p, b))
                if isinstance(b, int) and b == KC:
                    sp.dma_start(w_raw[0:MAXR, :], ffn_a).then_inc(w_loaded, 16)
                    sp.dma_start(w_raw[MAXR:AG, :], gate_w).then_inc(w_loaded, 16)
                elif p == O:
                    for g in range(4):
                        src = w_out.rearrange("n (c g d) -> n g c d", g=4, d=DH)[bass.ds(b * P, P), g, :, :]
                        sp.dma_start(w_raw[:, g * KC * DH:(g + 1) * KC * DH].rearrange("p (c d) -> p c d", d=DH), src).then_inc(w_loaded, 16)
                else:
                    sp.dma_start(w_raw[:, :], w_rows[p][bass.ds(b * P, P), :]).then_inc(w_loaded, 16)

            def load_act(p, t, i, u):
                sp.wait_ge(act_lo_ready[u], uses(p, i))
                if p == H and not (isinstance(t, int) and t < 2):
                    sp.wait_ge(u_done, t - 1)
                if p == F and isinstance(t, int) and t < 2:
                    sp.wait_ge(u_done, NT - 1 + t)
                if p == Q and isinstance(t, int) and t < 2:
                    sp.wait_ge(cT_stored[u], 16 * (PAIRS * (QUARTERS - 1) + 1))
                if p == O:
                    sp.wait_ge(tr_stored[u], 16 * (uses(V, i) + 1))
                if p == H:
                    sp.wait_ge(tr_stored[u], 16 * (uses(O, i) + 1))
                if p == F:
                    sp.wait_ge(tr_stored[u], 16 * (uses(H, i) + 1))
                sp.dma_start(act_raw[:, u, :, :].rearrange("p k n -> p (k n)"),
                             act_src[p][bass.ds(t, 1), :, :, :].rearrange("a p k n -> p (a k n)")).then_inc(act_loaded[u], 16)

            def load_lora(t):
                adapters = [sp.value_load(ids_sb[0:1, bass.ds(B + 2 * t + s, 1)], min_val=0, max_val=N_LORA - 1) for s in range(2)]
                if not (isinstance(t, int) and t == 0):
                    sp.wait_ge(lb_split, 4 * t)
                    sp.wait_ge(la_turned, t)
                for s, n in enumerate(adapters):
                    sp.dma_start(la_raw[s * RANK:(s + 1) * RANK, :],
                                 lora_a[bass.ds(n, 1), :, :].rearrange("a r i -> (a r) i")).then_inc(la_loaded[s], 16)
                    sp.dma_start(lb_raw[:, :, s * RANK:(s + 1) * RANK],
                                 lora_b_rows[bass.ds(n, 1), :, :, :].rearrange("a p o r -> p (a o) r")).then_inc(lb_loaded[s], 16)

            def load_qk(t, i, u):
                if not (isinstance(t, int) and t == 0):
                    sp.wait_ge(scores_done, 4 * t)
                sp.wait_ge(tr_stored[u], 16 * (uses(K, i) + 1))
                for n, (src, loaded) in enumerate(((tr_d[Q], q_loaded), (tr_d[K], k_loaded))):
                    sp.dma_start(aux[:, n, :], src[bass.ds(t, 1), :, :, :].rearrange("a p k n -> p (a k n)")).then_inc(loaded, 16)

            def before(p):
                if p == F:
                    sp.dma_start(gate[:, 0, :], gate_b.partition_broadcast(P)).then_inc(gate_b_in, 16)
                    sp.wait_ge(acc_free[1], NT * F)
                    sp.dma_start(bias_row[:, :], b_ffn.partition_broadcast(P)).then_inc(bias_f_in, 16)

            def main(p, t, i, u):
                last = isinstance(t, int) and t == NT - 1
                if p == H and not last:
                    load_lora(t + 1)
                if not (isinstance(t, int) and t >= NT - 2):
                    load_act(p, t + 2, i + 1, u)
                elif p != F:
                    load_act(p + 1, u, 0, u)
                if p == V and isinstance(t, int) and t == 0:
                    for w in range(2):
                        sp.wait_ge(tr_stored[w], 16 * uses(K, 0))
                    load_qk(0, 0, 0)
                if p == O:
                    if isinstance(t, int) and t == 0:
                        sp.wait_ge(scores_done, 4 * NT)
                    sp.wait_ge(acc_free[1], NT * O + t - 1)
                    sp.dma_start(aux[:, u, :], x_rows[bass.ds(t, 1), :, :].rearrange("a p d -> p (a d)")).then_inc(res_loaded[u], 16)
                    if isinstance(t, int) and t == NT - 3:
                        for w in range(2):
                            sp.wait_ge(turned[w], uses(V, PAIRS))
                        load_lora(0)
                        sp.dma_start(bias_row[:, :], b_base.partition_broadcast(P)).then_inc(bias_h_in, 16)
                if p == H and last:
                    sp.wait_ge(lb_turned, 2 * NT)
                    for w in range(2):
                        sp.dma_start(ffn_b_nat[:, :, w * MAXR:(w + 1) * MAXR], ffn_b_rows).then_inc(fb_loaded[w], 16)
                if p == F:
                    if not (isinstance(t, int) and t < 2):
                        sp.wait_ge(acc_free[2], t - 1)
                    sp.wait_ge(x1_stored[u], 16 * PAIRS)
                    sp.dma_start(aux[:, u, :], x1_d[bass.ds(t, 1), :, :].rearrange("a p d -> p (a d)")).then_inc(res_loaded[u], 16)

            def prep(p, b):
                if p != F:
                    load_w(p + 1, b)

            def tail(p, t, i, u):
                if p == F:
                    for c in range(3):
                        sp.wait_ge(acc_free[c], (NT * F if c < 2 else 0) + t + 1)
                    sp.dma_start(out_rows[bass.ds(t, 1), :, :].rearrange("a p d -> p (a d)"), nat[:, u, :]).then_inc(out_stored[u], 16)
                    return
                if p == O:
                    for c in range(2):
                        sp.wait_ge(acc_free[c], NT * O + t + 1)
                    sp.dma_start(x1_d[bass.ds(t, 1), :, :].rearrange("a p d -> p (a d)"), nat[:, u, :]).then_inc(x1_stored[u], 16)
                if p == V and not (isinstance(t, int) and t == NT - 1):
                    load_qk(t + 1, i + u, 1 - u)
                sp.wait_ge(tr_ready[u], uses(p, i) + 1)
                sp.dma_start(tr_d[p][bass.ds(t, 1), :, :, :].rearrange("a p k n -> p (a k n)"),
                               tr_sb[:, 1 if p == V else u, :, :].rearrange("p k n -> p (k n)")).then_inc(tr_stored[u], 16)

            for s in range(RAW_SLOTS):
                load_block(0, 0, s)
                if s < 2:
                    load_x(s, s)
            for q in range(QUARTERS):
                quarter(q)

            for u in range(2):
                sp.wait_ge(cT_stored[u], 16 * QUARTERS * PAIRS)
                sp.wait_ge(w_turned[u], KC)

            over_phases(sp, before, main, prep, tail, nothing)
            for u in range(2):
                sp.wait_ge(out_stored[u], 16 * PAIRS)
                sp.wait_ge(x1_stored[u], 16 * PAIRS)
                sp.wait_ge(tr_stored[u], 16 * PAIRS * 5)
                sp.wait_ge(xT_stored[u], 16 * PAIRS)

        @block.tensor
        def _(pe):
            pe.wait_ge(ident_ready, 2)

            pe.wait_ge(ids_in, 32)

            def turn_x(t, i, u):
                pe.wait_ge(x_loaded[u], 16 * i + 16)
                if not (isinstance(t, int) and t == 0):
                    pe.wait_ge(x_copied_a, t)
                    pe.wait_ge(x_copied_v, t)
                for k in range(KC):
                    last = nc.tensor.transpose(xps[2 + k // 4][:, k % 4 * P:(k % 4 + 1) * P], x_in[:, u, k, :], ident[:, :])
                last.then_inc(x_turned, 1)

            def quarter(q):
                def turn_blocks(m):
                    for s in range(RAW_SLOTS):
                        pe.wait_ge(wc_loaded[s], 16 * (2 * q + m + 1))
                        for h, b in enumerate(banks(s)):
                            if not (q == 0 and isinstance(m, int) and m == 0 and s < 2):
                                pe.wait_ge(wc_lo_ready[b], turns(q, m, s))
                            for k in range(4):
                                last = nc.tensor.transpose(xps[b][:, k * P:(k + 1) * P],
                                                           wc_raw[:, s, (4 * h + k) * P:(4 * h + k + 1) * P], ident[:, :])
                            last.then_inc(wc_turned[b], 1)

                def main(t, j, u):
                    experts = [pe.value_load(ids_sb[0:1, bass.ds(2 * t + s, 1)], min_val=0, max_val=E - 1) for s in range(2)]
                    if q == 0 and not (isinstance(t, int) and t == NT - 1):
                        turn_x(t + 1, j + u, 1 - u)
                    pe.wait_ge(xs_hi_ready[u], PAIRS * q + j + 1)
                    pe.wait_ge(xs_lo_ready[u], PAIRS * q + j + 1)
                    for s, e in enumerate(experts):
                        if not (q == 0 and isinstance(t, int) and t == 0):
                            pe.wait_ge(c_summed[s], NT * q + t)
                        for k in range(KC):
                            last = nc.tensor.matmul(
                                acc[s][:, :], x_st[:, u, k, s, :, :].rearrange("p a n -> p (a n)"),
                                wc[:, bass.ds(e, 1), k, :, :].rearrange("p e a n -> p (e a n)"),
                                start=(k == 0), stop=(k == KC - 1))
                        last.then_inc(cpair_done[u] if s else cfirst_done, 1)

                def tail(t, j, u):
                    pe.wait_ge(c_ready[u], PAIRS * q + j + 1)
                    pe.wait_ge(cT_ready[u], PAIRS * q + j)
                    for ob in range(OB):
                        last = nc.tensor.transpose(wps[u][:, ob * P:(ob + 1) * P], c_sum[:, u, 0, ob * P:(ob + 1) * P], ident[:, :])
                    last.then_inc(c_turned[u], 1)

                turn_blocks(0)
                turn_blocks(1)
                for b in range(4):
                    pe.wait_ge(wc_lo_ready[b], turns(q + 1, 0, 0))
                if q == 0:
                    turn_x(0, 0, 0)
                over_tiles(pe, main, tail)

            for q in range(QUARTERS):
                quarter(q)
            for w in range(2):
                pe.wait_ge(cT_ready[w], QUARTERS * PAIRS)

            def turn_w(p, b):
                rows = AG if isinstance(b, int) and b == KC else P
                extra = 16 if rows == AG else 0
                if p == Q:
                    pe.wait_ge(wc_loaded[b], 16 * (2 * QUARTERS + 1))
                else:
                    pe.wait_ge(w_loaded, 16 * loads(p, b) + extra)
                raw = wc_raw[:, b, :] if p == Q else w_raw[0:rows, :]
                for h in range(2):
                    if not (p == Q and b == 0):
                        pe.wait_ge(w_lo_ready[h], blocks(p, b))
                    for k in range(4):
                        last = nc.tensor.transpose(wps[h][:, k * P:k * P + rows],
                                                   raw[:, (4 * h + k) * P:(4 * h + k + 1) * P], ident[0:rows, 0:rows])
                    last.then_inc(w_turned[h], 1)

            def turn_b(t, r):
                if not (isinstance(t, int) and t == 0 and r == 0):
                    pe.wait_ge(lb_ready, 2 * t + r)
                for o in range(4):
                    last = nc.tensor.transpose(xps[3][:, o * P:(o + 1) * P],
                                               lb_parts[:, 4 * r + o, :, :].rearrange("p a r -> p (a r)"), ident[:, :])
                last.then_inc(lb_turned, 1)

            def turn_a(t):
                for s in range(2):
                    pe.wait_ge(la_loaded[s], 16 * t + 16)
                if not (isinstance(t, int) and t == 0):
                    pe.wait_ge(u_masked, t)
                    pe.wait_ge(la_ready, t)
                pe.wait_ge(lb_split, 4 * t + 4)
                turn_b(t, 0)
                for k in range(KC):
                    last = nc.tensor.transpose(xps[2][:, k * R2:(k + 1) * R2], la_raw[:, k * P:(k + 1) * P], ident[0:R2, 0:R2])
                last.then_inc(la_turned, 1)

            def before(p):
                for h in range(2):
                    pe.wait_ge(w_lo_ready[h], blocks(p + 1, 1 if p == F else 0))
                if p == H:
                    pe.wait_ge(tr_ready[1], uses(O, PAIRS - 1))
                    turn_a(0)
                    turn_b(0, 1)
                if p == F:
                    for w in range(2):
                        pe.wait_ge(fb_loaded[w], 16)
                    pe.wait_ge(lb_ready, 2 * NT)
                    pe.wait_ge(u_masked, NT)
                    for r in range(2):
                        for o in range(4):
                            last = nc.tensor.transpose(xps[2 + r][:, o * P:(o + 1) * P], ffn_b_nat[:, 4 * r + o, :], ident[:, :])
                    last.then_inc(fb_turned, 1)

            def score(t, i, u, step):
                half, chunks = step // 4, (2 * (step % 4), 2 * (step % 4) + 1)
                if step == 0:
                    pe.wait_ge(q_loaded, 16 * t + 16)
                    pe.wait_ge(k_loaded, 16 * t + 16)
                    if isinstance(t, int) and t == 0:
                        for w in range(2):
                            pe.wait_ge(tr_ready[w], uses(V, 0))
                    else:
                        pe.wait_ge(scores_biased, 4 * t)
                if step == 4 and not (isinstance(t, int) and t == 0):
                    pe.wait_ge(tr_ready[1 - u], uses(V, i + u))
                for c in chunks:
                    for g in (2 * half, 2 * half + 1):
                        rows = slice(DH * g, DH * g + DH)
                        for s in range(2):
                            last = nc.tensor.matmul(xps[g][s * S:(s + 1) * S, c * S:(c + 1) * S],
                                                    q_in[rows, c, s * S:(s + 1) * S], k_in[rows, c, s * S:(s + 1) * S],
                                                    start=True, stop=True)
                        if c == KC - 1:
                            last.then_inc(scores_done, 1)

            def products(p, u, c, dst, cols, close, between=nothing):
                r, done = p % 2, 0
                for k in range(KC):
                    for n, (a, w) in enumerate(((act_hi, w_hi[r]), (act_hi, w_lo[r]), (act_lo, w_hi[r]))):
                        last = nc.tensor.matmul(dst, a[:, u, k, :], w[:, k, cols], start=(k == 0 and n == 0),
                                                stop=(close and k == KC - 1 and n == 2))
                        done += 1
                        if done % 2 == 0 and done <= 16:
                            between(done // 2 - 1)
                return last

            def main(p, t, i, u):
                pe.wait_ge(act_hi_ready[u], uses(p, i) + 1)
                pe.wait_ge(act_lo_ready[u], uses(p, i) + 1)
                if p != F:
                    for c in range(2):
                        pe.wait_ge(acc_free[c], NT * p + t)
                        between = nothing
                        if c == 0 and p == V and not (isinstance(t, int) and t == 0):
                            between = partial(score, t - 1, i + u - 1, 1 - u)
                        if c == 0 and p == O and isinstance(t, int) and t == 0:
                            between = partial(score, NT - 1, PAIRS - 1, 1)
                        last = products(p, u, c, acc[c][:, :], slice(c * 512, (c + 1) * 512), True, between)
                        if p != H:
                            last.then_inc(acc_done[c][u], 1)
                        elif c == 0:
                            pe.wait_ge(la_ready, t + 1)
                            for k in range(KC):
                                last = nc.tensor.matmul(xps[2][0:R2, 256:256 + P], la_T[:, k, :], act_raw[:, u, k, :],
                                                        start=(k == 0), stop=(k == KC - 1))
                            last.then_inc(u_done, 1)
                    if p == H:
                        pe.wait_ge(u_ready, t + 1)
                        pe.wait_ge(lb_ready, 2 * t + 2)
                        for c in range(2):
                            nc.tensor.matmul(acc[c][:, :], u_st[:, :], lb_st[:, c * 512:(c + 1) * 512],
                                             start=False, stop=True, skip_group_check=True).then_inc(acc_done[c][u], 1)
                        if not (isinstance(t, int) and t in (0, NT - 1)):
                            turn_a(t + 1)
                    return
                for c in range(3):
                    pe.wait_ge(acc_free[c], (NT * F if c < 2 else 0) + t)
                    last = products(p, u, c, acc3[c][:, 0:FCH], slice(c * FCH, (c + 1) * FCH), True)
                    if c == 0:
                        last.then_inc(ag_done, 1)
                    if c == 1:
                        pe.wait_ge(a_ready, 2 * t + 2)
                        nc.tensor.transpose(wps[1][:, 0:P], a_parts[:, :, :].rearrange("p a r -> p (a r)"), ident[:, :]).then_inc(aT_done, 1)
                pe.wait_ge(aT_ready, t + 1)
                if isinstance(t, int) and t == 0:
                    pe.wait_ge(fb_lo, 2)
                for c in range(3):
                    first = AG if c == 0 else 0
                    for n, w in enumerate((w_hi[0], w_lo[0])):
                        last = nc.tensor.matmul(acc3[c][:, first:FCH], aT_st[:, :], w[:, 0, c * FCH + first - AG:(c + 1) * FCH - AG],
                                                start=False, stop=(n == 1), skip_group_check=True)
                    last.then_inc(acc_done[c][u], 1)

            def prep(p, b):
                if p != F:
                    turn_w(p + 1, b)

            def tail(p, t, i, u):
                if p == F:
                    return
                if p == V:
                    pe.wait_ge(v_spread, t + 1)
                    pe.wait_ge(tr_ready[1 - u], uses(V, i + u))

                    def turn_probs(g):
                        pe.wait_ge(probs_ready, 4 * t + g + 1)
                        pe.wait_ge(pT_ready[g % 2], 2 * t + g // 2)
                        for n in range(4):
                            h = 8 * g + 2 * n
                            last = nc.tensor.transpose(xps[g % 2][:, n * P:(n + 1) * P],
                                                       scores[:, h:h + 2, :].rearrange("p h k -> p (h k)"), ident[:, :])
                        last.then_inc(pT_done, 1)

                    def weigh_v(g):
                        pe.wait_ge(pT_ready[g % 2], 2 * t + g // 2 + 1)
                        for n in range(4):
                            hp = 4 * g + n
                            for s in range(2):
                                col = hp // 2 % 4 * P + s * S
                                last = nc.tensor.matmul(xps[2 + hp // 8][S * (hp % 2):S * (hp % 2) + S, col:col + S],
                                                        v_bd[:, s, hp, :], pT_sb[:, g % 2, n, s * S:(s + 1) * S], start=True, stop=True)
                        last.then_inc(pT_used[g % 2] if g < 3 else turned[u], 1)

                    turn_probs(0)
                    for g in range(4):
                        if g < 3:
                            turn_probs(g + 1)
                        weigh_v(g)
                    return
                a, b = (0, 1) if p == H else (2 * u, 2 * u + 1)
                if p in (Q, K):
                    pe.wait_ge(nat_ready[u], uses(p, i) + 1)
                else:
                    for c in range(2):
                        pe.wait_ge(acc_free[c], NT * p + t + 1)
                pe.wait_ge(tr_ready[u], uses(p, i))
                if p == H:
                    pe.wait_ge(tr_ready[1 - u], uses(p, i + u))
                if p == O and isinstance(t, int) and t == NT - 1:
                    pe.wait_ge(la_ready, 1)
                    pe.wait_ge(lb_ready, 2)
                    pe.wait_ge(u_masked, 1)
                for k in range(KC):
                    last = nc.tensor.transpose(xps[(a, b)[k // 4]][:, k % 4 * P:(k % 4 + 1) * P], nat[:, u, k * P:(k + 1) * P], ident[:, :])
                last.then_inc(turned[u], 1)

            def mid(p, t, i, u):
                if p == H and not (isinstance(t, int) and t == NT - 1):
                    if isinstance(t, int) and t == 0:
                        pe.wait_ge(tr_ready[1], uses(O, PAIRS))
                        turn_a(1)
                    turn_b(t + 1, 1)

            for b in range(KC):
                turn_w(Q, b)
            over_phases(pe, before, main, prep, tail, mid)

        @block.scalar
        def _(act):
            act.wait_ge(consts_ready, 1)

            def quarter(q):
                def copy_x(t, i, u):
                    act.wait_ge(x_turned, t + 1)
                    if not (isinstance(t, int) and t < 2):
                        act.wait_ge(xs_lo_ready[u], i)
                        act.wait_ge(xT_stored[u], 16 * i)
                    nc.scalar.activation(x_tr[:, u, 0:4, :].rearrange("p k n -> p (k n)"), xps[2][:, :], ACT.Copy).then_inc(x_copied_a, 1)

                def split_hi(q, t, i, u):
                    if q == 0:
                        copy_x(t, i, u)
                        act.wait_ge(x_copied_a, t + 1)
                        act.wait_ge(x_copied_v, t + 1)
                    else:
                        act.wait_ge(xT_loaded[u], 16 * (PAIRS * (q - 1) + i + 1))
                    if not (q == 0 and isinstance(t, int) and t < 2):
                        act.wait_ge(cpair_done[u], PAIRS * q + i)
                    nc.scalar.activation(x_st[:, u, :, :, 0, :], x_tr[:, u, :, :].rearrange("p k (s n) -> p k s n", s=2),
                                         ACT.Copy).then_inc(xs_hi_ready[u], 1)

                def main(t, j, u):
                    if not (isinstance(t, int) and t == NT - 1):
                        split_hi(q, t + 1, j + u, 1 - u)
                    elif q < QUARTERS - 1:
                        split_hi(q + 1, 0, 0, 0)
                    for s in range(2):
                        if s:
                            act.wait_ge(cpair_done[u], PAIRS * q + j + 1)
                        else:
                            act.wait_ge(cfirst_done, NT * q + t + 1)
                        if not (q == 0 and isinstance(t, int) and t == 0):
                            act.wait_ge(c_summed[s], NT * q + t)
                        nc.scalar.activation(c_low[:, s, :, :].rearrange("p a n -> p (a n)"), acc[s][S:P, :], ACT.Copy).then_inc(c_low_ready[s], 1)

                def tail(t, j, u):
                    act.wait_ge(c_turned[u], PAIRS * q + j + 1)
                    act.wait_ge(cT_stored[u], 16 * (PAIRS * q + j))
                    nc.scalar.activation(cT_sb[:, u, :, :].rearrange("p o n -> p (o n)"), wps[u][:, 0:QO], ACT.Copy).then_inc(cT_ready[u], 1)

                def copy_blocks(m):
                    for s in range(RAW_SLOTS):
                        for h, b in enumerate(banks(s)):
                            act.wait_ge(wc_turned[b], turns(q, m, s) + 1)
                            nc.scalar.activation(wc[:, 4 * m + s // OB, 4 * h:4 * h + 4, 0, s % OB * P:(s % OB + 1) * P],
                                                 xps[b][:, :].rearrange("p (k n) -> p k n", k=4), ACT.Copy).then_inc(wc_hi_ready[b], 1)

                if q > 0:
                    for w in range(2):
                        act.wait_ge(cpair_done[w], PAIRS * q)
                copy_blocks(0)
                copy_blocks(1)
                if q == 0:
                    split_hi(0, 0, 0, 0)
                over_tiles(act, main, tail)

            def split_w(p, b):
                r = p % 2
                last_block = isinstance(b, int) and b == KC
                n, off = (AG, 0) if last_block else (P, AG if p == F else 0)
                if p == Q and b == 0:
                    for w in range(2):
                        act.wait_ge(cpair_done[w], PAIRS * QUARTERS)
                if isinstance(b, int) and b == 0 and p >= 1:
                    for w in range(2):
                        act.wait_ge(acc_done[1][w], uses(p - 1, 0))
                for h in range(2):
                    act.wait_ge(w_turned[h], blocks(p, b) + 1)
                    cols = slice(0, AG) if last_block else bass.ds(off + b * P, P)
                    nc.scalar.activation(w_hi[r][:, 4 * h:4 * h + 4, cols],
                                         wps[h][:, :].rearrange("p (k n) -> p k n", k=4)[:, :, 0:n], ACT.Copy).then_inc(w_hi_ready[h], 1)

            def split_act(p, t, i, u):
                act.wait_ge(act_loaded[u], 16 * (uses(p, i) + 1))
                if p == F and not (isinstance(i, int) and i == 0):
                    act.wait_ge(acc_done[2][u], i)
                else:
                    act.wait_ge(acc_done[1][u], uses(p, i))
                nc.scalar.activation(act_hi[:, u, :, :], act_raw[:, u, :, :], ACT.Copy).then_inc(act_hi_ready[u], 1)

            def before(p):
                if p == H:
                    copy_a(0, 0, 0)
                    copy_b(0, 1, 0, 0)
                if p == F:
                    act.wait_ge(fb_turned, 1)
                    for r in range(2):
                        nc.scalar.activation(w_hi[0][:, 0, r * 512:(r + 1) * 512], xps[2 + r][:, :], ACT.Copy).then_inc(fb_hi, 1)

            def copy_b(t, r, i, u):
                act.wait_ge(lb_turned, 2 * t + r + 1)
                if not (isinstance(t, int) and t == 0):
                    act.wait_ge(acc_done[1][1 - u], uses(H, i + u))
                nc.scalar.activation(lb_st[:, r * 512:(r + 1) * 512], xps[3][:, :], ACT.Copy).then_inc(lb_ready, 1)

            def copy_a(t, i, u):
                act.wait_ge(la_turned, t + 1)
                if not (isinstance(t, int) and t == 0):
                    act.wait_ge(u_done, t)
                nc.scalar.activation(la_T[:, :, :].rearrange("p k r -> p (k r)"), xps[2][:, 0:KC * R2], ACT.Copy).then_inc(la_ready, 1)
                copy_b(t, 0, i, u)

            def exponentials(t):
                for g in range(4):
                    act.wait_ge(shifted, 4 * t + g + 1)
                    part = scores[:, 8 * g:8 * g + 8, :]
                    nc.scalar.activation(part, part, ACT.Exp).then_inc(exp_ready, 1)

            def main(p, t, i, u):
                if not (isinstance(t, int) and t == NT - 1):
                    split_act(p, t + 1, i + u, 1 - u)
                elif p != F:
                    split_act(p + 1, 0, 0, 0)
                if p == V and not (isinstance(t, int) and t == 0):
                    exponentials(t - 1)
                if p == O and isinstance(t, int) and t == 0:
                    exponentials(NT - 1)
                if p in (Q, K):
                    act.wait_ge(var_ready, NT * p + t + 1)
                    nc.scalar.activation(std_rstd[:, 0:1], mean_var[:, 1:2], ACT.Sqrt, bias=eps_col[:, 0:1]).then_inc(std_ready, 1)
                if p == H and not (isinstance(t, int) and t in (0, NT - 1)):
                    copy_a(t + 1, i + u, 1 - u)
                if p == F:
                    act.wait_ge(gate_step, 7 * t + 3)
                    nc.scalar.activation(gate[:, 4, :], gate[:, 3, :], ACT.Exp).then_inc(gate_exp, 1)
                    act.wait_ge(aT_done, t + 1)
                    act.wait_ge(acc_free[2], t)
                    nc.scalar.activation(aT_st[:, :], wps[1][:, 0:P], ACT.Copy).then_inc(aT_ready, 1)

            def prep(p, b):
                if p != F:
                    split_w(p + 1, b)

            def tail(p, t, i, u):
                if p == F:
                    return
                if p == V:
                    for g in range(4):
                        act.wait_ge(pT_done, 4 * t + g + 1)
                        if g >= 2:
                            act.wait_ge(pT_used[g % 2], (2 * t if g % 2 == 0 else t) + 1)
                        elif g == 0:
                            act.wait_ge(pT_used[0], 2 * t)
                        elif not (isinstance(t, int) and t == 0):
                            act.wait_ge(turned[1 - u], uses(V, i + u))
                        nc.scalar.activation(pT_sb[:, g % 2, :, :].rearrange("p a n -> p (a n)"), xps[g % 2][:, :], ACT.Copy).then_inc(pT_ready[g % 2], 1)
                act.wait_ge(turned[u], uses(p, i) + 1)
                if p == V:
                    act.wait_ge(tr_stored[1 - u], 16 * uses(p, i + u))
                else:
                    act.wait_ge(tr_stored[u], 16 * uses(p, i))
                if p in (Q, K):
                    for k in range(KC):
                        last = nc.scalar.activation(tr_sb[:, u, k, :], xps[2 * u + k // 4][:, k % 4 * P:(k % 4 + 1) * P], ACT.Identity,
                                                    scale=ln_cols[:, 2 * p, k:k + 1], bias=ln_cols[:, 2 * p + 1, k:k + 1])
                else:
                    a = {V: 2, O: 2 * u, H: 0}[p]
                    for h in range(2):
                        last = nc.scalar.activation(tr_sb[:, 1 if p == V else u, 4 * h:4 * h + 4, :].rearrange("p k n -> p (k n)"), xps[a + h][:, :], ACT.Copy)
                last.then_inc(tr_ready[u], 1)

            def mid(p, t, i, u):
                if p == H and not (isinstance(t, int) and t == NT - 1):
                    if isinstance(t, int) and t == 0:
                        copy_a(1, 0, 1)
                    copy_b(t + 1, 1, i + u, 1 - u)
                if p != V:
                    return
                if isinstance(t, int) and t == 0:
                    act.wait_ge(alibi_step, HEADS + 5)
                else:
                    act.wait_ge(turned[1 - u], uses(V, i + u))
                for c in range(2):
                    act.wait_ge(acc_free[c], NT * V + t + 1)
                heads = v_nat[:, :].rearrange("p (a two g d) -> p g a two d", two=2, g=4, d=DH)
                for s in range(2):
                    pairs = v_bd[:, s, :, :].rearrange("p (g m) d -> p g m d", g=4)
                    for two in range(2):
                        last = nc.scalar.activation(pairs[two * S:(two + 1) * S, :, :, two * DH:(two + 1) * DH],
                                                    heads[s * S:(s + 1) * S, :, :, two, :], ACT.Copy)
                last.then_inc(v_spread, 1)

            act.wait_ge(cols_scaled, 1)
            for q in range(QUARTERS):
                quarter(q)
            for w in range(2):
                act.wait_ge(xs_lo_ready[w], QUARTERS * PAIRS)
            split_act(Q, 0, 0, 0)
            for b in range(KC):
                split_w(Q, b)
            over_phases(act, before, main, prep, tail, mid)

        @block.vector
        def _(dve):
            dve.wait_ge(cols_in, 64)
            nc.vector.tensor_scalar(ln_cols[:, 0:2, :], ln_cols[:, 0:2, :], SCALE, None, ALU.mult).then_inc(cols_scaled, 1)

            def quarter(q):
                def copy_x(t, i, u):
                    dve.wait_ge(x_turned, t + 1)
                    if not (isinstance(t, int) and t < 2):
                        dve.wait_ge(xs_hi_ready[u], i)
                        dve.wait_ge(xs_lo_ready[u], i)
                        dve.wait_ge(xT_stored[u], 16 * i)
                    nc.vector.tensor_copy(x_tr[:, u, 4:8, :].rearrange("p k n -> p (k n)"), xps[3][:, :]).then_inc(x_copied_v, 1)

                def split_lo(q, t, i, u):
                    if q == 0:
                        copy_x(t, i, u)
                        dve.wait_ge(x_copied_v, t + 1)
                    dve.wait_ge(xs_hi_ready[u], PAIRS * q + i + 1)
                    nc.vector.tensor_tensor(x_st[:, u, :, :, 1, :], x_tr[:, u, :, :].rearrange("p k (s n) -> p k s n", s=2),
                                            x_st[:, u, :, :, 0, :].bitcast(F32), ALU.subtract).then_inc(xs_lo_ready[u], 1)

                def main(t, j, u):
                    if not (isinstance(t, int) and t == NT - 1):
                        split_lo(q, t + 1, j + u, 1 - u)
                    elif q < QUARTERS - 1:
                        split_lo(q + 1, 0, 0, 0)
                    for s in range(2):
                        dve.wait_ge(c_low_ready[s], NT * q + t + 1)
                        dve.wait_ge(c_turned[u], PAIRS * q + j)
                        nc.vector.tensor_tensor(c_sum[s * S:(s + 1) * S, u, :, :].rearrange("p a n -> p (a n)"), acc[s][0:S, :],
                                                c_low[:, s, :, :].rearrange("p a n -> p (a n)"), ALU.add).then_inc(c_summed[s], 1)

                def copy_blocks(m):
                    for s in range(RAW_SLOTS):
                        for h, b in enumerate(banks(s)):
                            dve.wait_ge(wc_hi_ready[b], turns(q, m, s) + 1)
                            hi, lo = (wc[:, 4 * m + s // OB, 4 * h:4 * h + 4, a, s % OB * P:(s % OB + 1) * P] for a in range(2))
                            nc.vector.tensor_tensor(lo, xps[b][:, :].rearrange("p (k n) -> p k n", k=4),
                                                    hi.bitcast(F32), ALU.subtract).then_inc(wc_lo_ready[b], 1)

                copy_blocks(0)
                copy_blocks(1)
                if q == 0:
                    split_lo(0, 0, 0, 0)
                over_tiles(dve, main, nothing)

            for q in range(QUARTERS):
                quarter(q)

            def split_w(p, b):
                r = p % 2
                last_block = isinstance(b, int) and b == KC
                n, off = (AG, 0) if last_block else (P, AG if p == F else 0)
                for h in range(2):
                    dve.wait_ge(w_hi_ready[h], blocks(p, b) + 1)
                    cols = slice(0, AG) if last_block else bass.ds(off + b * P, P)
                    nc.vector.tensor_tensor(w_lo[r][:, 4 * h:4 * h + 4, cols],
                                            wps[h][:, :].rearrange("p (k n) -> p k n", k=4)[:, :, 0:n],
                                            w_hi[r][:, 4 * h:4 * h + 4, cols].bitcast(F32), ALU.subtract).then_inc(w_lo_ready[h], 1)

            def split_b(t):
                for s in range(2):
                    dve.wait_ge(lb_loaded[s], 16 * t + 16)
                if not (isinstance(t, int) and t == 0):
                    dve.wait_ge(lb_turned, 2 * t)
                hi, lo = lb_parts[:, :, 0, :], lb_parts[:, :, 1, :]
                nc.vector.tensor_copy(hi.bitcast(F32R), lb_raw[:, :, :]).then_inc(lb_split, 1)
                nc.vector.tensor_copy(lb_parts[:, :, 2, :].bitcast(F32R), lb_raw[:, :, :]).then_inc(lb_split, 1)
                dve.wait_ge(lb_split, 4 * t + 1)
                nc.vector.tensor_tensor(lo.bitcast(F32R), lb_raw[:, :, :], hi, ALU.subtract).then_inc(lb_split, 1)
                nc.vector.tensor_tensor(lb_parts[:, :, 3, :].bitcast(F32R), lb_raw[:, :, :], hi, ALU.subtract).then_inc(lb_split, 1)

            def before(p):
                if p == H:
                    dve.wait_ge(bias_h_in, 16)
                    dve.wait_ge(mask_ready, 3)
                if p == F:
                    dve.wait_ge(fb_hi, 2)
                    for r in range(2):
                        nc.vector.tensor_tensor(w_lo[0][:, 0, r * 512:(r + 1) * 512], xps[2 + r][:, :],
                                                w_hi[0][:, 0, r * 512:(r + 1) * 512].bitcast(F32), ALU.subtract).then_inc(fb_lo, 1)
                    dve.wait_ge(gate_b_in, 16)

            def clip_v(t, i, u, c):
                if not (isinstance(t, int) and t == 0):
                    dve.wait_ge(v_spread, t)
                else:
                    dve.wait_ge(tr_stored[0], 16 * uses(V, 0))
                dve.wait_ge(acc_done[c][u], uses(V, i) + 1)
                nc.vector.tensor_scalar(v_nat[:, c * 512:(c + 1) * 512], acc[c][:, :], CLIP, -CLIP, ALU.min, ALU.max).then_inc(acc_free[c], 1)

            def bias_max(t, g):
                n, part = 4 * t + g, scores[:, 8 * g:8 * g + 8, :]
                dve.wait_ge(scores_done, n + 1)
                nc.vector.tensor_tensor(part, xps[g][:, :].rearrange("p (h k) -> p h k", k=S), alibi[:, 8 * g:8 * g + 8, :], ALU.add).then_inc(scores_biased, 1)
                dve.wait_ge(scores_biased, n + 1)
                nc.vector.tensor_reduce(smax[:, 8 * g:8 * g + 8], part, AX_X, ALU.max).then_inc(max_ready, 1)

            def normalize(t, g):
                n, part = 4 * t + g, scores[:, 8 * g:8 * g + 8, :]
                dve.wait_ge(exp_ready, n + 1)
                nc.vector.tensor_reduce(ssum[:, 8 * g:8 * g + 8], part, AX_X, ALU.add).then_inc(sum_ready, 1)
                dve.wait_ge(sum_ready, n + 1)
                nc.vector.reciprocal(smax[:, 8 * g:8 * g + 8], ssum[:, 8 * g:8 * g + 8]).then_inc(rsum_ready, 1)
                dve.wait_ge(rsum_ready, n + 1)
                nc.vector.tensor_tensor(part, part, smax[:, 8 * g:8 * g + 8].unsqueeze(2).to_broadcast([P, 8, S]), ALU.mult).then_inc(probs_ready, 1)

            def softmax(t, clip):
                if isinstance(t, int) and t == 0:
                    dve.wait_ge(alibi_step, HEADS + 5)
                    for w in range(2):
                        dve.wait_ge(turned[w], uses(V, 0))
                bias_max(t, 0)
                bias_max(t, 1)
                normalize(t, 0)
                bias_max(t, 2)
                normalize(t, 1)
                bias_max(t, 3)
                clip(0)
                normalize(t, 2)
                normalize(t, 3)
                clip(1)

            def main(p, t, i, u):
                if p in (Q, K):
                    n = NT * p + t
                    dve.wait_ge(turned[u], uses(p, i))
                    for c in range(2):
                        dve.wait_ge(acc_done[c][u], uses(p, i) + 1)
                        nc.vector.tensor_scalar(nat[:, u, c * 512:(c + 1) * 512], acc[c][:, :], CLIP, -CLIP, ALU.min, ALU.max).then_inc(acc_free[c], 1)
                    for c in range(2):
                        dve.wait_ge(acc_free[c], n + 1)
                        nc.vector.bn_stats(bn_st[:, c, :], nat[:, u, c * 512:(c + 1) * 512]).then_inc(stats_step, 1)
                    dve.wait_ge(stats_step, 3 * n + 2)
                    nc.vector.tensor_copy(wait_pad[:, :], bn_st[:, 1, 0:1])
                    nc.vector.bn_aggr(mean_var[:, :], bn_st[:, :, :].rearrange("p a b -> p (a b)")).then_inc(var_ready, 1)
                    dve.wait_ge(std_ready, n + 1)
                    nc.vector.reciprocal(std_rstd[:, 1:2], std_rstd[:, 0:1]).then_inc(stats_step, 1)
                    dve.wait_ge(stats_step, 3 * n + 3)
                    dve.wait_ge(var_ready, n + 1)
                    nc.vector.tensor_scalar(nat[:, u, :], nat[:, u, :], mean_var[:, 0:1], std_rstd[:, 1:2],
                                            ALU.subtract, ALU.mult).then_inc(nat_ready[u], 1)
                if p == V:
                    if isinstance(t, int) and t == 0:
                        clip_v(t, i, u, 0)
                        clip_v(t, i, u, 1)
                    else:
                        softmax(t - 1, partial(clip_v, t, i, u))
                if p == O and isinstance(t, int) and t == 0:
                    softmax(NT - 1, nothing)
                if p == O:
                    dve.wait_ge(turned[u], uses(p, i))
                    if isinstance(t, int) and t == 0:
                        dve.wait_ge(turned[1], uses(O, 0))
                    dve.wait_ge(x1_stored[u], 16 * i)
                    dve.wait_ge(res_loaded[u], 16 * i + 16)
                    for c in range(2):
                        dve.wait_ge(acc_done[c][u], uses(p, i) + 1)
                        part = (slice(None), u, slice(c * 512, (c + 1) * 512))
                        nc.vector.tensor_tensor(nat[part], acc[c][:, :], aux[part], ALU.add).then_inc(acc_free[c], 1)
                    if isinstance(t, int) and t == NT - 2:
                        split_b(0)
                if p == H:
                    dve.wait_ge(u_done, t + 1)
                    nc.vector.tensor_tensor(u_seq[:, :], xps[2][0:R2, 256:256 + P], seq_mask[:, :], ALU.mult).then_inc(u_masked, 1)
                    dve.wait_ge(u_masked, t + 1)
                    if not (isinstance(t, int) and t == 0):
                        dve.wait_ge(acc_done[1][1 - u], uses(H, i + u))
                    nc.vector.tensor_copy(u_st[0:R2, :], u_seq[:, :]).then_inc(u_step, 1)
                    nc.vector.tensor_copy(u_st[R2:2 * R2, :], u_seq[:, :]).then_inc(u_step, 1)
                    dve.wait_ge(u_step, 3 * t + 2)
                    nc.vector.tensor_tensor(u_st[2 * R2:3 * R2, :], u_seq[:, :], u_st[0:R2, :].bitcast(F32), ALU.subtract).then_inc(u_step, 1)
                    nc.vector.tensor_tensor(u_st[3 * R2:4 * R2, :], u_seq[:, :], u_st[0:R2, :].bitcast(F32), ALU.subtract).then_inc(u_ready, 1)
                    if not (isinstance(t, int) and t == NT - 1):
                        split_b(t + 1)
                    dve.wait_ge(turned[u], uses(p, i))
                    dve.wait_ge(x1_stored[u], 16 * PAIRS)
                    for c in range(2):
                        dve.wait_ge(acc_done[c][u], uses(p, i) + 1)
                        nc.vector.tensor_tensor(nat[:, u, c * 512:(c + 1) * 512], acc[c][:, :], bias_row[:, c * 512:(c + 1) * 512], ALU.add).then_inc(acc_free[c], 1)
                if p == F:
                    gates(t)
                    dve.wait_ge(turned[u], uses(F, 0))
                    dve.wait_ge(out_stored[u], 16 * i)
                    dve.wait_ge(xb_ready, t + 1)
                    for c in range(3):
                        dve.wait_ge(acc_done[c][u], (uses(p, i) if c < 2 else i) + 1)
                        first = AG if c == 0 else 0
                        part = (slice(None), u, slice(c * FCH + first - AG, (c + 1) * FCH - AG))
                        nc.vector.tensor_tensor(nat[part], acc3[c][:, first:FCH], aux[part], ALU.add).then_inc(acc_free[c], 1)

            def gates(t):
                n = 7 * t
                dve.wait_ge(ag_done, t + 1)
                nc.vector.tensor_tensor(gate[:, 1, :], acc[0][:, MAXR:AG], gate[:, 0, :], ALU.add).then_inc(gate_step, 1)
                dve.wait_ge(gate_step, n + 1)
                nc.vector.tensor_reduce(gate[:, 2, 0:1], gate[:, 1, :], AX_X, ALU.max).then_inc(gate_step, 1)
                dve.wait_ge(gate_step, n + 2)
                nc.vector.tensor_scalar(gate[:, 3, :], gate[:, 1, :], gate[:, 2, 0:1], None, ALU.subtract).then_inc(gate_step, 1)
                dve.wait_ge(gate_exp, t + 1)
                nc.vector.tensor_scalar(gate[:, 5, :], gate[:, 4, :], 1.0, None, ALU.is_lt).then_inc(gate_step, 1)
                dve.wait_ge(gate_step, n + 4)
                nc.vector.tensor_tensor(gate[:, 6, 0:1], gate[:, 5, 0:1], gate[:, 5, 1:2], ALU.mult).then_inc(gate_step, 1)
                dve.wait_ge(gate_step, n + 5)
                nc.vector.tensor_tensor(gate[:, 7, 0:1], gate[:, 6, 0:1], gate[:, 5, 2:3], ALU.mult).then_inc(gate_step, 1)
                dve.wait_ge(gate_step, n + 6)
                nc.vector.tensor_copy(a_msk[:, 0:8], acc[0][:, 0:8])
                nc.vector.tensor_scalar(a_msk[:, 8:16], acc[0][:, 8:16], gate[:, 5, 0:1], None, ALU.mult)
                nc.vector.tensor_scalar(a_msk[:, 16:32], acc[0][:, 16:32], gate[:, 6, 0:1], None, ALU.mult)
                nc.vector.tensor_scalar(a_msk[:, 32:64], acc[0][:, 32:64], gate[:, 7, 0:1], None, ALU.mult).then_inc(gate_step, 1)
                dve.wait_ge(gate_step, n + 7)
                dve.wait_ge(aT_done, t)
                nc.vector.tensor_copy(a_parts[:, 0, :].bitcast(F32R), a_msk[:, :]).then_inc(a_ready, 1)
                dve.wait_ge(a_ready, 2 * t + 1)
                nc.vector.tensor_tensor(a_parts[:, 1, :].bitcast(F32R), a_msk[:, :], a_parts[:, 0, :], ALU.subtract).then_inc(a_ready, 1)

            def prep(p, b):
                if p != F:
                    split_w(p + 1, b)

            for b in range(KC):
                split_w(Q, b)
            over_phases(dve, before, main, prep, nothing, nothing)

        @block.gpsimd
        def _(pool):
            nc.gpsimd.memset(ident[:, :], 0.0).then_inc(ident_ready, 1)
            nc.gpsimd.memset(eps_col[:, :], LN_EPS).then_inc(consts_ready, 1)
            pool.wait_ge(ident_ready, 1)
            nc.gpsimd.affine_select(out=ident[:, :], in_=ident[:, :], compare_op=ALU.not_equal, fill=1.0, base=0,
                                    pattern=[[-1, P]], channel_multiplier=1).then_inc(ident_ready, 1)
            nc.gpsimd.memset(seq_mask[:, :], 1.0).then_inc(mask_ready, 1)
            pool.wait_ge(mask_ready, 1)
            nc.gpsimd.affine_select(out=seq_mask[:, :].rearrange("r (s n) -> r s n", s=2), in_=seq_mask[:, :].rearrange("r (s n) -> r s n", s=2),
                                    compare_op=ALU.is_ge, fill=0.0, base=0, pattern=[[-RANK, 2], [0, S]], channel_multiplier=1).then_inc(mask_ready, 1)
            pool.wait_ge(mask_ready, 2)
            nc.gpsimd.affine_select(out=seq_mask[:, :].rearrange("r (s n) -> r s n", s=2), in_=seq_mask[:, :].rearrange("r (s n) -> r s n", s=2),
                                    compare_op=ALU.is_ge, fill=0.0, base=RANK - 1, pattern=[[RANK, 2], [0, S]], channel_multiplier=-1).then_inc(mask_ready, 1)

            for q in range(QUARTERS):
                def main(t, j, u):
                    for s in range(2):
                        pool.wait_ge(c_summed[s], NT * q + t + 1)
                    nc.gpsimd.tensor_tensor(c_sum[:, u, 0, :], c_sum[:, u, 0, :], c_sum[:, u, 1, :], ALU.add).then_inc(c_ready[u], 1)

                over_tiles(pool, main, nothing)


            def split_act(p, i, u):
                pool.wait_ge(act_hi_ready[u], uses(p, i) + 1)
                nc.gpsimd.tensor_tensor(act_lo[:, u, :, :], act_raw[:, u, :, :], act_hi[:, u, :, :].bitcast(F32), ALU.subtract).then_inc(act_lo_ready[u], 1)

            def build_alibi(part):
                if part == 0:
                    nc.gpsimd.memset(v_bd[:, :, :, :], 0.0).then_inc(alibi_step, 1)
                    for s in range(2):
                        pool.wait_ge(alibi_step, s + 1)
                        nc.gpsimd.iota(rel[s * S:(s + 1) * S, :], pattern=[[1, S]], base=0, channel_multiplier=-1,
                                       allow_small_or_imprecise_dtypes=True).then_inc(alibi_step, 1)
                    pool.wait_ge(alibi_step, 3)
                elif part < 3:
                    pool.wait_ge(alibi_step, 3)
                    for n in range((part - 1) * HEADS // 2, part * HEADS // 2):
                        nc.gpsimd.tensor_scalar(alibi[:, n, :], rel[:, :], SLOPES[4 * (n % 8) + n // 8], None, ALU.mult).then_inc(alibi_step, 1)
                else:
                    s = part - 3
                    pool.wait_ge(alibi_step, HEADS + 3 + s)
                    rows = alibi[s * S:(s + 1) * S, :, :]
                    nc.gpsimd.affine_select(out=rows, in_=rows, compare_op=ALU.is_ge, fill=MASKED, base=0,
                                            pattern=[[0, HEADS], [-1, S]], channel_multiplier=1).then_inc(alibi_step, 1)
                    pool.wait_ge(alibi_step, HEADS + 4 + s)

            def shift(t):
                for g in range(4):
                    part = scores[:, 8 * g:8 * g + 8, :]
                    pool.wait_ge(max_ready, 4 * t + g + 1)
                    nc.gpsimd.tensor_tensor(part, part, smax[:, 8 * g:8 * g + 8].unsqueeze(2).to_broadcast([P, 8, S]), ALU.subtract).then_inc(shifted, 1)

            def main(p, t, i, u):
                if not (isinstance(t, int) and t == NT - 1):
                    split_act(p, i + u, 1 - u)
                elif p != F:
                    split_act(p + 1, 0, 0)
                if p == V and not (isinstance(t, int) and t == 0):
                    shift(t - 1)
                if p == O and isinstance(t, int) and t == 0:
                    shift(NT - 1)
                if p == Q and isinstance(t, int) and t == NT - 1:
                    build_alibi(0)
                if p == K and isinstance(t, int):
                    if t >= NT - 2:
                        pool.wait_ge(act_lo_ready[1 - u], uses(K, PAIRS - 1) + 1 if t == NT - 2 else uses(V, 0) + 1)
                    build_alibi({0: 1, NT - 3: 2, NT - 2: 3, NT - 1: 4}[t])
                if p == F:
                    if isinstance(t, int) and t == 0:
                        pool.wait_ge(bias_f_in, 16)
                    pool.wait_ge(res_loaded[u], 16 * (PAIRS + i + 1))
                    nc.gpsimd.tensor_tensor(aux[:, u, :], aux[:, u, :], bias_row[:, :], ALU.add).then_inc(xb_ready, 1)

            for w in range(2):
                pool.wait_ge(cpair_done[w], QUARTERS * PAIRS)
            split_act(Q, 0, 0)
            over_phases(pool, nothing, main, nothing, nothing, nothing)


_INS = ["x", "itok_B_3_7", "itok_B_6_15", "L0_cond_weight", "L0_attn_w_qkv", "L0_attn_q_ln_w", "L0_attn_q_ln_b",
        "L0_attn_k_ln_w", "L0_attn_k_ln_b", "L0_attn_w_out", "L0_cond2_base_weight", "L0_cond2_base_bias",
        "L0_cond2_lora_A_w", "L0_cond2_lora_B_w", "L0_ffn_W", "L0_ffn_b", "L0_ffn_A", "L0_ffn_B",
        "L0_ffn_gate_w", "L0_ffn_gate_b"]


def kernel(**inputs):
    import numpy as _np
    import concourse.bacc as _bacc
    from concourse import mybir as _mybir
    from concourse.bass_utils import run_bass_kernel_spmd as _run

    nc = _bacc.Bacc("TRN2", target_bir_lowering=False, num_devices=1)
    arrays, args = {}, []
    for name in _INS:
        a = _np.ascontiguousarray(inputs[name])
        arrays[f"in_{name}"] = a
        args.append(nc.dram_tensor(f"in_{name}", a.shape, _mybir.dt.from_np(a.dtype), kind="ExternalInput").ap())
    args.append(nc.dram_tensor("out_0", inputs["x"].shape, _mybir.dt.float32, kind="ExternalOutput").ap())
    adaln_attention_ffn(nc, *args)
    r = _run(nc, [arrays], core_ids=[0])
    return r.results[0]["out_0"]
```

```python
from contextlib import ExitStack
from functools import partial

import numpy as np

import concourse.bass as bass
from concourse import mybir

ALU = mybir.AluOpType
ACT = mybir.ActivationFunctionType
AX_X = mybir.AxisListType.X
F32 = mybir.dt.float32
F32R = mybir.dt.float32r
I32 = mybir.dt.int32

P = 128
MASKED = -3.0e38
CLIP = 8.0
LN_EPS = 1e-5
QUARTERS = 4
RAW_SLOTS = 8

Q, K, V, O, H, F = range(6)


def adaln_attention_ffn(nc, x, ids_expert, ids_lora, w_cond, w_qkv, q_w, q_b, k_w, k_b, w_out,
                        w_base, b_base, lora_a, lora_b, w_ffn, b_ffn, ffn_a, ffn_b, gate_w, gate_b, out):
    B, S, D = x.shape
    E = w_cond.shape[0]
    KC = D // P
    NT = B * S // P
    PAIRS = NT // 2
    HEADS = 32
    DH = D // HEADS
    QO = D // QUARTERS
    OB = QO // P
    RANK = lora_a.shape[1]
    N_LORA = lora_a.shape[0]
    MAXR = ffn_a.shape[0]
    NG = gate_w.shape[0]
    AG = MAXR + NG
    R2 = 2 * RANK
    FCH = (D + AG) // 3
    assert S * 2 == P and FCH * 3 == D + AG and 4 * R2 == P and 2 * MAXR == P and NG == 4
    assert RAW_SLOTS == KC and E * OB == 2 * RAW_SLOTS and OB == 2 and E == 8
    assert D % 512 == 0 and NT % 2 == 0 and HEADS * S == 2048
    SCALE = float(DH) ** -0.5
    SLOPES = [float(np.float32(1.0) / np.float32(2.0) ** np.float32((h + 1) * 8.0 / HEADS)) for h in range(HEADS)]

    x_rows = x.rearrange("b s d -> (b s) d").rearrange("(t p) d -> t p d", p=P)
    out_rows = out.rearrange("b s d -> (b s) d").rearrange("(t p) d -> t p d", p=P)
    wc_rows = w_cond.rearrange("e (q ob p) i -> q ob e p i", q=QUARTERS, p=P)
    w_rows = {Q: w_qkv[0:D, :], K: w_qkv[D:2 * D, :], V: w_qkv[2 * D:3 * D, :], O: w_out, H: w_base, F: w_ffn}
    lora_b_rows = lora_b.rearrange("n (o p) r -> n p o r", p=P)
    ffn_b_rows = ffn_b.rearrange("(o p) r -> p o r", p=P)

    def dram(name, chunked):
        return nc.dram_tensor(name, (NT, P, KC, P) if chunked else (NT, P, D), F32).ap()

    xT_d = dram("xT_d", True)
    cT_d = dram("cT_d", True)
    tr_d = {Q: dram("qT_d", True), K: dram("kT_d", True), V: dram("attT_d", True),
            O: dram("x1T_d", True), H: dram("hT_d", True)}
    x1_d = dram("x1_d", False)
    act_src = {Q: cT_d, K: cT_d, V: cT_d, O: tr_d[V], H: tr_d[O], F: tr_d[H]}

    with ExitStack() as ctx:
        def sb(name, shape, dt=F32, scope=ctx):
            return scope.enter_context(nc.sbuf_tensor(name, shape, dt))

        def sem(name):
            return ctx.enter_context(nc.semaphore(name))

        def sem2(name):
            return [sem(f"{name}{u}") for u in range(2)]

        ident = sb("ident", [P, P])
        ids_sb = sb("ids_sb", [1, 2 * B], I32)
        ln_cols = sb("ln_cols", [P, 4, KC])
        eps_col = sb("eps_col", [P, 1])
        bn_st = sb("bn_st", [P, 2, 6])
        mean_var = sb("mean_var", [P, 2])
        std_rstd = sb("std_rstd", [P, 2])
        wait_pad = sb("wait_pad", [P, 1])
        seq_mask = sb("seq_mask", [R2, P])
        w_raw = sb("w_raw", [P, D])

        cond = ExitStack()
        wc = sb("wc", [P, E, KC, 2, QO], F32R, cond)
        c_sum = sb("c_sum", [P, 2, 2, QO], F32, cond)
        over_w = sb("over_w", [P, 2 * KC * (D + D + AG) - 2 * E * KC * QO - 4 * QO], F32, cond)
        x_in = sb("x_in", [P, 2, KC, P], F32, cond)
        x_tr = sb("x_tr", [P, 2, KC, P], F32, cond)
        x_st = sb("x_st", [P, 2, KC, 2, 2, S], F32R, cond)
        wc_raw = sb("wc_raw", [P, RAW_SLOTS, D], F32, cond)
        c_low = sb("c_low", [S, 2, 2, QO], F32, cond)
        cT_sb = sb("cT_sb", [P, 2, OB, P], F32, cond)
        cond.close()

        w_hi = [sb("w0_hi", [P, KC, D], F32R), sb("w1_hi", [P, KC, AG + D], F32R)]
        w_lo = [sb("w0_lo", [P, KC, D], F32R), sb("w1_lo", [P, KC, AG + D], F32R)]
        act_raw = sb("act_raw", [P, 2, KC, P])
        act_hi = sb("act_hi", [P, 2, KC, P], F32R)
        act_lo = sb("act_lo", [P, 2, KC, P], F32R)
        nat = sb("nat", [P, 2, D])
        aux = sb("aux", [P, 2, D])
        tr_sb = sb("tr_sb", [P, 2, KC, P])
        attn = ExitStack()
        v_bd = sb("v_bd", [P, 2, HEADS // 2, 2 * DH], F32, attn)
        alibi = sb("alibi", [P, HEADS, S], F32, attn)
        pT_sb = sb("pT_sb", [P, 2, 4, P], F32, attn)
        rel = sb("rel", [P, S], F32, attn)
        smax = sb("smax", [P, HEADS], F32, attn)
        ssum = sb("ssum", [P, HEADS], F32, attn)
        attn.close()
        bias_row = sb("bias_row", [P, D])
        la_T = sb("la_T", [P, KC, R2])
        la_raw = sb("la_raw", [R2, D])
        lb_raw = sb("lb_raw", [P, KC, R2])
        lb_parts = sb("lb_parts", [P, KC, 4, R2])
        lb_st = sb("lb_st", [P, D], F32R)
        u_seq = sb("u_seq", [R2, P])
        u_st = sb("u_st", [P, P], F32R)
        a_msk = sb("a_msk", [P, MAXR])
        a_parts = sb("a_parts", [P, 2, MAXR])
        aT_st = sb("aT_st", [P, P], F32R)
        gate = sb("gate", [P, 10, NG])
        q_in, k_in = (aux[:, n, :].rearrange("p (k n) -> p k n", k=KC) for n in range(2))
        v_nat = tr_sb[:, 0, :, :].rearrange("p k n -> p (k n)")
        scores = nat[:, :, :].rearrange("p a n -> p (a n)").rearrange("p (h k) -> p h k", k=S)
        ffn_b_nat = lb_parts[:, :, :, :].rearrange("p k a r -> p k (a r)")

        def bank(name):
            return ctx.enter_context(nc.psum_tensor(name, [P, 512], F32))

        acc = [bank("acc0"), bank("acc1")]
        wps = [bank("wps0"), bank("wps1")]
        xps = [bank(f"xps{n}") for n in range(4)]
        acc3 = [acc[0], acc[1], wps[0]]

        ids_in, ident_ready, cols_in, cols_scaled, consts_ready = (
            sem(n) for n in ("ids_in", "ident_ready", "cols_in", "cols_scaled", "consts_ready"))
        x_loaded, xT_stored = sem2("x_loaded"), sem2("xT_stored")
        x_turned, x_copied_a, x_copied_v = (sem(n) for n in ("x_turned", "x_copied_a", "x_copied_v"))
        wc_loaded = [sem(f"wc_loaded{s}") for s in range(RAW_SLOTS)]
        wc_turned, wc_hi_ready, wc_lo_ready = (
            [sem(f"{n}{b}") for b in range(4)] for n in ("wc_turned", "wc_hi_ready", "wc_lo_ready"))
        xT_loaded, xs_hi_ready, xs_lo_ready, c_low_ready, c_summed, c_ready, cpair_done, c_turned, cT_ready, cT_stored = (
            sem2(n) for n in ("xT_loaded", "xs_hi_ready", "xs_lo_ready", "c_low_ready", "c_summed", "c_ready",
                              "cpair_done", "c_turned", "cT_ready", "cT_stored"))
        cfirst_done, w_loaded = sem("cfirst_done"), sem("w_loaded")
        w_turned, w_hi_ready, w_lo_ready = (sem2(n) for n in ("w_turned", "w_hi_ready", "w_lo_ready"))
        act_loaded, act_hi_ready, act_lo_ready = (sem2(n) for n in ("act_loaded", "act_hi_ready", "act_lo_ready"))
        acc_done = [sem2(f"acc_done{c}_") for c in range(3)]
        acc_free = [sem(f"acc_free{c}") for c in range(3)]
        stats_step, var_ready, std_ready = (sem(n) for n in ("stats_step", "var_ready", "std_ready"))
        nat_ready, turned, tr_ready, tr_stored = (sem2(n) for n in ("nat_ready", "turned", "tr_ready", "tr_stored"))
        q_loaded, k_loaded, scores_done, scores_biased, max_ready, shifted, exp_ready, sum_ready, rsum_ready, probs_ready, pT_done = (
            sem(n) for n in ("q_loaded", "k_loaded", "scores_done", "scores_biased", "max_ready", "shifted",
                             "exp_ready", "sum_ready", "rsum_ready", "probs_ready", "pT_done"))
        pT_ready, pT_used = sem2("pT_ready"), sem2("pT_used")
        alibi_step, v_spread = sem("alibi_step"), sem("v_spread")
        res_loaded, x1_stored, out_stored = (sem2(n) for n in ("res_loaded", "x1_stored", "out_stored"))
        bias_h_in, bias_f_in, gate_b_in, mask_ready = (
            sem(n) for n in ("bias_h_in", "bias_f_in", "gate_b_in", "mask_ready"))
        la_loaded, lb_loaded, fb_loaded = sem2("la_loaded"), sem2("lb_loaded"), sem2("fb_loaded")
        la_turned, la_ready, lb_split, lb_turned, lb_ready = (
            sem(n) for n in ("la_turned", "la_ready", "lb_split", "lb_turned", "lb_ready"))
        u_done, u_masked, u_step, u_ready = (sem(n) for n in ("u_done", "u_masked", "u_step", "u_ready"))
        fb_turned, fb_hi, fb_lo = (sem(n) for n in ("fb_turned", "fb_hi", "fb_lo"))
        ag_done, gate_step, gate_exp, a_ready, aT_done, aT_ready, xb_ready = (
            sem(n) for n in ("ag_done", "gate_step", "gate_exp", "a_ready", "aT_done", "aT_ready", "xb_ready"))

        from_one_pe = [*turned, *c_turned, *pT_used]
        from_one_act = [*cT_ready, *tr_ready, *pT_ready]
        from_one_dve = [*acc_free, scores_biased]
        from_one_sp = [*cT_stored, *tr_stored, *x1_stored, *out_stored]

        def start(eng, counters):
            for counter in counters:
                eng.sem_inc(counter, 1)

        def over_tiles(eng, main, tail):
            def pair(j):
                main(2 * j + 1, j, 1)
                tail(2 * j, j, 0)
                main(2 * j + 2, j + 1, 0)
                tail(2 * j + 1, j, 1)

            main(0, 0, 0)
            with eng.Fori(0, PAIRS - 2) as j:
                pair(j)
            pair(PAIRS - 2)
            main(NT - 1, PAIRS - 1, 1)
            tail(NT - 2, PAIRS - 1, 0)

        def over_quarters(blocks, tiles, last_tail):
            for q in range(QUARTERS):
                blocks(q, 0)
                if q > 0:
                    last_tail(q - 1)
                blocks(q, 1)
                tiles(q)
            last_tail(QUARTERS - 1)

        def banks(s):
            return 2 * (s % 2), 2 * (s % 2) + 1

        def turns(q, m, s):
            return RAW_SLOTS * q + RAW_SLOTS // 2 * m + s // 2

        def over_phases(eng, before, main, prep, tail, mid):
            for p in (Q, K, V, O, H, F):
                def pair(j):
                    main(p, 2 * j + 1, j, 1)
                    prep(p, j + 1)
                    tail(p, 2 * j, j, 0)
                    mid(p, 2 * j + 1, j, 1)
                    main(p, 2 * j + 2, j + 1, 0)
                    tail(p, 2 * j + 1, j, 1)
                    mid(p, 2 * j + 2, j + 1, 0)

                before(p)
                main(p, 0, 0, 0)
                prep(p, 0)
                if p != Q:
                    tail(p - 1, NT - 1, PAIRS - 1, 1)
                mid(p, 0, 0, 0)
                with eng.Fori(0, PAIRS - 2) as j:
                    pair(j)
                pair(PAIRS - 2)
                main(p, NT - 1, PAIRS - 1, 1)
                if p == H:
                    prep(p, KC)
                tail(p, NT - 2, PAIRS - 1, 0)
                mid(p, NT - 1, PAIRS - 1, 1)
            tail(F, NT - 1, PAIRS - 1, 1)

        def uses(p, i):
            return PAIRS * p + i

        def blocks(p, b):
            return KC * p + b

        def w_banks(p, b):
            return xps[2:4] if p == Q and b % 2 else wps

        def nothing(*_):
            pass

        def loads(p, b):
            if p < O:
                return KC * (p - 1) + b + 1
            return KC * (p - 1) + 4 * (b + 1) if p == O else KC * (p + 2) + b + 1

        block = ctx.enter_context(nc.Block())

        @block.sync
        def _(sp):
            start(sp, from_one_sp)
            sp.dma_start(ids_sb[0:1, 0:B], ids_expert.rearrange("(a n) -> a n", a=1)).then_inc(ids_in, 16)
            sp.dma_start(ids_sb[0:1, B:2 * B], ids_lora.rearrange("(a n) -> a n", a=1)).then_inc(ids_in, 16)
            with nc.allow_non_contiguous_dma(reason="layer norm weights by column"):
                for n, col in enumerate((q_w, q_b, k_w, k_b)):
                    sp.dma_start(ln_cols[:, n, :], col.rearrange("(k p) -> p k", p=P)).then_inc(cols_in, 16)

            def load_block(q, m, s):
                if q == QUARTERS:
                    sp.dma_start(wc_raw[:, s, :], w_rows[Q][s * P:(s + 1) * P, :]).then_inc(wc_loaded[s], 16)
                else:
                    sp.dma_start(wc_raw[:, s, :], wc_rows[q, s % OB, (RAW_SLOTS * m + s) // OB, :, :]).then_inc(wc_loaded[s], 16)

            def load_next(q, slots):
                for s in slots:
                    sp.wait_ge(wc_turned[banks(s)[1]], turns(q, 1, s) + 1)
                    load_block(q + 1, 0, s)

            def load_x(t, u):
                sp.dma_start(x_in[:, u, :, :].rearrange("p k n -> p (k n)"),
                             x_rows[bass.ds(t, 1), :, :].rearrange("a p d -> p (a d)")).then_inc(x_loaded[u], 16)

            def load_xT(q, t, i, u):
                sp.wait_ge(xs_lo_ready[u], PAIRS * q + i)
                sp.wait_ge(xT_stored[u], 16 * PAIRS)
                sp.dma_start(x_tr[:, u, :, :].rearrange("p k n -> p (k n)"),
                             xT_d[bass.ds(t, 1), :, :, :].rearrange("a p k n -> p (a k n)")).then_inc(xT_loaded[u], 16)

            def store_c(q, t, j, u):
                sp.wait_ge(cT_ready[u], PAIRS * q + j + 2)
                sp.dma_start(cT_d[bass.ds(t, 1), :, OB * q:OB * q + OB, :].rearrange("a p k n -> p (a k n)"),
                             cT_sb[:, u, :, :].rearrange("p k n -> p (k n)")).then_inc(cT_stored[u], 16)

            def tiles(q):
                def main(t, j, u):
                    last = isinstance(t, int) and t >= NT - 2
                    if q == 0:
                        if not last:
                            sp.wait_ge(x_turned, t + 1)
                            load_x(t + 2, u)
                        sp.wait_ge(x_copied_a, t + 1)
                        sp.wait_ge(x_copied_v, t + 1)
                        sp.dma_start(xT_d[bass.ds(t, 1), :, :, :].rearrange("a p k n -> p (a k n)"),
                                     x_tr[:, u, :, :].rearrange("p k n -> p (k n)")).then_inc(xT_stored[u], 16)
                    elif not last:
                        load_xT(q, t + 2, j + 1, u)
                    if last and q < QUARTERS - 1:
                        load_xT(q + 1, u, 0, u)
                    if last and q == QUARTERS - 1:
                        load_act(Q, u, 0, u)
                    if isinstance(t, int):
                        load_next(q, {0: (2, 3), NT - 3: (4, 5), NT - 2: (6,), NT - 1: (7,)}[t])

                load_next(q, (0, 1))
                if q == QUARTERS - 1:
                    load_w(K, 0)
                over_tiles(sp, main, partial(store_c, q))

            def reload(q, m):
                if m == 0:
                    for s in range(RAW_SLOTS):
                        sp.wait_ge(wc_turned[banks(s)[1]], turns(q, 0, s) + 1)
                        load_block(q, 1, s)

            def load_w(p, b):
                if not (p == K and isinstance(b, int) and b == 0):
                    sp.wait_ge(w_turned[1], blocks(p, b))
                if isinstance(b, int) and b == KC:
                    sp.dma_start(w_raw[0:MAXR, :], ffn_a).then_inc(w_loaded, 16)
                    sp.dma_start(w_raw[MAXR:AG, :], gate_w).then_inc(w_loaded, 16)
                elif p == O:
                    for g in range(4):
                        src = w_out.rearrange("n (c g d) -> n g c d", g=4, d=DH)[bass.ds(b * P, P), g, :, :]
                        sp.dma_start(w_raw[:, g * KC * DH:(g + 1) * KC * DH].rearrange("p (c d) -> p c d", d=DH), src).then_inc(w_loaded, 16)
                else:
                    sp.dma_start(w_raw[:, :], w_rows[p][bass.ds(b * P, P), :]).then_inc(w_loaded, 16)

            def load_act(p, t, i, u):
                sp.wait_ge(act_lo_ready[u], uses(p, i))
                if p == H and not (isinstance(t, int) and t < 2):
                    sp.wait_ge(u_done, t - 1)
                if p == F and isinstance(t, int) and t < 2:
                    sp.wait_ge(u_done, NT - 1 + t)
                if p == Q and isinstance(t, int) and t < 2:
                    sp.wait_ge(cT_stored[u], 16 * (PAIRS * (QUARTERS - 1) + 1) + 1)
                if p == O:
                    sp.wait_ge(tr_stored[u], 16 * (uses(V, i) + 1) + 1)
                if p == H:
                    sp.wait_ge(tr_stored[u], 16 * (uses(O, i) + 1) + 1)
                if p == F:
                    sp.wait_ge(tr_stored[u], 16 * (uses(H, i) + 1) + 1)
                sp.dma_start(act_raw[:, u, :, :].rearrange("p k n -> p (k n)"),
                             act_src[p][bass.ds(t, 1), :, :, :].rearrange("a p k n -> p (a k n)")).then_inc(act_loaded[u], 16)

            def load_lora(t):
                adapters = [sp.value_load(ids_sb[0:1, bass.ds(B + 2 * t + s, 1)], min_val=0, max_val=N_LORA - 1) for s in range(2)]
                if not (isinstance(t, int) and t == 0):
                    sp.wait_ge(lb_split, 4 * t)
                    sp.wait_ge(la_turned, t)
                for s, n in enumerate(adapters):
                    sp.dma_start(la_raw[s * RANK:(s + 1) * RANK, :],
                                 lora_a[bass.ds(n, 1), :, :].rearrange("a r i -> (a r) i")).then_inc(la_loaded[s], 16)
                    sp.dma_start(lb_raw[:, :, s * RANK:(s + 1) * RANK],
                                 lora_b_rows[bass.ds(n, 1), :, :, :].rearrange("a p o r -> p (a o) r")).then_inc(lb_loaded[s], 16)

            def load_qk(t, i, u):
                if not (isinstance(t, int) and t == 0):
                    sp.wait_ge(scores_done, 4 * t)
                sp.wait_ge(tr_stored[u], 16 * (uses(K, i) + 1) + 1)
                for n, (src, loaded) in enumerate(((tr_d[Q], q_loaded), (tr_d[K], k_loaded))):
                    sp.dma_start(aux[:, n, :], src[bass.ds(t, 1), :, :, :].rearrange("a p k n -> p (a k n)")).then_inc(loaded, 16)

            def before(p):
                if p == F:
                    sp.dma_start(gate[:, 0, :], gate_b.partition_broadcast(P)).then_inc(gate_b_in, 16)
                    sp.wait_ge(acc_free[1], NT * F + 1)
                    sp.dma_start(bias_row[:, :], b_ffn.partition_broadcast(P)).then_inc(bias_f_in, 16)

            def main(p, t, i, u):
                last = isinstance(t, int) and t == NT - 1
                if p == H and not last:
                    load_lora(t + 1)
                if not (isinstance(t, int) and t >= NT - 2):
                    load_act(p, t + 2, i + 1, u)
                elif p != F:
                    load_act(p + 1, u, 0, u)
                if p == V:
                    if isinstance(t, int) and t == 0:
                        for w in range(2):
                            sp.wait_ge(tr_stored[w], 16 * uses(K, 0) + 1)
                    load_qk(t, i, u)
                if p == O:
                    if isinstance(t, int) and t == 0:
                        sp.wait_ge(scores_done, 4 * NT)
                    sp.wait_ge(acc_free[1], NT * O + t)
                    sp.dma_start(aux[:, u, :], x_rows[bass.ds(t, 1), :, :].rearrange("a p d -> p (a d)")).then_inc(res_loaded[u], 16)
                    if isinstance(t, int) and t == NT - 3:
                        for w in range(2):
                            sp.wait_ge(turned[w], uses(V, PAIRS) + 1)
                        load_lora(0)
                        sp.dma_start(bias_row[:, :], b_base.partition_broadcast(P)).then_inc(bias_h_in, 16)
                if p == H and last:
                    sp.wait_ge(lb_turned, 2 * NT)
                    for w in range(2):
                        sp.dma_start(ffn_b_nat[:, :, w * MAXR:(w + 1) * MAXR], ffn_b_rows).then_inc(fb_loaded[w], 16)
                if p == F:
                    if not (isinstance(t, int) and t < 2):
                        sp.wait_ge(acc_free[2], t)
                    sp.wait_ge(x1_stored[u], 16 * PAIRS + 1)
                    sp.dma_start(aux[:, u, :], x1_d[bass.ds(t, 1), :, :].rearrange("a p d -> p (a d)")).then_inc(res_loaded[u], 16)

            def prep(p, b):
                if not (isinstance(b, int) and b >= KC - 1):
                    if p != F:
                        load_w(p + 1, b + 1)
                elif p == H and b == KC - 1:
                    load_w(F, KC)
                elif p < H:
                    load_w(p + 2, 0)

            def tail(p, t, i, u):
                if p == F:
                    sp.wait_ge(acc_free[2], t + 2)
                    sp.dma_start(out_rows[bass.ds(t, 1), :, :].rearrange("a p d -> p (a d)"), nat[:, u, :]).then_inc(out_stored[u], 16)
                    return
                if p == O:
                    for c in range(2):
                        sp.wait_ge(acc_free[c], NT * O + t + 2)
                    sp.dma_start(x1_d[bass.ds(t, 1), :, :].rearrange("a p d -> p (a d)"), nat[:, u, :]).then_inc(x1_stored[u], 16)
                sp.wait_ge(tr_ready[u], uses(p, i) + 2)
                sp.dma_start(tr_d[p][bass.ds(t, 1), :, :, :].rearrange("a p k n -> p (a k n)"),
                               tr_sb[:, 1 if p == V else u, :, :].rearrange("p k n -> p (k n)")).then_inc(tr_stored[u], 16)

            for s in range(RAW_SLOTS):
                load_block(0, 0, s)
            for u in range(2):
                load_x(u, u)
            over_quarters(reload, tiles, lambda q: store_c(q, NT - 1, PAIRS - 1, 1))

            for u in range(2):
                sp.wait_ge(cT_stored[u], 16 * QUARTERS * PAIRS + 1)
                sp.wait_ge(w_turned[u], KC)

            over_phases(sp, before, main, prep, tail, nothing)
            for u in range(2):
                sp.wait_ge(out_stored[u], 16 * PAIRS + 1)
                sp.wait_ge(x1_stored[u], 16 * PAIRS + 1)
                sp.wait_ge(tr_stored[u], 16 * PAIRS * 5 + 1)
                sp.wait_ge(xT_stored[u], 16 * PAIRS)

        @block.tensor
        def _(pe):
            start(pe, from_one_pe)
            pe.wait_ge(ident_ready, 2)

            pe.wait_ge(ids_in, 32)

            def turn_x(t, i, u):
                pe.wait_ge(x_loaded[u], 16 * i + 16)
                if not (isinstance(t, int) and t == 0):
                    pe.wait_ge(x_copied_a, t)
                    pe.wait_ge(x_copied_v, t)
                for k in range(KC):
                    last = nc.tensor.transpose(xps[2 + k // 4][:, k % 4 * P:(k % 4 + 1) * P], x_in[:, u, k, :], ident[:, :])
                last.then_inc(x_turned, 1)

            def turn_blocks(q, m):
                for s in range(RAW_SLOTS):
                    pe.wait_ge(wc_loaded[s], 16 * (2 * q + m + 1))
                    for h, b in enumerate(banks(s)):
                        if not (q == 0 and isinstance(m, int) and m == 0 and s < 2):
                            pe.wait_ge(wc_lo_ready[b], turns(q, m, s))
                        for k in range(4):
                            last = nc.tensor.transpose(xps[b][:, k * P:(k + 1) * P],
                                                       wc_raw[:, s, (4 * h + k) * P:(4 * h + k + 1) * P], ident[:, :])
                        last.then_inc(wc_turned[b], 1)

            def turn_c(q, t, j, u):
                pe.wait_ge(c_ready[u], PAIRS * q + j + 1)
                pe.wait_ge(cT_ready[u], PAIRS * q + j + 1)
                for ob in range(OB):
                    last = nc.tensor.transpose(wps[u][:, ob * P:(ob + 1) * P], c_sum[:, u, 0, ob * P:(ob + 1) * P], ident[:, :])
                last.then_inc(c_turned[u], 1)

            def tiles(q):
                def main(t, j, u):
                    if q == 0 and not (isinstance(t, int) and t == NT - 1):
                        turn_x(t + 1, j + u, 1 - u)
                    for s in range(2):
                        e = pe.value_load(ids_sb[0:1, bass.ds(2 * t + s, 1)], min_val=0, max_val=E - 1)
                        if s == 0:
                            pe.wait_ge(xs_hi_ready[u], PAIRS * q + j + 1)
                            pe.wait_ge(xs_lo_ready[u], PAIRS * q + j + 1)
                        if not (q == 0 and isinstance(t, int) and t == 0):
                            pe.wait_ge(c_summed[s], NT * q + t)
                        for k in range(KC):
                            last = nc.tensor.matmul(
                                acc[s][:, :], x_st[:, u, k, s, :, :].rearrange("p a n -> p (a n)"),
                                wc[:, bass.ds(e, 1), k, :, :].rearrange("p e a n -> p (e a n)"),
                                start=(k == 0), stop=(k == KC - 1))
                        last.then_inc(cpair_done[u] if s else cfirst_done, 1)

                for b in range(4):
                    pe.wait_ge(wc_lo_ready[b], turns(q + 1, 0, 0))
                if q == 0:
                    turn_x(0, 0, 0)
                over_tiles(pe, main, partial(turn_c, q))

            over_quarters(turn_blocks, tiles, lambda q: turn_c(q, NT - 1, PAIRS - 1, 1))
            for w in range(2):
                pe.wait_ge(cT_ready[w], QUARTERS * PAIRS + 1)

            def turn_w(p, b):
                rows = AG if isinstance(b, int) and b == KC else P
                extra = 16 if rows == AG else 0
                if p == Q:
                    pe.wait_ge(wc_loaded[b], 16 * (2 * QUARTERS + 1))
                else:
                    pe.wait_ge(w_loaded, 16 * loads(p, b) + extra)
                raw = wc_raw[:, b, :] if p == Q else w_raw[0:rows, :]
                for h in range(2):
                    if p != Q:
                        pe.wait_ge(w_lo_ready[h], blocks(p, b))
                    elif b >= 2:
                        pe.wait_ge(w_lo_ready[h], b - 1)
                    for k in range(4):
                        last = nc.tensor.transpose(w_banks(p, b)[h][:, k * P:k * P + rows],
                                                   raw[:, (4 * h + k) * P:(4 * h + k + 1) * P], ident[0:rows, 0:rows])
                    last.then_inc(w_turned[h], 1)

            def turn_b(t, r):
                if not (isinstance(t, int) and t == 0 and r == 0):
                    pe.wait_ge(lb_ready, 2 * t + r)
                for o in range(4):
                    last = nc.tensor.transpose(xps[3][:, o * P:(o + 1) * P],
                                               lb_parts[:, 4 * r + o, :, :].rearrange("p a r -> p (a r)"), ident[:, :])
                last.then_inc(lb_turned, 1)

            def turn_a(t):
                for s in range(2):
                    pe.wait_ge(la_loaded[s], 16 * t + 16)
                if not (isinstance(t, int) and t == 0):
                    pe.wait_ge(u_masked, t)
                    pe.wait_ge(la_ready, t)
                pe.wait_ge(lb_split, 4 * t + 4)
                turn_b(t, 0)
                for k in range(KC):
                    last = nc.tensor.transpose(xps[2][:, k * R2:(k + 1) * R2], la_raw[:, k * P:(k + 1) * P], ident[0:R2, 0:R2])
                last.then_inc(la_turned, 1)

            def before(p):
                for h in range(2):
                    pe.wait_ge(w_lo_ready[h], blocks(p + 1, 1 if p == F else 0))
                if p == H:
                    pe.wait_ge(tr_ready[1], uses(O, PAIRS - 1) + 1)
                    turn_a(0)
                    turn_b(0, 1)
                if p == F:
                    for w in range(2):
                        pe.wait_ge(fb_loaded[w], 16)
                    pe.wait_ge(lb_ready, 2 * NT)
                    pe.wait_ge(u_masked, NT)
                    for r in range(2):
                        for o in range(4):
                            last = nc.tensor.transpose(xps[2 + r][:, o * P:(o + 1) * P], ffn_b_nat[:, 4 * r + o, :], ident[:, :])
                    last.then_inc(fb_turned, 1)

            def score(t, i, u, step):
                if step >= 8:
                    return
                half, chunks = step // 4, (2 * (step % 4), 2 * (step % 4) + 1)
                if step == 0:
                    pe.wait_ge(q_loaded, 16 * t + 16)
                    pe.wait_ge(k_loaded, 16 * t + 16)
                    if isinstance(t, int) and t == 0:
                        for w in range(2):
                            pe.wait_ge(tr_ready[w], uses(V, 0) + 1)
                    else:
                        pe.wait_ge(scores_biased, 4 * t + 1)
                if step == 4 and not (isinstance(t, int) and t == 0):
                    pe.wait_ge(tr_ready[1 - u], uses(V, i + u) + 1)
                for c in chunks:
                    for g in (2 * half, 2 * half + 1):
                        rows = slice(DH * g, DH * g + DH)
                        for s in range(2):
                            last = nc.tensor.matmul(xps[g][s * S:(s + 1) * S, c * S:(c + 1) * S],
                                                    q_in[rows, c, s * S:(s + 1) * S], k_in[rows, c, s * S:(s + 1) * S],
                                                    start=True, stop=True)
                        if c == KC - 1:
                            last.then_inc(scores_done, 1)

            def turn_probs(t, g):
                pe.wait_ge(probs_ready, 4 * t + g + 1)
                pe.wait_ge(pT_ready[g % 2], 2 * t + g // 2 + 1)
                for n in range(4):
                    h = 8 * g + 2 * n
                    last = nc.tensor.transpose(xps[g % 2][:, n * P:(n + 1) * P],
                                               scores[:, h:h + 2, :].rearrange("p h k -> p (h k)"), ident[:, :])
                last.then_inc(pT_done, 1)

            def turn_early(t, i, u, step):
                if step in (9, 10):
                    turn_probs(t, step - 9)

            def products(p, u, c, dst, cols, close, between=nothing):
                r, done = p % 2, 0
                for k in range(KC):
                    for n, (a, w) in enumerate(((act_hi, w_hi[r]), (act_hi, w_lo[r]), (act_lo, w_hi[r]))):
                        last = nc.tensor.matmul(dst, a[:, u, k, :], w[:, k, cols], start=(k == 0 and n == 0),
                                                stop=(close and k == KC - 1 and n == 2))
                        done += 1
                        if done % 2 == 0:
                            between(done // 2 - 1)
                return last

            def main(p, t, i, u):
                pe.wait_ge(act_hi_ready[u], uses(p, i) + 1)
                pe.wait_ge(act_lo_ready[u], uses(p, i) + 1)
                if p != F:
                    for c in range(2):
                        pe.wait_ge(acc_free[c], NT * p + t + 1)
                        between = nothing
                        if p == V and not (isinstance(t, int) and t == 0):
                            between = partial((score, turn_early)[c], t - 1, i + u - 1, 1 - u)
                        if p == O and isinstance(t, int) and t == 0:
                            between = partial((score, turn_early)[c], NT - 1, PAIRS - 1, 1)
                        last = products(p, u, c, acc[c][:, :], slice(c * 512, (c + 1) * 512), True, between)
                        if p != H:
                            last.then_inc(acc_done[c][u], 1)
                        elif c == 0:
                            pe.wait_ge(la_ready, t + 1)
                            for k in range(KC):
                                last = nc.tensor.matmul(xps[2][0:R2, 256:256 + P], la_T[:, k, :], act_raw[:, u, k, :],
                                                        start=(k == 0), stop=(k == KC - 1))
                            last.then_inc(u_done, 1)
                    if p == H:
                        pe.wait_ge(u_ready, t + 1)
                        pe.wait_ge(lb_ready, 2 * t + 2)
                        for c in range(2):
                            nc.tensor.matmul(acc[c][:, :], u_st[:, :], lb_st[:, c * 512:(c + 1) * 512],
                                             start=False, stop=True, skip_group_check=True).then_inc(acc_done[c][u], 1)
                        if not (isinstance(t, int) and t in (0, NT - 1)):
                            turn_a(t + 1)
                    return
                for c in range(3):
                    pe.wait_ge(acc_free[c], (NT * F if c < 2 else 0) + t + 1)
                    last = products(p, u, c, acc3[c][:, 0:FCH], slice(c * FCH, (c + 1) * FCH), True)
                    if c == 0:
                        last.then_inc(ag_done, 1)
                    if c == 1:
                        pe.wait_ge(a_ready, 2 * t + 2)
                        nc.tensor.transpose(wps[1][:, 0:P], a_parts[:, :, :].rearrange("p a r -> p (a r)"), ident[:, :]).then_inc(aT_done, 1)
                pe.wait_ge(aT_ready, t + 1)
                if isinstance(t, int) and t == 0:
                    pe.wait_ge(fb_lo, 2)
                for c in range(3):
                    first = AG if c == 0 else 0
                    for n, w in enumerate((w_hi[0], w_lo[0])):
                        last = nc.tensor.matmul(acc3[c][:, first:FCH], aT_st[:, :], w[:, 0, c * FCH + first - AG:(c + 1) * FCH - AG],
                                                start=False, stop=(n == 1), skip_group_check=True)
                    last.then_inc(acc_done[c][u], 1)

            def prep(p, b):
                if p != F:
                    turn_w(p + 1, b)

            def tail(p, t, i, u):
                if p == F:
                    return
                if p == V:
                    pe.wait_ge(v_spread, t + 1)
                    pe.wait_ge(tr_ready[1 - u], uses(V, i + u) + 1)

                    def weigh_v(g):
                        pe.wait_ge(pT_ready[g % 2], 2 * t + g // 2 + 2)
                        for n in range(4):
                            hp = 4 * g + n
                            for s in range(2):
                                col = hp // 2 % 4 * P + s * S
                                last = nc.tensor.matmul(xps[2 + hp // 8][S * (hp % 2):S * (hp % 2) + S, col:col + S],
                                                        v_bd[:, s, hp, :], pT_sb[:, g % 2, n, s * S:(s + 1) * S], start=True, stop=True)
                        last.then_inc(pT_used[g % 2] if g < 3 else turned[u], 1)

                    for g in range(4):
                        if g > 0 and g < 3:
                            turn_probs(t, g + 1)
                        weigh_v(g)
                    return
                a, b = (0, 1) if p == H else (2 * u, 2 * u + 1)
                if p in (Q, K):
                    pe.wait_ge(nat_ready[u], uses(p, i) + 1)
                else:
                    for c in range(2):
                        pe.wait_ge(acc_free[c], NT * p + t + 2)
                pe.wait_ge(tr_ready[u], uses(p, i) + 1)
                if p == H:
                    pe.wait_ge(tr_ready[1 - u], uses(p, i + u) + 1)
                if p == O and isinstance(t, int) and t == NT - 1:
                    pe.wait_ge(la_ready, 1)
                    pe.wait_ge(lb_ready, 2)
                    pe.wait_ge(u_masked, 1)
                for k in range(KC):
                    last = nc.tensor.transpose(xps[(a, b)[k // 4]][:, k % 4 * P:(k % 4 + 1) * P], nat[:, u, k * P:(k + 1) * P], ident[:, :])
                last.then_inc(turned[u], 1)

            def mid(p, t, i, u):
                if p == H and not (isinstance(t, int) and t == NT - 1):
                    if isinstance(t, int) and t == 0:
                        pe.wait_ge(tr_ready[1], uses(O, PAIRS) + 1)
                        turn_a(1)
                    turn_b(t + 1, 1)

            for b in range(KC):
                turn_w(Q, b)
            over_phases(pe, before, main, prep, tail, mid)

        @block.scalar
        def _(act):
            start(act, from_one_act)
            act.wait_ge(consts_ready, 1)

            def copy_c(q, t, j, u):
                act.wait_ge(c_turned[u], PAIRS * q + j + 2)
                act.wait_ge(cT_stored[u], 16 * (PAIRS * q + j) + 1)
                nc.scalar.activation(cT_sb[:, u, :, :].rearrange("p o n -> p (o n)"), wps[u][:, 0:QO], ACT.Copy).then_inc(cT_ready[u], 1)

            def copy_blocks(q, m):
                if q > 0 and m == 0:
                    for w in range(2):
                        act.wait_ge(cpair_done[w], PAIRS * q)
                for s in range(RAW_SLOTS):
                    for h, b in enumerate(banks(s)):
                        act.wait_ge(wc_turned[b], turns(q, m, s) + 1)
                        nc.scalar.activation(wc[:, 4 * m + s // OB, 4 * h:4 * h + 4, 0, s % OB * P:(s % OB + 1) * P],
                                             xps[b][:, :].rearrange("p (k n) -> p k n", k=4), ACT.Copy).then_inc(wc_hi_ready[b], 1)

            def tiles(q):
                def copy_x(t, i, u):
                    act.wait_ge(x_turned, t + 1)
                    if not (isinstance(t, int) and t < 2):
                        act.wait_ge(xs_lo_ready[u], i)
                        act.wait_ge(xT_stored[u], 16 * i)
                    nc.scalar.activation(x_tr[:, u, 0:4, :].rearrange("p k n -> p (k n)"), xps[2][:, :], ACT.Copy).then_inc(x_copied_a, 1)

                def split_hi(q, t, i, u):
                    if q == 0:
                        copy_x(t, i, u)
                        act.wait_ge(x_copied_a, t + 1)
                        act.wait_ge(x_copied_v, t + 1)
                    else:
                        act.wait_ge(xT_loaded[u], 16 * (PAIRS * (q - 1) + i + 1))
                    if not (q == 0 and isinstance(t, int) and t < 2):
                        act.wait_ge(cpair_done[u], PAIRS * q + i)
                    nc.scalar.activation(x_st[:, u, :, :, 0, :], x_tr[:, u, :, :].rearrange("p k (s n) -> p k s n", s=2),
                                         ACT.Copy).then_inc(xs_hi_ready[u], 1)

                def main(t, j, u):
                    if not (isinstance(t, int) and t == NT - 1):
                        split_hi(q, t + 1, j + u, 1 - u)
                    elif q < QUARTERS - 1:
                        split_hi(q + 1, 0, 0, 0)
                    for s in range(2):
                        if s:
                            act.wait_ge(cpair_done[u], PAIRS * q + j + 1)
                        else:
                            act.wait_ge(cfirst_done, NT * q + t + 1)
                        if not (q == 0 and isinstance(t, int) and t == 0):
                            act.wait_ge(c_summed[s], NT * q + t)
                        nc.scalar.activation(c_low[:, s, :, :].rearrange("p a n -> p (a n)"), acc[s][S:P, :], ACT.Copy).then_inc(c_low_ready[s], 1)

                if q == 0:
                    split_hi(0, 0, 0, 0)
                over_tiles(act, main, partial(copy_c, q))

            def split_w(p, b):
                r = p % 2
                last_block = isinstance(b, int) and b == KC
                n, off = (AG, 0) if last_block else (P, AG if p == F else 0)
                if p == Q and b == 0:
                    for w in range(2):
                        act.wait_ge(cpair_done[w], PAIRS * QUARTERS)
                if isinstance(b, int) and b == 0 and p >= 1:
                    for w in range(2):
                        act.wait_ge(acc_done[1][w], uses(p - 1, 0))
                for h in range(2):
                    act.wait_ge(w_turned[h], blocks(p, b) + 1)
                    cols = slice(0, AG) if last_block else bass.ds(off + b * P, P)
                    nc.scalar.activation(w_hi[r][:, 4 * h:4 * h + 4, cols],
                                         w_banks(p, b)[h][:, :].rearrange("p (k n) -> p k n", k=4)[:, :, 0:n], ACT.Copy).then_inc(w_hi_ready[h], 1)

            def split_act(p, t, i, u):
                act.wait_ge(act_loaded[u], 16 * (uses(p, i) + 1))
                if p == F and not (isinstance(i, int) and i == 0):
                    act.wait_ge(acc_done[2][u], i)
                else:
                    act.wait_ge(acc_done[1][u], uses(p, i))
                nc.scalar.activation(act_hi[:, u, :, :], act_raw[:, u, :, :], ACT.Copy).then_inc(act_hi_ready[u], 1)

            def before(p):
                if p == H:
                    copy_a(0, 0, 0)
                    copy_b(0, 1, 0, 0)
                if p == F:
                    act.wait_ge(fb_turned, 1)
                    for r in range(2):
                        nc.scalar.activation(w_hi[0][:, 0, r * 512:(r + 1) * 512], xps[2 + r][:, :], ACT.Copy).then_inc(fb_hi, 1)

            def copy_b(t, r, i, u):
                act.wait_ge(lb_turned, 2 * t + r + 1)
                if not (isinstance(t, int) and t == 0):
                    act.wait_ge(acc_done[1][1 - u], uses(H, i + u))
                nc.scalar.activation(lb_st[:, r * 512:(r + 1) * 512], xps[3][:, :], ACT.Copy).then_inc(lb_ready, 1)

            def copy_a(t, i, u):
                act.wait_ge(la_turned, t + 1)
                if not (isinstance(t, int) and t == 0):
                    act.wait_ge(u_done, t)
                nc.scalar.activation(la_T[:, :, :].rearrange("p k r -> p (k r)"), xps[2][:, 0:KC * R2], ACT.Copy).then_inc(la_ready, 1)
                copy_b(t, 0, i, u)

            def copy_probs(t, i, u, g):
                act.wait_ge(pT_done, 4 * t + g + 1)
                if g >= 2:
                    act.wait_ge(pT_used[g % 2], (2 * t if g % 2 == 0 else t) + 2)
                elif g == 0:
                    act.wait_ge(pT_used[0], 2 * t + 1)
                elif not (isinstance(t, int) and t == 0):
                    act.wait_ge(turned[1 - u], uses(V, i + u) + 1)
                nc.scalar.activation(pT_sb[:, g % 2, :, :].rearrange("p a n -> p (a n)"), xps[g % 2][:, :], ACT.Copy).then_inc(pT_ready[g % 2], 1)

            def exponentials(t):
                for g in range(4):
                    act.wait_ge(shifted, 4 * t + g + 1)
                    part = scores[:, 8 * g:8 * g + 8, :]
                    nc.scalar.activation(part, part, ACT.Exp).then_inc(exp_ready, 1)

            def main(p, t, i, u):
                if not (isinstance(t, int) and t == NT - 1):
                    split_act(p, t + 1, i + u, 1 - u)
                elif p != F:
                    split_act(p + 1, 0, 0, 0)
                if p == V and not (isinstance(t, int) and t == 0):
                    exponentials(t - 1)
                    for g in range(2):
                        copy_probs(t - 1, i + u - 1, 1 - u, g)
                if p == O and isinstance(t, int) and t == 0:
                    exponentials(NT - 1)
                    for g in range(2):
                        copy_probs(NT - 1, PAIRS - 1, 1, g)
                if p in (Q, K):
                    act.wait_ge(var_ready, NT * p + t + 1)
                    nc.scalar.activation(std_rstd[:, 0:1], mean_var[:, 1:2], ACT.Sqrt, bias=eps_col[:, 0:1]).then_inc(std_ready, 1)
                if p == H and not (isinstance(t, int) and t in (0, NT - 1)):
                    copy_a(t + 1, i + u, 1 - u)
                if p == F:
                    act.wait_ge(gate_step, 7 * t + 3)
                    nc.scalar.activation(gate[:, 4, :], gate[:, 3, :], ACT.Exp).then_inc(gate_exp, 1)
                    act.wait_ge(aT_done, t + 1)
                    act.wait_ge(acc_free[2], t + 1)
                    nc.scalar.activation(aT_st[:, :], wps[1][:, 0:P], ACT.Copy).then_inc(aT_ready, 1)

            def prep(p, b):
                if p != F:
                    split_w(p + 1, b)

            def tail(p, t, i, u):
                if p == F:
                    return
                if p == V:
                    copy_probs(t, i, u, 2)
                    copy_probs(t, i, u, 3)
                act.wait_ge(turned[u], uses(p, i) + 2)
                if p == V:
                    act.wait_ge(tr_stored[1 - u], 16 * uses(p, i + u) + 1)
                else:
                    act.wait_ge(tr_stored[u], 16 * uses(p, i) + 1)
                if p in (Q, K):
                    for k in range(KC):
                        last = nc.scalar.activation(tr_sb[:, u, k, :], xps[2 * u + k // 4][:, k % 4 * P:(k % 4 + 1) * P], ACT.Identity,
                                                    scale=ln_cols[:, 2 * p, k:k + 1], bias=ln_cols[:, 2 * p + 1, k:k + 1])
                else:
                    a = {V: 2, O: 2 * u, H: 0}[p]
                    for h in range(2):
                        last = nc.scalar.activation(tr_sb[:, 1 if p == V else u, 4 * h:4 * h + 4, :].rearrange("p k n -> p (k n)"), xps[a + h][:, :], ACT.Copy)
                last.then_inc(tr_ready[u], 1)

            def mid(p, t, i, u):
                if p == H and not (isinstance(t, int) and t == NT - 1):
                    if isinstance(t, int) and t == 0:
                        copy_a(1, 0, 1)
                    copy_b(t + 1, 1, i + u, 1 - u)
                if p != V:
                    return
                if isinstance(t, int) and t == 0:
                    act.wait_ge(alibi_step, HEADS + 5)
                else:
                    act.wait_ge(turned[1 - u], uses(V, i + u) + 1)
                for c in range(2):
                    act.wait_ge(acc_free[c], NT * V + t + 2)
                heads = v_nat[:, :].rearrange("p (a two g d) -> p g a two d", two=2, g=4, d=DH)
                for s in range(2):
                    pairs = v_bd[:, s, :, :].rearrange("p (g m) d -> p g m d", g=4)
                    for two in range(2):
                        last = nc.scalar.activation(pairs[two * S:(two + 1) * S, :, :, two * DH:(two + 1) * DH],
                                                    heads[s * S:(s + 1) * S, :, :, two, :], ACT.Copy)
                last.then_inc(v_spread, 1)

            act.wait_ge(cols_scaled, 1)
            over_quarters(copy_blocks, tiles, lambda q: copy_c(q, NT - 1, PAIRS - 1, 1))
            for w in range(2):
                act.wait_ge(xs_lo_ready[w], QUARTERS * PAIRS)
            split_act(Q, 0, 0, 0)
            for b in range(KC):
                split_w(Q, b)
            over_phases(act, before, main, prep, tail, mid)

        @block.vector
        def _(dve):
            start(dve, from_one_dve)
            dve.wait_ge(cols_in, 64)
            nc.vector.tensor_scalar(ln_cols[:, 0:2, :], ln_cols[:, 0:2, :], SCALE, None, ALU.mult).then_inc(cols_scaled, 1)

            def copy_blocks(q, m):
                for s in range(RAW_SLOTS):
                    for h, b in enumerate(banks(s)):
                        dve.wait_ge(wc_hi_ready[b], turns(q, m, s) + 1)
                        hi, lo = (wc[:, 4 * m + s // OB, 4 * h:4 * h + 4, a, s % OB * P:(s % OB + 1) * P] for a in range(2))
                        nc.vector.tensor_tensor(lo, xps[b][:, :].rearrange("p (k n) -> p k n", k=4),
                                                hi.bitcast(F32), ALU.subtract).then_inc(wc_lo_ready[b], 1)

            def tiles(q):
                def copy_x(t, i, u):
                    dve.wait_ge(x_turned, t + 1)
                    if not (isinstance(t, int) and t < 2):
                        dve.wait_ge(xs_hi_ready[u], i)
                        dve.wait_ge(xs_lo_ready[u], i)
                        dve.wait_ge(xT_stored[u], 16 * i)
                    nc.vector.tensor_copy(x_tr[:, u, 4:8, :].rearrange("p k n -> p (k n)"), xps[3][:, :]).then_inc(x_copied_v, 1)

                def split_lo(q, t, i, u):
                    if q == 0:
                        copy_x(t, i, u)
                        dve.wait_ge(x_copied_v, t + 1)
                    dve.wait_ge(xs_hi_ready[u], PAIRS * q + i + 1)
                    nc.vector.tensor_tensor(x_st[:, u, :, :, 1, :], x_tr[:, u, :, :].rearrange("p k (s n) -> p k s n", s=2),
                                            x_st[:, u, :, :, 0, :].bitcast(F32), ALU.subtract).then_inc(xs_lo_ready[u], 1)

                def main(t, j, u):
                    if not (isinstance(t, int) and t == NT - 1):
                        split_lo(q, t + 1, j + u, 1 - u)
                    elif q < QUARTERS - 1:
                        split_lo(q + 1, 0, 0, 0)
                    for s in range(2):
                        dve.wait_ge(c_low_ready[s], NT * q + t + 1)
                        dve.wait_ge(c_turned[u], PAIRS * q + j + 1)
                        nc.vector.tensor_tensor(c_sum[s * S:(s + 1) * S, u, :, :].rearrange("p a n -> p (a n)"), acc[s][0:S, :],
                                                c_low[:, s, :, :].rearrange("p a n -> p (a n)"), ALU.add).then_inc(c_summed[s], 1)

                if q == 0:
                    split_lo(0, 0, 0, 0)
                over_tiles(dve, main, nothing)

            over_quarters(copy_blocks, tiles, nothing)

            def split_w(p, b):
                r = p % 2
                last_block = isinstance(b, int) and b == KC
                n, off = (AG, 0) if last_block else (P, AG if p == F else 0)
                for h in range(2):
                    dve.wait_ge(w_hi_ready[h], blocks(p, b) + 1)
                    cols = slice(0, AG) if last_block else bass.ds(off + b * P, P)
                    nc.vector.tensor_tensor(w_lo[r][:, 4 * h:4 * h + 4, cols],
                                            w_banks(p, b)[h][:, :].rearrange("p (k n) -> p k n", k=4)[:, :, 0:n],
                                            w_hi[r][:, 4 * h:4 * h + 4, cols].bitcast(F32), ALU.subtract).then_inc(w_lo_ready[h], 1)

            def split_b(t):
                for s in range(2):
                    dve.wait_ge(lb_loaded[s], 16 * t + 16)
                if not (isinstance(t, int) and t == 0):
                    dve.wait_ge(lb_turned, 2 * t)
                hi, lo = lb_parts[:, :, 0, :], lb_parts[:, :, 1, :]
                nc.vector.tensor_copy(hi.bitcast(F32R), lb_raw[:, :, :]).then_inc(lb_split, 1)
                nc.vector.tensor_copy(lb_parts[:, :, 2, :].bitcast(F32R), lb_raw[:, :, :]).then_inc(lb_split, 1)
                dve.wait_ge(lb_split, 4 * t + 1)
                nc.vector.tensor_tensor(lo.bitcast(F32R), lb_raw[:, :, :], hi, ALU.subtract).then_inc(lb_split, 1)
                nc.vector.tensor_tensor(lb_parts[:, :, 3, :].bitcast(F32R), lb_raw[:, :, :], hi, ALU.subtract).then_inc(lb_split, 1)

            def before(p):
                if p == H:
                    dve.wait_ge(bias_h_in, 16)
                    dve.wait_ge(mask_ready, 3)
                if p == F:
                    dve.wait_ge(fb_hi, 2)
                    for r in range(2):
                        nc.vector.tensor_tensor(w_lo[0][:, 0, r * 512:(r + 1) * 512], xps[2 + r][:, :],
                                                w_hi[0][:, 0, r * 512:(r + 1) * 512].bitcast(F32), ALU.subtract).then_inc(fb_lo, 1)
                    dve.wait_ge(gate_b_in, 16)

            def clip_v(t, i, u, c):
                if not (isinstance(t, int) and t == 0):
                    dve.wait_ge(v_spread, t)
                else:
                    dve.wait_ge(tr_stored[0], 16 * uses(V, 0) + 1)
                dve.wait_ge(acc_done[c][u], uses(V, i) + 1)
                nc.vector.tensor_scalar(v_nat[:, c * 512:(c + 1) * 512], acc[c][:, :], CLIP, -CLIP, ALU.min, ALU.max).then_inc(acc_free[c], 1)

            def bias_max(t, g):
                n, part = 4 * t + g, scores[:, 8 * g:8 * g + 8, :]
                dve.wait_ge(scores_done, n + 1)
                nc.vector.tensor_tensor(part, xps[g][:, :].rearrange("p (h k) -> p h k", k=S), alibi[:, 8 * g:8 * g + 8, :], ALU.add).then_inc(scores_biased, 1)
                dve.wait_ge(scores_biased, n + 2)
                nc.vector.tensor_reduce(smax[:, 8 * g:8 * g + 8], part, AX_X, ALU.max).then_inc(max_ready, 1)

            def normalize(t, g):
                n, part = 4 * t + g, scores[:, 8 * g:8 * g + 8, :]
                dve.wait_ge(exp_ready, n + 1)
                nc.vector.tensor_reduce(ssum[:, 8 * g:8 * g + 8], part, AX_X, ALU.add).then_inc(sum_ready, 1)
                dve.wait_ge(sum_ready, n + 1)
                nc.vector.reciprocal(smax[:, 8 * g:8 * g + 8], ssum[:, 8 * g:8 * g + 8]).then_inc(rsum_ready, 1)
                dve.wait_ge(rsum_ready, n + 1)
                nc.vector.tensor_tensor(part, part, smax[:, 8 * g:8 * g + 8].unsqueeze(2).to_broadcast([P, 8, S]), ALU.mult).then_inc(probs_ready, 1)

            def softmax(t, clip):
                if isinstance(t, int) and t == 0:
                    dve.wait_ge(alibi_step, HEADS + 5)
                    for w in range(2):
                        dve.wait_ge(turned[w], uses(V, 0) + 1)
                bias_max(t, 0)
                bias_max(t, 1)
                normalize(t, 0)
                bias_max(t, 2)
                normalize(t, 1)
                bias_max(t, 3)
                clip(0)
                normalize(t, 2)
                normalize(t, 3)
                clip(1)

            def main(p, t, i, u):
                if p in (Q, K):
                    n = NT * p + t
                    dve.wait_ge(turned[u], uses(p, i) + 1)
                    for c in range(2):
                        dve.wait_ge(acc_done[c][u], uses(p, i) + 1)
                        nc.vector.tensor_scalar(nat[:, u, c * 512:(c + 1) * 512], acc[c][:, :], CLIP, -CLIP, ALU.min, ALU.max).then_inc(acc_free[c], 1)
                    for c in range(2):
                        dve.wait_ge(acc_free[c], n + 2)
                        nc.vector.bn_stats(bn_st[:, c, :], nat[:, u, c * 512:(c + 1) * 512]).then_inc(stats_step, 1)
                    dve.wait_ge(stats_step, 3 * n + 2)
                    nc.vector.tensor_copy(wait_pad[:, :], bn_st[:, 1, 0:1])
                    nc.vector.bn_aggr(mean_var[:, :], bn_st[:, :, :].rearrange("p a b -> p (a b)")).then_inc(var_ready, 1)
                    dve.wait_ge(std_ready, n + 1)
                    nc.vector.reciprocal(std_rstd[:, 1:2], std_rstd[:, 0:1]).then_inc(stats_step, 1)
                    dve.wait_ge(stats_step, 3 * n + 3)
                    dve.wait_ge(var_ready, n + 1)
                    nc.vector.tensor_scalar(nat[:, u, :], nat[:, u, :], mean_var[:, 0:1], std_rstd[:, 1:2],
                                            ALU.subtract, ALU.mult).then_inc(nat_ready[u], 1)
                if p == V:
                    if isinstance(t, int) and t == 0:
                        clip_v(t, i, u, 0)
                        clip_v(t, i, u, 1)
                    else:
                        softmax(t - 1, partial(clip_v, t, i, u))
                if p == O and isinstance(t, int) and t == 0:
                    softmax(NT - 1, nothing)
                if p == O:
                    dve.wait_ge(turned[u], uses(p, i) + 1)
                    if isinstance(t, int) and t == 0:
                        dve.wait_ge(turned[1], uses(O, 0) + 1)
                    dve.wait_ge(x1_stored[u], 16 * i + 1)
                    dve.wait_ge(res_loaded[u], 16 * i + 16)
                    for c in range(2):
                        dve.wait_ge(acc_done[c][u], uses(p, i) + 1)
                        part = (slice(None), u, slice(c * 512, (c + 1) * 512))
                        nc.vector.tensor_tensor(nat[part], acc[c][:, :], aux[part], ALU.add).then_inc(acc_free[c], 1)
                    if isinstance(t, int) and t == NT - 2:
                        split_b(0)
                if p == H:
                    dve.wait_ge(u_done, t + 1)
                    nc.vector.tensor_tensor(u_seq[:, :], xps[2][0:R2, 256:256 + P], seq_mask[:, :], ALU.mult).then_inc(u_masked, 1)
                    dve.wait_ge(u_masked, t + 1)
                    if not (isinstance(t, int) and t == 0):
                        dve.wait_ge(acc_done[1][1 - u], uses(H, i + u))
                    nc.vector.tensor_copy(u_st[0:R2, :], u_seq[:, :]).then_inc(u_step, 1)
                    nc.vector.tensor_copy(u_st[R2:2 * R2, :], u_seq[:, :]).then_inc(u_step, 1)
                    dve.wait_ge(u_step, 3 * t + 2)
                    nc.vector.tensor_tensor(u_st[2 * R2:3 * R2, :], u_seq[:, :], u_st[0:R2, :].bitcast(F32), ALU.subtract).then_inc(u_step, 1)
                    nc.vector.tensor_tensor(u_st[3 * R2:4 * R2, :], u_seq[:, :], u_st[0:R2, :].bitcast(F32), ALU.subtract).then_inc(u_ready, 1)
                    if not (isinstance(t, int) and t == NT - 1):
                        split_b(t + 1)
                    dve.wait_ge(turned[u], uses(p, i) + 1)
                    dve.wait_ge(x1_stored[u], 16 * PAIRS + 1)
                    for c in range(2):
                        dve.wait_ge(acc_done[c][u], uses(p, i) + 1)
                        nc.vector.tensor_tensor(nat[:, u, c * 512:(c + 1) * 512], acc[c][:, :], bias_row[:, c * 512:(c + 1) * 512], ALU.add).then_inc(acc_free[c], 1)
                if p == F:
                    gates(t)
                    dve.wait_ge(turned[u], uses(F, 0) + 1)
                    dve.wait_ge(out_stored[u], 16 * i + 1)
                    dve.wait_ge(xb_ready, t + 1)
                    for c in range(3):
                        dve.wait_ge(acc_done[c][u], (uses(p, i) if c < 2 else i) + 1)
                        first = AG if c == 0 else 0
                        part = (slice(None), u, slice(c * FCH + first - AG, (c + 1) * FCH - AG))
                        nc.vector.tensor_tensor(nat[part], acc3[c][:, first:FCH], aux[part], ALU.add).then_inc(acc_free[c], 1)

            def gates(t):
                n = 7 * t
                dve.wait_ge(ag_done, t + 1)
                nc.vector.tensor_tensor(gate[:, 1, :], acc[0][:, MAXR:AG], gate[:, 0, :], ALU.add).then_inc(gate_step, 1)
                dve.wait_ge(gate_step, n + 1)
                nc.vector.tensor_reduce(gate[:, 2, 0:1], gate[:, 1, :], AX_X, ALU.max).then_inc(gate_step, 1)
                dve.wait_ge(gate_step, n + 2)
                nc.vector.tensor_scalar(gate[:, 3, :], gate[:, 1, :], gate[:, 2, 0:1], None, ALU.subtract).then_inc(gate_step, 1)
                dve.wait_ge(gate_exp, t + 1)
                nc.vector.tensor_scalar(gate[:, 5, :], gate[:, 4, :], 1.0, None, ALU.is_lt).then_inc(gate_step, 1)
                dve.wait_ge(gate_step, n + 4)
                nc.vector.tensor_tensor(gate[:, 6, 0:1], gate[:, 5, 0:1], gate[:, 5, 1:2], ALU.mult).then_inc(gate_step, 1)
                dve.wait_ge(gate_step, n + 5)
                nc.vector.tensor_tensor(gate[:, 7, 0:1], gate[:, 6, 0:1], gate[:, 5, 2:3], ALU.mult).then_inc(gate_step, 1)
                dve.wait_ge(gate_step, n + 6)
                nc.vector.tensor_copy(a_msk[:, 0:8], acc[0][:, 0:8])
                nc.vector.tensor_scalar(a_msk[:, 8:16], acc[0][:, 8:16], gate[:, 5, 0:1], None, ALU.mult)
                nc.vector.tensor_scalar(a_msk[:, 16:32], acc[0][:, 16:32], gate[:, 6, 0:1], None, ALU.mult)
                nc.vector.tensor_scalar(a_msk[:, 32:64], acc[0][:, 32:64], gate[:, 7, 0:1], None, ALU.mult).then_inc(gate_step, 1)
                dve.wait_ge(gate_step, n + 7)
                dve.wait_ge(aT_done, t)
                nc.vector.tensor_copy(a_parts[:, 0, :].bitcast(F32R), a_msk[:, :]).then_inc(a_ready, 1)
                dve.wait_ge(a_ready, 2 * t + 1)
                nc.vector.tensor_tensor(a_parts[:, 1, :].bitcast(F32R), a_msk[:, :], a_parts[:, 0, :], ALU.subtract).then_inc(a_ready, 1)

            def prep(p, b):
                if p != F:
                    split_w(p + 1, b)

            for b in range(KC):
                split_w(Q, b)
            over_phases(dve, before, main, prep, nothing, nothing)

        @block.gpsimd
        def _(pool):
            nc.gpsimd.memset(ident[:, :], 0.0).then_inc(ident_ready, 1)
            nc.gpsimd.memset(eps_col[:, :], LN_EPS).then_inc(consts_ready, 1)
            pool.wait_ge(ident_ready, 1)
            nc.gpsimd.affine_select(out=ident[:, :], in_=ident[:, :], compare_op=ALU.not_equal, fill=1.0, base=0,
                                    pattern=[[-1, P]], channel_multiplier=1).then_inc(ident_ready, 1)
            nc.gpsimd.memset(seq_mask[:, :], 1.0).then_inc(mask_ready, 1)
            pool.wait_ge(mask_ready, 1)
            nc.gpsimd.affine_select(out=seq_mask[:, :].rearrange("r (s n) -> r s n", s=2), in_=seq_mask[:, :].rearrange("r (s n) -> r s n", s=2),
                                    compare_op=ALU.is_ge, fill=0.0, base=0, pattern=[[-RANK, 2], [0, S]], channel_multiplier=1).then_inc(mask_ready, 1)
            pool.wait_ge(mask_ready, 2)
            nc.gpsimd.affine_select(out=seq_mask[:, :].rearrange("r (s n) -> r s n", s=2), in_=seq_mask[:, :].rearrange("r (s n) -> r s n", s=2),
                                    compare_op=ALU.is_ge, fill=0.0, base=RANK - 1, pattern=[[RANK, 2], [0, S]], channel_multiplier=-1).then_inc(mask_ready, 1)

            for q in range(QUARTERS):
                def main(t, j, u):
                    for s in range(2):
                        pool.wait_ge(c_summed[s], NT * q + t + 1)
                    nc.gpsimd.tensor_tensor(c_sum[:, u, 0, :], c_sum[:, u, 0, :], c_sum[:, u, 1, :], ALU.add).then_inc(c_ready[u], 1)

                over_tiles(pool, main, nothing)


            def split_act(p, i, u):
                pool.wait_ge(act_hi_ready[u], uses(p, i) + 1)
                nc.gpsimd.tensor_tensor(act_lo[:, u, :, :], act_raw[:, u, :, :], act_hi[:, u, :, :].bitcast(F32), ALU.subtract).then_inc(act_lo_ready[u], 1)

            def build_alibi(part):
                if part == 0:
                    nc.gpsimd.memset(v_bd[:, :, :, :], 0.0).then_inc(alibi_step, 1)
                    for s in range(2):
                        pool.wait_ge(alibi_step, s + 1)
                        nc.gpsimd.iota(rel[s * S:(s + 1) * S, :], pattern=[[1, S]], base=0, channel_multiplier=-1,
                                       allow_small_or_imprecise_dtypes=True).then_inc(alibi_step, 1)
                    pool.wait_ge(alibi_step, 3)
                elif part < 3:
                    pool.wait_ge(alibi_step, 3)
                    for n in range((part - 1) * HEADS // 2, part * HEADS // 2):
                        nc.gpsimd.tensor_scalar(alibi[:, n, :], rel[:, :], SLOPES[4 * (n % 8) + n // 8], None, ALU.mult).then_inc(alibi_step, 1)
                else:
                    s = part - 3
                    pool.wait_ge(alibi_step, HEADS + 3 + s)
                    rows = alibi[s * S:(s + 1) * S, :, :]
                    nc.gpsimd.affine_select(out=rows, in_=rows, compare_op=ALU.is_ge, fill=MASKED, base=0,
                                            pattern=[[0, HEADS], [-1, S]], channel_multiplier=1).then_inc(alibi_step, 1)
                    pool.wait_ge(alibi_step, HEADS + 4 + s)

            def shift(t):
                for g in range(4):
                    part = scores[:, 8 * g:8 * g + 8, :]
                    pool.wait_ge(max_ready, 4 * t + g + 1)
                    nc.gpsimd.tensor_tensor(part, part, smax[:, 8 * g:8 * g + 8].unsqueeze(2).to_broadcast([P, 8, S]), ALU.subtract).then_inc(shifted, 1)

            def main(p, t, i, u):
                if not (isinstance(t, int) and t == NT - 1):
                    split_act(p, i + u, 1 - u)
                elif p != F:
                    split_act(p + 1, 0, 0)
                if p == V and not (isinstance(t, int) and t == 0):
                    shift(t - 1)
                if p == O and isinstance(t, int) and t == 0:
                    shift(NT - 1)
                if p == Q and isinstance(t, int) and t == NT - 1:
                    build_alibi(0)
                if p == K and isinstance(t, int):
                    if t >= NT - 2:
                        pool.wait_ge(act_lo_ready[1 - u], uses(K, PAIRS - 1) + 1 if t == NT - 2 else uses(V, 0) + 1)
                    build_alibi({0: 1, NT - 3: 2, NT - 2: 3, NT - 1: 4}[t])
                if p == F:
                    if isinstance(t, int) and t == 0:
                        pool.wait_ge(bias_f_in, 16)
                    pool.wait_ge(res_loaded[u], 16 * (PAIRS + i + 1))
                    nc.gpsimd.tensor_tensor(aux[:, u, :], aux[:, u, :], bias_row[:, :], ALU.add).then_inc(xb_ready, 1)

            for w in range(2):
                pool.wait_ge(cpair_done[w], QUARTERS * PAIRS)
            split_act(Q, 0, 0)
            over_phases(pool, nothing, main, nothing, nothing, nothing)


_INS = ["x", "itok_B_3_7", "itok_B_6_15", "L0_cond_weight", "L0_attn_w_qkv", "L0_attn_q_ln_w", "L0_attn_q_ln_b",
        "L0_attn_k_ln_w", "L0_attn_k_ln_b", "L0_attn_w_out", "L0_cond2_base_weight", "L0_cond2_base_bias",
        "L0_cond2_lora_A_w", "L0_cond2_lora_B_w", "L0_ffn_W", "L0_ffn_b", "L0_ffn_A", "L0_ffn_B",
        "L0_ffn_gate_w", "L0_ffn_gate_b"]


def kernel(**inputs):
    import numpy as _np
    import concourse.bacc as _bacc
    from concourse import mybir as _mybir
    from concourse.bass_utils import run_bass_kernel_spmd as _run

    nc = _bacc.Bacc("TRN2", target_bir_lowering=False, num_devices=1)
    arrays, args = {}, []
    for name in _INS:
        a = _np.ascontiguousarray(inputs[name])
        arrays[f"in_{name}"] = a
        args.append(nc.dram_tensor(f"in_{name}", a.shape, _mybir.dt.from_np(a.dtype), kind="ExternalInput").ap())
    args.append(nc.dram_tensor("out_0", inputs["x"].shape, _mybir.dt.float32, kind="ExternalOutput").ap())
    adaln_attention_ffn(nc, *args)
    r = _run(nc, [arrays], core_ids=[0])
    return r.results[0]["out_0"]
```
